# Optimizing a Trainium2 kernel written in Bass

```python
import numpy as np
import jax
import jax.numpy as jnp

def _softmax(x, axis=-1):
    return jax.nn.softmax(x, axis=axis)

def _gelu(x):
    return jax.nn.gelu(x, approximate=True)

def _silu(x):
    return jax.nn.silu(x)

def _sigmoid(x):
    return jax.nn.sigmoid(x)

def _layernorm(x, axis=-1, eps=1e-05):
    m = jnp.mean(x, axis=axis, keepdims=True)
    v = jnp.var(x, axis=axis, keepdims=True)
    return (x - m) / jnp.sqrt(v + eps)

def _scatter_add(tgt, idx, src, axis=0):
    return tgt.at[idx].add(src)

def _segment_sum(src, seg, n):
    return jax.ops.segment_sum(src, seg, n)
kernel_name = 'mk_gps_d1_gnn_r8_b8ba03'

def setup_inputs(seed: int=0):
    np.random.seed(seed)
    _w = jnp.asarray

    def _rec_inputs():
        import jax
        import jax.numpy as jnp
        _gk = jax.random.key(seed)
        x = -0.0003713 + 1 * jax.random.normal(jax.random.fold_in(_gk, 1), (6250, 256), jnp.float32)
        _s = jax.random.randint(jax.random.fold_in(_gk, 2), (100000,), 0, 6250, jnp.int32)
        _d = jax.random.randint(jax.random.fold_in(_gk, 3), (100000,), 0, 6250, jnp.int32)
        _loop = jnp.arange(6250, dtype=jnp.int32)
        src = jnp.concatenate([_s, _d, _loop])
        dst = jnp.concatenate([_d, _s, _loop])
        _o = jnp.argsort(dst, stable=True)
        src = src[_o]
        dst = dst[_o]
        return (x, src, dst)
    x, src, dst = _rec_inputs()

    def _L0_gnn_setup():
        import jax, jax.numpy as jnp
        import numpy as np
        N, E, D, K, L = (6250, 200000, 256, 4, 2)
        TAU = 1.0

        def _scatter_mean(src, row, num_segments):
            sums = jax.ops.segment_sum(src, row, num_segments=num_segments)
            cnt = jax.ops.segment_sum(jnp.ones((src.shape[0],), dtype=src.dtype), row, num_segments=num_segments)
            return sums / jnp.maximum(cnt, 1.0)[:, None]
        key = jax.random.key(seed)
        k1, k2, k3, k4, k5 = jax.random.split(key, 5)
        x = jax.random.normal(k1, (N, D), dtype=jnp.float32)
        edge_index = jax.random.randint(k2, (2, E), 0, N, dtype=jnp.int64)
        lim_w = float(np.sqrt(6.0 / (2 * D + D)))
        W = jax.random.uniform(k3, (L, K, 2 * D, D), minval=-lim_w, maxval=lim_w, dtype=jnp.float32)
        lim_e = float(np.sqrt(1.0 / D))
        envW = jax.random.uniform(k4, (L, D, K), minval=-lim_e, maxval=lim_e, dtype=jnp.float32)
        envb = jax.random.uniform(k5, (L, K), minval=-lim_e, maxval=lim_e, dtype=jnp.float32)
        return {'x': x, 'edge_index': edge_index, 'W': W, 'envW': envW, 'envb': envb}
    _L0_gnn_all = _L0_gnn_setup()
    _L0_gnn_in = {k: v for k, v in _L0_gnn_all.items() if k in ('W', 'envW', 'envb')}
    del _L0_gnn_all

    def _L0_mix_setup():
        import jax, jax.numpy as jnp
        import numpy as np
        HEADS, DIM_HEAD = (8, 64)
        EPS = 1e-05

        def instance_norm(t):
            mu = jnp.mean(t, axis=-1, keepdims=True)
            var = jnp.mean((t - mu) ** 2, axis=-1, keepdims=True)
            return (t - mu) * jax.lax.rsqrt(var + EPS)
        key = jax.random.key(seed)
        k1, k2, k3, k4 = jax.random.split(key, 4)
        B, N, D = (8, 1024, 256)
        inner = HEADS * DIM_HEAD
        x = jax.random.normal(k1, (B, N, D), jnp.float32)
        w_qkv = jax.random.normal(k2, (3 * inner, D), jnp.float32) / np.sqrt(D).astype(np.float32)
        w_out = jax.random.normal(k3, (D, inner), jnp.float32) / np.sqrt(inner).astype(np.float32)
        b_out = 0.01 * jax.random.normal(k4, (D,), jnp.float32)
        return {'x': x, 'w_qkv': w_qkv, 'w_out': w_out, 'b_out': b_out}
    _L0_mix_all = _L0_mix_setup()
    _L0_mix_in = {k: v for k, v in _L0_mix_all.items() if k in ('w_qkv', 'w_out', 'b_out')}
    del _L0_mix_all

    def _L0_ffn_setup():
        import jax, jax.numpy as jnp
        import numpy as np
        B, S, D = (8, 512, 256)
        H = 4 * D
        CAPACITY = 0.5
        key = jax.random.key(seed)
        ks = jax.random.split(key, 6)
        x = jax.random.normal(ks[0], (B, S, D), dtype=jnp.float32)
        attention_mask = jnp.zeros((B, 1, 1, S), dtype=jnp.float32)
        wr = jax.random.normal(ks[1], (D, 1), dtype=jnp.float32) * 0.02
        br = jnp.zeros((1,), dtype=jnp.float32)
        w1 = jax.random.normal(ks[2], (D, H), dtype=jnp.float32) * 0.02
        b1 = jnp.zeros((H,), dtype=jnp.float32)
        w2 = jax.random.normal(ks[3], (H, D), dtype=jnp.float32) * 0.02
        b2 = jnp.zeros((D,), dtype=jnp.float32)
        return {'x': x, 'attention_mask': attention_mask, 'wr': wr, 'br': br, 'w1': w1, 'b1': b1, 'w2': w2, 'b2': b2}
    _L0_ffn_all = _L0_ffn_setup()
    _L0_ffn_in = {k: v for k, v in _L0_ffn_all.items() if k in ('attention_mask', 'wr', 'br', 'w1', 'b1', 'w2', 'b2')}
    del _L0_ffn_all
    return {'x': x, 'src': src, 'dst': dst, 'L0_gnn_W': _L0_gnn_in['W'], 'L0_gnn_envW': _L0_gnn_in['envW'], 'L0_gnn_envb': _L0_gnn_in['envb'], 'L0_mix_w_qkv': _L0_mix_in['w_qkv'], 'L0_mix_w_out': _L0_mix_in['w_out'], 'L0_mix_b_out': _L0_mix_in['b_out'], 'L0_ffn_attention_mask': _L0_ffn_in['attention_mask'], 'L0_ffn_wr': _L0_ffn_in['wr'], 'L0_ffn_br': _L0_ffn_in['br'], 'L0_ffn_w1': _L0_ffn_in['w1'], 'L0_ffn_b1': _L0_ffn_in['b1'], 'L0_ffn_w2': _L0_ffn_in['w2'], 'L0_ffn_b2': _L0_ffn_in['b2']}

def reference(x, src, dst, L0_gnn_W, L0_gnn_envW, L0_gnn_envb, L0_mix_w_qkv, L0_mix_w_out, L0_mix_b_out, L0_ffn_attention_mask, L0_ffn_wr, L0_ffn_br, L0_ffn_w1, L0_ffn_b1, L0_ffn_w2, L0_ffn_b2):
    import jax
    import jax.numpy as jnp

    def _L0_gnn_ref(x, edge_index, W, envW, envb):
        import jax, jax.numpy as jnp
        import numpy as np
        N, E, D, K, L = (6250, 200000, 256, 4, 2)
        TAU = 1.0

        def _scatter_mean(src, row, num_segments):
            sums = jax.ops.segment_sum(src, row, num_segments=num_segments)
            cnt = jax.ops.segment_sum(jnp.ones((src.shape[0],), dtype=src.dtype), row, num_segments=num_segments)
            return sums / jnp.maximum(cnt, 1.0)[:, None]
        row, col = (edge_index[0], edge_index[1])
        z = x
        for l in range(L):
            logits = z @ envW[l] + envb[l]
            weights = jax.nn.softmax(logits / TAU, axis=-1)
            agg = _scatter_mean(z[col], row, N)
            combined = jnp.concatenate([agg, z], axis=-1)
            outputs = jnp.einsum('nd,kdo->nko', combined, W[l]) + z[:, None, :]
            z = jnp.einsum('nk,nko->no', weights, outputs)
            z = jax.nn.relu(z)
        return z

    def _L0_mix_ref(x, w_qkv, w_out, b_out):
        import jax, jax.numpy as jnp
        import numpy as np
        HEADS, DIM_HEAD = (8, 64)
        EPS = 1e-05

        def instance_norm(t):
            mu = jnp.mean(t, axis=-1, keepdims=True)
            var = jnp.mean((t - mu) ** 2, axis=-1, keepdims=True)
            return (t - mu) * jax.lax.rsqrt(var + EPS)
        B, N, _ = x.shape
        H, Dh = (HEADS, DIM_HEAD)
        qkv = jnp.einsum('bnd,ed->bne', x, w_qkv)
        q, k, v = jnp.split(qkv, 3, axis=-1)

        def to_heads(t):
            return t.reshape(B, N, H, Dh).transpose(0, 2, 1, 3)
        q, k, v = (to_heads(q), to_heads(k), to_heads(v))
        k = instance_norm(k)
        v = instance_norm(v)
        dots = jnp.einsum('bhnd,bhne->bhde', k, v)
        out = jnp.einsum('bhnd,bhde->bhne', q, dots) / N
        out = out.transpose(0, 2, 1, 3).reshape(B, N, H * Dh)
        return jnp.einsum('bne,de->bnd', out, w_out) + b_out

    def _L0_ffn_ref(x, attention_mask, wr, br, w1, b1, w2, b2):
        import jax, jax.numpy as jnp
        import numpy as np
        B, S, D = (8, 512, 256)
        H = 4 * D
        CAPACITY = 0.5
        b, s, d = x.shape
        weights = (jnp.einsum('bsd,do->bso', x, wr) + br)[..., 0]
        k = max(1, int(CAPACITY * s))
        kk = k - 1 if k > 1 else 1
        _, idx = jax.lax.top_k(weights, k)
        sel_idx = idx[:, :kk]
        sel = jnp.take_along_axis(x, sel_idx[:, :, None], axis=1)
        h = jax.nn.gelu(jnp.einsum('bkd,dh->bkh', sel, w1) + b1)
        y = jnp.einsum('bkh,hd->bkd', h, w2) + b2
        w_sel = jnp.take_along_axis(weights, sel_idx, axis=1)
        y = y * w_sel[..., None]
        batch_idx = jnp.arange(b)[:, None]
        processed = jnp.zeros_like(x).at[batch_idx, sel_idx].set(y)
        return processed + x
    edge_index = jnp.stack([src, dst])
    xn = _layernorm(x, axis=-1)
    x = x + _L0_gnn_ref(xn, edge_index, L0_gnn_W, L0_gnn_envW, L0_gnn_envb) + _L0_mix_ref(xn[None], L0_mix_w_qkv, L0_mix_w_out, L0_mix_b_out)[0]
    x = x + _L0_ffn_ref(_layernorm(x, axis=-1)[None], L0_ffn_attention_mask, L0_ffn_wr, L0_ffn_br, L0_ffn_w1, L0_ffn_b1, L0_ffn_w2, L0_ffn_b2)[0]
    return x

_drawn_inputs = setup_inputs


def setup_inputs(seed=0):
    import zlib

    import numpy as np

    out = dict(_drawn_inputs(seed))
    spreads = {'L0_ffn_b1': (0.0, 0.8), 'L0_ffn_b2': (0.0, 0.8)}
    factors = {'L0_gnn_envb': 5.022,
     'L0_mix_b_out': 8.0,
     'L0_ffn_wr': 4.81,
     'L0_ffn_w1': 6.901,
     'L0_ffn_w2': 6.508}
    for name, (base, spread) in spreads.items():
        noise = np.random.default_rng([zlib.crc32(name.encode()), seed]).standard_normal(out[name].shape)
        drawn = base * np.exp(spread * noise) if base else spread * noise
        out[name] = jnp.asarray(drawn.astype(out[name].dtype))
    for name, factor in factors.items():
        out[name] = (out[name] * factor).astype(out[name].dtype)
    return out
```

```python
import concourse.bass as bass
from concourse import mybir
from contextlib import ExitStack
import numpy as np

P = 128
N = 6250
D = 256
E = 206250
TG = 7
NT = TG * TG
NP = NT * P
GR = TG * P
HR = GR // 2
EXPERTS = 4
H = 1024
KV = 1024
HEAD = 64
EPS = 1e-5
F = 2048
BITS, ROW_BITS = 18, 11
EP = 125
EC = E // EP
CB = 13
NODE = (1 << CB) - 1
KEY_BASE = 0x40000000
KEY_PAD = 0x44000000
SPARE = 7168
A_ROWS = SPARE + (1 << (BITS - CB))
TURN = F // P
TURNS = E // F
LAST = -(-(E - TURNS * F) // P)
TOPK = N // 2 - 1
CH = 5
CHUNKS = CH * CH
SLOTS = CHUNKS * P
LIST_SPARE = 4096
FH = CH * P // 2


def before(j, ring):
    if j >= ring:
        return j - ring + 1
    return max(i for i in range(TG) if i % ring == j % ring) - TG + 1


def ge(eng, sem, value, nop=False):
    if not (isinstance(value, int) and value <= 0):
        eng.wait_ge(sem, value)
        if nop and not isinstance(value, int):
            eng.nop(nofuse=True)


def build(nc, x, src, dst, gw, envw, envb, wkv, wq, wo, bo, wr, br, w1, b1, w2, b2, out):
    f32, i32, f16 = mybir.dt.float32, mybir.dt.int32, mybir.dt.float16
    ALU = mybir.AluOpType
    ACT = mybir.ActivationFunctionType
    AX = mybir.AxisListType.X
    ctx = ExitStack()
    with ctx:
        def sb(name, shape, dt):
            return ctx.enter_context(nc.sbuf_tensor(name, shape, dt))

        def sem(name):
            return ctx.enter_context(nc.semaphore(name))

        def sems(name, n):
            return [sem(f"{name}{i}") for i in range(n)]

        def dram(name, shape, dt):
            return nc.dram_tensor(name, shape, dt).ap()

        class Carver:

            def __init__(self, base):
                self.base, self.at = base, 0

            def __call__(self, n, dt=f32):
                a = self.base[:, self.at:self.at + n]
                self.at += n
                assert self.at <= self.base.shape[1]
                return a if dt == f32 else a.bitcast(dt)

        ZW = NT * D
        zs1 = sb("zs1", [P, NT, 2, D], f16)
        arena = sb("arena", [P, ZW + TG * TG * HR // 2], f32)
        zs2 = arena[:, 0:ZW].bitcast(f16).rearrange("p (t s d) -> p t s d", t=NT, s=2)
        a_ring = arena[:, ZW:].bitcast(f16).rearrange("p (u c r) -> p u c r", u=TG, c=TG)
        addr = sb("addr", [P, F], i32)
        cnt16 = sb("cnt16", [P, F], f16)
        cur_addr = sb("cur_addr", [P, 2, TURN], i32)
        cur_cnt = sb("cur_cnt", [P, 2, TURN], f16)
        gw_sb = sb("gw_sb", [P, 4, EXPERTS * D], f32)
        aggT = sb("aggT", [P, 2, GR], f32)
        zT = sb("zT", [P, TG, D], f32)
        z_in = sb("z_in", [P, TG, D], f32)
        zn = sb("zn", [P, 4, D], f32)
        acc = sb("acc", [P, 2, D], f32)
        inv = sb("inv", [P, GR], f32)
        ident = sb("ident", [P, P], f32)
        ones_f = sb("ones_f", [P, P], f32)
        tri = sb("tri", [P, P], f32)
        ones16 = sb("ones16", [P, P], f16)
        eps = sb("eps", [P, 1], f32)
        envw_sb = sb("envw_sb", [P, 2, 2, EXPERTS], f32)
        envb_sb = sb("envb_sb", [P, 2, EXPERTS], f32)
        lg = sb("lg", [P, TG, EXPERTS], f32)
        wts = sb("wts", [P, TG, EXPERTS], f32)
        red = sb("red", [P, 4, TG], f32)
        wsum = sb("wsum", [P, TG], f32)
        mv = sb("mv", [P, TG, 2], f32)
        stats = sb("stats", [P, TG, 6], f32)
        std = sb("std", [P, TG], f32)
        rstd = sb("rstd", [P, TG], f32)
        wcol = sb("wcol", [P, NT], f32)
        bound = sb("bound", [P, 2 * TG], i32)
        ps = ctx.enter_context(nc.psum_tensor("ps", [P, 8, 512], f32))

        c = Carver(arena)
        keys = [c(F), c(F)]
        src_in, dst_in = c(EC, i32), c(EC, i32)
        pos, spare, same, run, tmp = c(F), c(F, i32), c(F, i32), c(F), c(F, i32)
        qid, qbit, qxor, sgn = c(1, i32), c(9, i32), c(8, i32), c(9)
        edge_next, edge_prev, carry, crow, cexcl = c(1), c(1), c(1), c(P), c(P + 1)
        below = c(2 * TG)
        assert c.at <= ZW + TG * TG * HR // 2
        c = Carver(arena)
        x_in = c(TG * D).rearrange("p (j d) -> p j d", j=TG)
        xn = c(TG * D).rearrange("p (j d) -> p j d", j=TG)
        xnT = c(TG * D).rearrange("p (j d) -> p j d", j=TG)
        sq = c(2 * KV).rearrange("p (s e) -> p s e", s=2)
        k_sb = c(KV).rearrange("p (s e) -> p s e", s=2)
        v_sb = c(KV).rearrange("p (s e) -> p s e", s=2)
        wkv_sb = c(2 * KV).rearrange("p (c e) -> p c e", c=2)
        wmean = c(32).rearrange("p (c h) -> p c h", c=2)
        ss = c(32).rearrange("p (s h) -> p s h", s=2)
        sd = c(32).rearrange("p (s h) -> p s h", s=2)
        rs = c(16)
        rr = c(8)
        wq_sb = c(4 * D).rearrange("p (c e) -> p c e", c=4)
        wo_sb = c(4 * D).rearrange("p (c e) -> p c e", c=4)
        dT = c(4 * P).rearrange("p (c e) -> p c e", c=4)
        g_sb = c(4 * D).rearrange("p (c e) -> p c e", c=4)
        m_sb = c(2 * D).rearrange("p (c e) -> p c e", c=2)
        bo_sb = c(D)
        z1_words = zs1[:].rearrange("p t s d -> p (t s d)").bitcast(f32)
        c = Carver(z1_words)
        xp_in = c(TG * D).rearrange("p (j d) -> p j d", j=TG)
        x1 = c(TG * D).rearrange("p (j d) -> p j d", j=TG)
        xn2 = c(TG * D).rearrange("p (j d) -> p j d", j=TG)
        base = c(TG * D).rearrange("p (j d) -> p j d", j=TG)
        wr_sb, junk = c(D), c(D)
        br_sb = c(1)
        w1_sb = c(2 * H).rearrange("p (c e) -> p c e", c=2)
        c = Carver(arena)
        w2_sb = c(8 * D).rearrange("p (c e) -> p c e", c=8)
        b1_sb, b2_sb = c(8), c(D)
        hT = c(8 * CH * P).rearrange("p (m r) -> p m r", m=8)
        x2T = c(2 * CH * P).rearrange("p (k r) -> p k r", k=2)
        xg = c(CH * D).rearrange("p (j d) -> p j d", j=CH)
        bg = c(CH * D).rearrange("p (j d) -> p j d", j=CH)
        yo = c(CH * D).rearrange("p (j d) -> p j d", j=CH)
        yt = c(2 * D).rearrange("p (j d) -> p j d", j=2)
        fj, fw = c(D), c(CH)
        u_t, cand, t1, take = c(1, i32), c(1, i32), c(1, i32), c(1, i32)
        hits, part = c(NT), c(1)
        gt, eq, cum, tot, scan, sel = c(NT), c(NT), c(NT), c(NT), c(NT), c(NT)
        ntot = c(1)
        nid, slot_i, skip_i = c(NT, i32), c(NT, i32), c(NT, i32)
        pad_ids = c(SLOTS - TOPK, i32)
        idx = c(CHUNKS, i32)
        cur_g, cur_s = c(CH, i32), c(CH, i32)

        A = dram("A", [A_ROWS << CB, 1], f16)
        A_tiles = A[0:NP << CB, :].rearrange("(ct p r) o -> p ct (r o)", p=P, r=NODE + 1)
        zero_rows = zs1[:].rearrange("p t s d -> p (t s d)")[:, 0:NP]
        zd = [dram("zd0", [NP, D], f32), dram("zd1", [NP, D], f32)]
        xTd = dram("xTd", [P, NT, D], f32)
        xpd = dram("xpd", [NP, D], f32)
        invd = dram("invd", [1, NP], f32)
        xn2d = dram("xn2d", [NP + P, D], f32)
        d_last, d_carry = dram("d_last", [P, 1], f32), dram("d_carry", [P, 1], f32)
        chosen = dram("chosen", [LIST_SPARE + NP, 1], i32)

        def rows(t):
            return t.rearrange("(n p) d -> p n d", p=P)

        consts = sem("consts")
        order_in = sem("order_in")
        edges_in, step = sem("edges_in"), sem("step")
        order_out, tposed, half_copied = sem("order_out"), sem("tposed"), sem("half_copied")
        sorted_s, carry_s, lists_ready = sem("sorted_s"), sem("carry_s"), sem("lists_ready")
        zero_made, a_zeroed = sem("zero_made"), sem("a_zeroed")
        scat, landed = sems("scat", 3), sem("landed")
        small_in, wmix_in, gw_in, ffn_in = sem("small_in"), sem("wmix_in"), sem("gw_in"), sem("ffn_in")
        below_ready, below_summed, bound_ready = sem("below_ready"), sem("below_summed"), sem("bound_ready")
        early_free = sem("early_free")
        x_ld, xn_st, xT_st = sems("x_ld", TG), sems("xn_st", TG), sems("xT_st", TG)
        var_ready, std_ready = sem("var_ready"), sem("std_ready")
        xn_done, hi_done, xT_done, xT_copied = sem("xn_done"), sem("hi_done"), sem("xT_done"), sem("xT_copied")
        wkv_ready, kv_done, sq_done, ss_done, sd_done = sem("wkv_ready"), sem("kv_done"), sem("sq_done"), sem("ss_done"), sem("sd_done")
        v_done, dots_done, dT_done, lo_done = sem("v_done"), sem("dots_done"), sem("dT_done"), sem("lo_done")
        gm_done, gm_copied = sem("gm_done"), sem("gm_copied")
        mix_done, xp_ready, xp_st = sem("mix_done"), sem("xp_ready"), sems("xp_st", TG)
        a_in, a_used, agg_evac = sems("a_in", TG), sem("a_used"), sem("agg_evac")
        z_ld, t_done, t_copied = sems("z_ld", TG), sem("t_done"), sem("t_copied")
        logit_done, lg_read, lg_sub, lg_exp, wts_ready = sem("logit_done"), sem("lg_read"), sem("lg_sub"), sem("lg_exp"), sem("wts_ready")
        w_done, acc_init, acc_done = sem("w_done"), sem("acc_init"), sem("acc_done")
        zn_ready, hi2_done, lo2_done, zn_st = sem("zn_ready"), sem("hi2_done"), sem("lo2_done"), sems("zn_st", 4)
        inv_st, inv_ld, xp_ld = sem("inv_st"), sem("inv_ld"), sems("xp_ld", TG)
        x1_done, var2_ready, std2_ready, end_ready = sem("x1_done"), sem("var2_ready"), sem("std2_ready"), sem("end_ready")
        end_st = sems("end_st", TG)
        wcol_ready, wcol_cut, cand_ready, counted, cnt_read = sem("wcol_ready"), sem("wcol_cut"), sem("cand_ready"), sem("counted"), sem("cnt_read")
        slots_ready, list_st, list_in, pads_st = sem("slots_ready"), sem("list_st"), sem("list_in"), sem("pads_st")
        idx_cp = sem("idx_cp")
        g_in, f_t, f_tc, h_done, h_act, y_done, y_read, yo_ready, y_st = (
            sems("g_in", CH), sem("f_t"), sem("f_tc"), sem("h_done"), sem("h_act"), sem("y_done"), sem("y_read"), sem("yo_ready"), sems("y_st", CH))
        fw_ready = sem("fw_ready")

        NSTEP = [0]
        T_ORDER = [(4, 5), (6,), (0, 1), (2, 3)]
        TB = len(T_ORDER)

        def bank(b, n=1):
            return ps[:, b:b + n, :].rearrange("p b c -> p (b c)")

        ps_sort = bank(0, 4)
        ps_kv = [bank(0, 2), bank(2, 2)]
        ps_T = ps[:, 4:6, 0:D]
        ps_dots = bank(6)
        ps_agg = [[bank(0), bank(1)], [bank(2), bank(3)]]
        ps_out = [bank(4, 2), bank(6, 2)]
        ps_cnt = [bank(2), bank(0)]
        ps_zT = bank(4, 4)
        ps_lg = bank(7)[:, 256:256 + TG * EXPERTS].rearrange("p (j k) -> p j k", j=TG)

        block = ctx.enter_context(nc.Block())

        def groups(eng, body, last_apart=False):
            body(0)
            with eng.Fori(1, TG - 1 if last_apart else TG) as g:
                body(g)
            if last_apart:
                body(TG - 1)

        @block.sync
        def _(sp):
            sp.dma_start(src_in[0:EP, :], src.rearrange("(p t) -> p t", p=EP)).then_inc(edges_in, 16)
            sp.dma_start(dst_in[0:EP, :], dst.rearrange("(p t) -> p t", p=EP)).then_inc(edges_in, 16)
            sp.dma_start(envw_sb[:], envw).then_inc(small_in, 16)
            sp.dma_start(envb_sb[:], envb).then_inc(small_in, 16)
            sp.dma_start(gw_sb[:], gw[0]).then_inc(gw_in, 16)
            sp.wait_ge(sorted_s, 1)
            sp.dma_start(edge_next[0:P - 1, :], keys[0][1:P, 0:1]).then_inc(carry_s, 16)
            sp.dma_start(edge_prev[1:P, :], keys[0][0:P - 1, F - 1:F]).then_inc(carry_s, 16)
            sp.wait_ge(sorted_s, 2)
            sp.dma_start(d_last[:, :], keys[1][:, F - 1:F]).then_inc(carry_s, 16)
            sp.wait_ge(carry_s, 48)
            sp.dma_start(crow[0:1, 0:P], d_last.rearrange("p o -> o p")).then_inc(carry_s, 16)
            sp.wait_ge(sorted_s, 3)
            sp.dma_start(d_carry.rearrange("p o -> o p"), cexcl[0:1, 0:P]).then_inc(carry_s, 16)
            sp.wait_ge(carry_s, 80)
            sp.dma_start(carry[:, :], d_carry[:, :]).then_inc(carry_s, 16)

            sp.wait_ge(early_free, 1)
            sp.dma_start(wkv_sb, wkv).then_inc(wmix_in, 16)
            sp.dma_start(wq_sb, wq).then_inc(wmix_in, 16)
            sp.dma_start(wo_sb, wo).then_inc(wmix_in, 16)
            sp.dma_start(bo_sb, bo).then_inc(wmix_in, 16)

            def loads(g):
                for j in range(TG):
                    ge(sp, xn_done, g * TG - TG + j + 1, nop=True)
                    sp.dma_start(x_in[:, j, :], rows(x)[:, g * TG + j, :]).then_inc(x_ld[j], 16)

            def stores(g):
                for j in range(TG):
                    ge(sp, xn_done, g * TG + j + 1, nop=True)
                    sp.dma_start(rows(zd[0])[:, g * TG + j, :], xn[:, j, :]).then_inc(xn_st[j], 16)
                    ge(sp, xT_copied, g * TG + j + 1, nop=True)
                    sp.dma_start(xTd[:, g * TG + j, :], xnT[:, j, :]).then_inc(xT_st[j], 16)

            loads(0)
            loads(1)
            stores(0)
            with sp.Fori(1, TG - 1) as g:
                loads(g + 1)
                stores(g)
            stores(TG - 1)
            for j in range(TG):
                sp.wait_ge(xn_st[j], 16 * TG)
                sp.wait_ge(xT_st[j], 16 * TG)

            def mix_loads(g):
                for j in range(TG):
                    ge(sp, xp_ready, g * TG - TG + j + 1, nop=True)
                    if isinstance(g, int) and g == 0:
                        sp.wait_ge(kv_done, NT)
                    sp.dma_start(x_in[:, j, :], rows(x)[:, g * TG + j, :]).then_inc(x_ld[j], 16)
                    sp.dma_start(xnT[:, j, :], xTd[:, g * TG + j, :]).then_inc(x_ld[j], 16)

            def mix_stores(g):
                for j in range(TG):
                    ge(sp, xp_ready, g * TG + j + 1, nop=True)
                    sp.dma_start(rows(xpd)[:, g * TG + j, :], xn[:, j, :]).then_inc(xp_st[j], 16)

            mix_loads(0)
            mix_loads(1)
            mix_stores(0)
            with sp.Fori(1, TG - 1) as g:
                mix_loads(g + 1)
                mix_stores(g)
            mix_stores(TG - 1)
            for j in range(TG):
                sp.wait_ge(xp_st[j], 16 * TG)

            sp.wait_ge(bound_ready, 1)
            for l in range(2):
                def tiles_of_a(g, b, us=range(TG)):
                    if l == 0 and 0 in us:
                        sp.wait_ge(landed, sp.value_load(bound[0:1, bass.ds(2 * g + b, 1)], min_val=1, max_val=TURNS + 1))
                        sp.nop(nofuse=True)
                    for u in us:
                        ge(sp, a_used, TG * (2 * (TG * l + g) + b - 1) + u + 1, nop=True)
                        sp.dma_start(a_ring[:, u, :, :],
                                     A_tiles[:, u * TG:(u + 1) * TG, bass.ds(g * GR + b * HR, HR)]).then_inc(a_in[u], 16)

                def ends(g):
                    for j in range(TG):
                        ge(sp, end_ready, g * TG + j + 1, nop=True)
                        sp.dma_start(rows(xn2d[0:NP, :])[:, g * TG + j, :], xn2[:, j, :]).then_inc(end_st[j], 16)
                        sp.dma_start(rows(out[0:NP, :])[:, g * TG + j, :], base[:, j, :]).then_inc(end_st[j], 16)

                def z_loads(g, js):
                    for j in js:
                        ge(sp, acc_init, NT * l + g * TG - TG + j + 1, nop=True)
                        sp.dma_start(z_in[:, j, :], rows(zd[l])[:, g * TG + j, :]).then_inc(z_ld[j], 16)

                def layer(g):
                    first = isinstance(g, int) and g == 0
                    if l == 1 and first:
                        tiles_of_a(g, 0)
                        sp.wait_ge(w_done, NT)
                        sp.dma_start(gw_sb[:], gw[1]).then_inc(gw_in, 16)
                        for s in range(4):
                            sp.wait_ge(zn_st[s], 16 * TG * (2 if s < 3 else 1))
                        z_loads(g, range(TG))
                        sp.wait_ge(inv_st, 16 * TG)
                    else:
                        z_loads(g, range(0, 5))
                        tiles_of_a(g, 0, range(0, 4))
                        z_loads(g, range(5, TG))
                        tiles_of_a(g, 0, range(4, TG))
                    if l == 1:
                        ge(sp, agg_evac, 4 * (TG + g), nop=True)
                        sp.dma_start(inv[:], invd[0:1, bass.ds(g * GR, GR)].to_broadcast([P, GR])).then_inc(inv_ld, 16)
                        if first:
                            sp.wait_ge(a_used, 2 * TG * TG)
                            sp.dma_start(wr_sb, wr).then_inc(ffn_in, 16)
                            sp.dma_start(br_sb, br).then_inc(ffn_in, 16)
                            sp.dma_start(w1_sb, w1).then_inc(ffn_in, 16)
                        for j in range(TG):
                            ge(sp, x1_done, g * TG - TG + j + 1, nop=True)
                            sp.dma_start(xp_in[:, j, :], rows(xpd)[:, g * TG + j, :]).then_inc(xp_ld[j], 16)
                        if not first:
                            ends(g - 1)
                    tiles_of_a(g, 1)

                groups(sp, layer)
                if l == 1:
                    ends(TG - 1)
            sp.wait_ge(a_used, 4 * TG * TG)
            sp.wait_ge(w_done, 2 * NT)
            sp.dma_start(w2_sb, w2).then_inc(ffn_in, 16)
            sp.dma_start(b1_sb, b1).then_inc(ffn_in, 16)
            sp.dma_start(b2_sb, b2).then_inc(ffn_in, 16)
            sp.wait_ge(slots_ready, 2)
            sp.dma_start(chosen[TOPK:SLOTS, :].rearrange("s o -> o s"), pad_ids[0:1, :]).then_inc(pads_st, 16)
            sp.dma_start(xn2d[NP:NP + P, :], xn2[:, 0, :]).then_inc(pads_st, 16)
            sp.dma_start(out[NP:NP + P, :], xn2[:, 0, :]).then_inc(pads_st, 16)
            sp.wait_ge(pads_st, 48)
            sp.wait_ge(list_st, 16 * NT)
            sp.dma_start(idx, chosen[0:SLOTS, :].rearrange("(p c) o -> p (c o)", p=P)).then_inc(list_in, 16)

        @block.gpsimd
        def _(pool):
            nc.gpsimd.memset(ones_f[:], 1.0).then_inc(order_in, 1)
            pool.wait_ge(order_in, 1)
            nc.gpsimd.affine_select(out=ident[:], in_=ones_f[:], compare_op=ALU.is_equal, fill=0.0, base=0,
                                    pattern=[[-1, P]], channel_multiplier=1).then_inc(consts, 1)
            nc.gpsimd.iota(qid, pattern=[[0, 1]], base=0, channel_multiplier=1).then_inc(consts, 1)
            nc.gpsimd.iota(pos, pattern=[[1, F]], base=0, channel_multiplier=F,
                           allow_small_or_imprecise_dtypes=True).then_inc(consts, 1)
            nc.gpsimd.iota(same, pattern=[[1, F]], base=0, channel_multiplier=F).then_inc(consts, 1)
            nc.gpsimd.affine_select(out=tri[:], in_=ones_f[:], compare_op=ALU.is_ge, fill=0.0, base=0,
                                    pattern=[[1, P]], channel_multiplier=-1).then_inc(consts, 1)

            pool.wait_ge(a_zeroed, 16 * NT)
            pool.wait_ge(lists_ready, 2)
            by_turn = addr[:].rearrange("p (m q) -> p q m", q=P)
            by_turn_cnt = cnt16[:].rearrange("p (m q) -> p q m", q=P)
            cp = [0]

            def turn(i, s, n=TURN, sem_=None, q=None):
                q = 2 * i + s if q is None else q
                nc.gpsimd.tensor_copy(cur_addr[:, s, 0:n], by_turn[:, q, 0:n]).then_inc(idx_cp, 1)
                nc.gpsimd.tensor_copy(cur_cnt[:, s, 0:n], by_turn_cnt[:, q, 0:n]).then_inc(idx_cp, 1)
                ge(pool, idx_cp, 2 * q + 2, nop=True)
                for m in range(n):
                    nc.gpsimd.indirect_dma_start(A, bass.IndirectOffsetOnAxis(ap=cur_addr[:, s, m:m + 1], axis=0),
                                                 cur_cnt[:, s, m:m + 1], None).then_inc(scat[s] if sem_ is None else sem_, 16)

            def pair(i):
                for s in (0, 1):
                    if not (isinstance(i, int) and i == 0):
                        ge(pool, scat[s], 16 * TURN * i, nop=True)
                        pool.sem_inc(landed, 1)
                    turn(i, s)

            pair(0)
            with pool.Fori(1, TURNS // 2) as i:
                pair(i)
            pool.wait_ge(scat[0], 16 * TURN * (TURNS // 2))
            pool.sem_inc(landed, 1)
            turn(0, 0, LAST, scat[2], TURNS)
            pool.wait_ge(scat[1], 16 * TURN * (TURNS // 2))
            pool.sem_inc(landed, 1)
            pool.wait_ge(scat[2], 16 * LAST)
            pool.sem_inc(landed, 1)

            pool.wait_ge(wcol_ready, 1)
            nc.gpsimd.affine_select(out=wcol[:, NT - 1:NT], in_=wcol[:, NT - 1:NT], compare_op=ALU.is_ge,
                                    fill=-3.0e38, base=N - 1 - (NT - 1) * P, pattern=[[0, 1]],
                                    channel_multiplier=-1).then_inc(wcol_cut, 1)
            nc.gpsimd.iota(nid, pattern=[[P, NT]], base=0, channel_multiplier=1).then_inc(wcol_cut, 1)
            nc.gpsimd.iota(skip_i, pattern=[[P, NT]], base=LIST_SPARE, channel_multiplier=1).then_inc(wcol_cut, 1)
            nc.gpsimd.iota(pad_ids, pattern=[[1, SLOTS - TOPK]], base=NP, channel_multiplier=0).then_inc(wcol_cut, 1)
            pool.wait_ge(slots_ready, 1)
            for t in range(NT):
                nc.gpsimd.indirect_dma_start(chosen, bass.IndirectOffsetOnAxis(ap=slot_i[:, t:t + 1], axis=0),
                                             nid[:, t:t + 1], None).then_inc(list_st, 16)
            pool.wait_ge(list_in, 16)
            for j in range(TG):
                pool.wait_ge(end_st[j], 32 * TG)

            CP0 = 2 * TURNS + 2

            def gathers(g):
                ge(pool, h_done, 16 * g, nop=True)
                ge(pool, yo_ready, CH * g, nop=True)
                nc.gpsimd.tensor_copy(cur_g, idx[:, bass.ds(g * CH, CH)]).then_inc(idx_cp, 1)
                ge(pool, idx_cp, CP0 + 2 * g + 1, nop=True)
                for j in range(CH):
                    nc.gpsimd.indirect_dma_start(xg[:, j, :], None, xn2d,
                                                 bass.IndirectOffsetOnAxis(ap=cur_g[:, j:j + 1], axis=0)).then_inc(g_in[j], 16)
                    nc.gpsimd.indirect_dma_start(bg[:, j, :], None, out,
                                                 bass.IndirectOffsetOnAxis(ap=cur_g[:, j:j + 1], axis=0)).then_inc(g_in[j], 16)

            def scatters(g):
                if not (isinstance(g, int) and g == 0):
                    for j in range(CH):
                        ge(pool, y_st[j], 16 * g, nop=True)
                nc.gpsimd.tensor_copy(cur_s, idx[:, bass.ds(g * CH, CH)]).then_inc(idx_cp, 1)
                ge(pool, idx_cp, CP0 + 2 * g + 2, nop=True)
                for j in range(CH):
                    ge(pool, yo_ready, CH * g + j + 1, nop=True)
                    nc.gpsimd.indirect_dma_start(out, bass.IndirectOffsetOnAxis(ap=cur_s[:, j:j + 1], axis=0),
                                                 yo[:, j, :], None).then_inc(y_st[j], 16)

            gathers(0)
            scatters(0)
            with pool.Fori(1, CH) as g:
                gathers(g)
                scatters(g)
            for j in range(CH):
                pool.wait_ge(y_st[j], 16 * CH)

        @block.scalar
        def _(act):
            act.wait_ge(zero_made, 1)
            with act.Fori(0, NT) as t:
                act.dma_start(A_tiles[:, t, 0:NP], zero_rows).then_inc(a_zeroed, 16)
            a = sum(range(1, ROW_BITS + 1)) % 2
            c = 0
            for k in range(ROW_BITS + 1, BITS + 1):
                for stages in (k - ROW_BITS, ROW_BITS):
                    c += 1
                    act.wait_ge(tposed, 2 * c - 1)
                    nc.scalar.copy(keys[1 - a][:, 0:F // 2], ps_sort[:, 0:F // 2]).then_inc(half_copied, 1)
                    a = (a + 1 + stages) % 2
            act.wait_ge(a_zeroed, 16 * NT)

            def deviations(g):
                act.wait_ge(var_ready, g + 1)
                nc.scalar.activation(std[:], mv[:, :, 1], ACT.Sqrt, bias=eps[:]).then_inc(std_ready, 1)

            def first(g, more=True):
                for s in range(TG + 2):
                    if s == 5 and more:
                        deviations(g + 1)
                    if s < TG:
                        n = g * TG + s
                        act.wait_ge(xn_done, n + 1)
                        nc.scalar.copy(zs1[:, n, 0, :], xn[:, s, :]).then_inc(hi_done, 1)
                        act.wait_ge(xT_done, n + 1)
                        ge(act, kv_done, n + 1 - TG)
                        ge(act, xT_st[s], 16 * g)
                        nc.scalar.copy(xnT[:, s, :], ps_T[:, s % 2, :]).then_inc(xT_copied, 1)
                    if 1 <= s <= TG:
                        j = s - 1
                        n = g * TG + j
                        act.wait_ge(kv_done, n + 1)
                        ge(act, ss_done, g * TG + before(j, 2))
                        nc.scalar.activation(sq[:, j % 2, :], ps_kv[j % 2], ACT.Square).then_inc(sq_done, 1)
                        ge(act, dots_done, g * TG + before(j, 2))
                        nc.scalar.copy(k_sb[:, j % 2, :], ps_kv[j % 2][:, 0:512])
                    if s >= 2:
                        j = s - 2
                        n = g * TG + j
                        act.wait_ge(ss_done, n + 1)
                        ge(act, v_done, g * TG + before(j, 2))
                        nc.scalar.activation(sd[:, j % 2, :], ss[:, j % 2, :], ACT.Sqrt, bias=eps[:],
                                             scale=1.0 / HEAD).then_inc(sd_done, 1)

            deviations(0)
            first(0)
            with act.Fori(1, TG - 1) as g:
                first(g)
            first(TG - 1, False)
            act.wait_ge(gm_done, 1)
            nc.scalar.copy(g_sb.rearrange("p c e -> p (c e)"), ps_kv[0]).then_inc(gm_copied, 1)
            act.wait_ge(gm_done, 2)
            nc.scalar.copy(m_sb.rearrange("p c e -> p (c e)"), ps_kv[1][:, 0:512]).then_inc(gm_copied, 1)

            for l in range(2):
                def layer(g):
                    G = g + TG * l
                    for i, js in enumerate(T_ORDER):
                        act.wait_ge(t_done, G * TB + i + 1)
                        nc.scalar.copy(zT[:, js[0]:js[-1] + 1, :].rearrange("p j d -> p (j d)"),
                                       ps_zT[:, js[0] * D:(js[-1] + 1) * D]).then_inc(t_copied, 1)
                    act.wait_ge(lg_sub, G + 1)
                    nc.scalar.activation(lg[:], lg[:], ACT.Exp).then_inc(lg_exp, 1)
                    for s in range(TG + 1):
                        if l == 0 and s == 5:
                            act.wait_ge(agg_evac, 4 * G + 4)
                            act.dma_start(invd[0:1, bass.ds(g * GR, GR)], inv[0:1, :]).then_inc(inv_st, 16)
                        if s < TG:
                            n = G * TG + s
                            act.wait_ge(wts_ready, G + 1)
                            act.wait_ge(z_ld[s], 16 * (G + 1))
                            if l == 1:
                                ge(act, x1_done, g * TG + before(s, 2))
                            else:
                                ge(act, hi2_done, g * TG + before(s, 2))
                            nc.scalar.activation(acc[:, s % 2, :], z_in[:, s, :], ACT.Copy,
                                                 scale=wsum[:, s:s + 1]).then_inc(acc_init, 1)
                        if s >= 1 and l == 0:
                            j = s - 1
                            n = G * TG + j
                            act.wait_ge(acc_done, n + 1)
                            ge(act, zn_st[j % 4], 16 * ((2 if j % 4 < 3 else 1) * g + j // 4))
                            ge(act, lo2_done, g * TG + before(j, 4))
                            nc.scalar.activation(zn[:, j % 4, :], acc[:, j % 2, :], ACT.Relu).then_inc(zn_ready, 1)
                            nc.scalar.activation(zs2[:, n, 0, :], acc[:, j % 2, :], ACT.Relu).then_inc(hi2_done, 1)
                            act.wait_ge(zn_ready, n + 1)
                            act.dma_start(rows(zd[1])[:, n, :], zn[:, j % 4, :]).then_inc(zn_st[j % 4], 16)
                    if l == 1:
                        act.wait_ge(var2_ready, g + 1)
                        nc.scalar.activation(std[:], mv[:, :, 1], ACT.Sqrt, bias=eps[:]).then_inc(std2_ready, 1)

                groups(act, layer)

            def ffn(g):
                for j in range(CH):
                    act.wait_ge(f_t, CH * g + j + 1)
                    nc.scalar.copy(x2T[:, :, j * P:(j + 1) * P],
                                   ps_T[:, j % 2, :].rearrange("p (k r) -> p k r", k=2)).then_inc(f_tc, 1)
                for half in range(2):
                    for m in range(8):
                        q = half * 8 + m
                        act.wait_ge(h_done, 16 * g + q + 1)
                        if q == 0:
                            ge(act, y_done, CH * g)
                        nc.scalar.activation(hT[:, m, half * FH:(half + 1) * FH], bank(q % 2)[:, 0:FH],
                                             ACT.Gelu_apprx_tanh, bias=b1_sb[:, m:m + 1]).then_inc(h_act, 1)

            act.wait_ge(ffn_in, 96)
            ffn(0)
            with act.Fori(1, CH) as g:
                ffn(g)

        @block.vector
        def _(dve):
            base_n, k_n = [0], [0]

            def link(ins):
                k_n[0] += 1
                ins.then_inc(step, 1)
                dve.wait_ge(step, base_n[0] + k_n[0])

            def linked(body, count=TG, last_apart=False):
                start = base_n[0] + k_n[0]
                base_n[0], k_n[0] = start, 0
                body(0)
                per = k_n[0]
                looped = count - 1 if last_apart else count
                with dve.Fori(1, looped) as g:
                    base_n[0], k_n[0] = start + g * per, 0
                    body(g)
                    assert k_n[0] == per
                base_n[0], k_n[0] = start + looped * per, 0
                if last_apart:
                    body(count - 1, False)

            I = lambda ap: ap.bitcast(i32)
            nc.vector.memset(zero_rows.bitcast(f32), 0.0).then_inc(zero_made, 1)
            link(nc.vector.memset(I(keys[0]), KEY_PAD))
            link(nc.vector.memset(ones16[:], 1.0))
            link(nc.vector.memset(eps[:], EPS))
            dve.wait_ge(edges_in, 32)
            link(nc.vector.tensor_scalar(src_in[0:EP, :], src_in[0:EP, :], CB, KEY_BASE, ALU.logical_shift_left, ALU.bitwise_or))
            link(nc.vector.tensor_tensor(I(keys[0][0:EP, 0:EC]), dst_in[0:EP, :], src_in[0:EP, :], ALU.bitwise_or))
            dve.wait_ge(consts, 5)
            link(nc.vector.memset(qbit, 0))
            for b in range(7):
                link(nc.vector.tensor_scalar(qbit[:, b + 1:b + 2], qid, b, 1, ALU.logical_shift_right, ALU.bitwise_and))
            link(nc.vector.tensor_tensor(qxor, qbit[:, 0:8], qbit[:, 1:9], ALU.bitwise_xor))
            link(nc.vector.tensor_scalar(sgn[:, 0:8], qxor, -2.0, 1.0, ALU.mult, ALU.add))
            link(nc.vector.tensor_scalar(sgn[:, 8:9], sgn[:, 0:1], -1.0, None, ALU.mult))
            link(nc.vector.tensor_scalar(tmp, same, NODE, CB, ALU.bitwise_and, ALU.logical_shift_left))
            link(nc.vector.tensor_scalar(spare, same, CB, KEY_BASE | SPARE, ALU.logical_shift_right, ALU.bitwise_or))
            link(nc.vector.tensor_tensor(spare, spare, tmp, ALU.bitwise_or))

            a = [0]

            def exchange(d):
                s = keys[a[0]].rearrange("p (n two d) -> p n two d", two=2, d=d)
                t = keys[1 - a[0]].rearrange("p (n two d) -> p n two d", two=2, d=d)
                nc.vector.tensor_tensor(t[:, :, 0, :], s[:, :, 0, :], s[:, :, 1, :], ALU.min).then_inc(step, 1)
                k_n[0] += 1
                link(nc.vector.tensor_tensor(t[:, :, 1, :], s[:, :, 0, :], s[:, :, 1, :], ALU.max))
                a[0] = 1 - a[0]

            v = keys[0].rearrange("p (n four) -> p n four", four=4)
            link(nc.vector.tensor_scalar(v[:, :, 2:4], v[:, :, 2:4], -1.0, None, ALU.mult))
            turned = 0
            for k in range(1, BITS + 1):
                if k > ROW_BITS:
                    for half in (0, 1):
                        turned += 1
                        nc.vector.sem_inc(order_out, 1)
                        dve.wait_ge(tposed, 2 * turned)
                        link(nc.vector.tensor_copy(keys[1 - a[0]][:, F // 2:F], ps_sort[:, F // 2:F]))
                        dve.wait_ge(half_copied, turned)
                        a[0] = 1 - a[0]
                        if half == 0:
                            for b in range(k - ROW_BITS - 1, -1, -1):
                                exchange(1 << b)
                for b in range(min(k, ROW_BITS) - 1, -1, -1):
                    exchange(1 << b)
                K = keys[a[0]]
                if k < ROW_BITS - 1:
                    v = K.rearrange("p (n q) -> p n q", q=1 << (k + 2))[:, :, (1 << k):(3 << k)]
                    link(nc.vector.tensor_scalar(v, v, -1.0, None, ALU.mult))
                elif k == ROW_BITS - 1:
                    h = F // 2
                    nc.vector.tensor_scalar(K[:, 0:h], K[:, 0:h], sgn[:, 0:1], None, ALU.mult).then_inc(step, 1)
                    k_n[0] += 1
                    link(nc.vector.tensor_scalar(K[:, h:F], K[:, h:F], sgn[:, 8:9], None, ALU.mult))
                elif k < BITS:
                    b = k - ROW_BITS + 1
                    link(nc.vector.tensor_scalar(K, K, sgn[:, b:b + 1], None, ALU.mult))
            if a[0] == 1:
                link(nc.vector.tensor_copy(keys[0], keys[1]))
            K = keys[0]

            link(nc.vector.memset(edge_next, 0.0))
            link(nc.vector.memset(edge_prev, 0.0))
            link(nc.vector.memset(cexcl, 0.0))
            nc.vector.sem_inc(sorted_s, 1)
            link(nc.vector.tensor_tensor(same[:, 0:F - 1], K[:, 0:F - 1], K[:, 1:F], ALU.is_equal))
            link(nc.vector.tensor_tensor(run[:, 1:F], K[:, 0:F - 1], K[:, 1:F], ALU.not_equal))
            dve.wait_ge(carry_s, 32)
            link(nc.vector.tensor_tensor(same[:, F - 1:F], K[:, F - 1:F], edge_next, ALU.is_equal))
            link(nc.vector.tensor_tensor(run[:, 0:1], K[:, 0:1], edge_prev, ALU.not_equal))
            link(nc.vector.tensor_tensor(run, run, pos, ALU.mult))
            link(nc.vector.tensor_tensor_scan(keys[1], run, run, 0.0, ALU.max, ALU.max))
            nc.vector.sem_inc(sorted_s, 1)
            link(nc.vector.copy_predicated(I(K), same, spare))
            dve.wait_ge(carry_s, 64)
            link(nc.vector.tensor_tensor_scan(cexcl[0:1, 1:P + 1], crow[0:1, 0:P], crow[0:1, 0:P], 0.0, ALU.max, ALU.max))
            nc.vector.sem_inc(sorted_s, 1)
            nc.vector.sem_inc(order_out, 1)
            dve.wait_ge(carry_s, 96)
            link(nc.vector.scalar_tensor_tensor(keys[1], keys[1], carry, pos, ALU.max, ALU.subtract))
            link(nc.vector.tensor_scalar(keys[1], keys[1], -1.0, 1.0, ALU.mult, ALU.add))
            dve.wait_ge(tposed, 2 * turned + 2)
            link(nc.vector.tensor_copy(run, ps_sort))
            nc.vector.sem_inc(order_out, 1)
            link(nc.vector.tensor_scalar(tmp, I(run), NODE, CB, ALU.bitwise_and, ALU.logical_shift_left))
            link(nc.vector.tensor_scalar(same, I(run), CB, NODE, ALU.logical_shift_right, ALU.bitwise_and))
            nc.vector.tensor_tensor(addr[:], tmp, same, ALU.bitwise_or).then_inc(lists_ready, 1)
            dve.wait_ge(tposed, 2 * turned + 4)
            nc.vector.tensor_copy(cnt16[:], ps_sort).then_inc(lists_ready, 1)
            dve.wait_ge(lists_ready, 2)
            for i in range(2 * TG):
                limit = float(np.array(KEY_BASE + ((i + 1) * HR << CB), np.int32).view(np.float32))
                link(nc.vector.tensor_scalar(run[0:EP, 0:EC], src_in[0:EP, :].bitcast(f32), limit, None, ALU.is_lt, ALU.add,
                                             accum_out=below[0:EP, i:i + 1]))
            nc.vector.sem_inc(below_ready, 1)
            dve.wait_ge(below_summed, 1)
            link(nc.vector.tensor_copy(bound[:], bank(0)[:, 0:2 * TG]))
            link(nc.vector.tensor_scalar(bound[:], bound[:], ROW_BITS, None, ALU.logical_shift_right))
            nc.vector.tensor_scalar(bound[:], bound[:], 1, None, ALU.add).then_inc(bound_ready, 1)
            nc.vector.sem_inc(early_free, 1)

            dve.wait_ge(wmix_in, 64)
            heads = wkv_sb.rearrange("p c (h e) -> p c h e", e=HEAD)
            link(nc.vector.reduce_sum(wmean, heads, AX))
            link(nc.vector.tensor_scalar(wmean, wmean, 1.0 / HEAD, None, ALU.mult))
            for kc in range(2):
                link(nc.vector.tensor_tensor(heads[:, kc], heads[:, kc],
                                             wmean[:, kc, :].unsqueeze(2).to_broadcast([P, 16, HEAD]), ALU.subtract))
            nc.vector.memset(dT, 0.0).then_inc(wkv_ready, 1)

            def statistics(g):
                for j in range(TG):
                    dve.wait_ge(x_ld[j], 16 * (g + 1))
                    ins = nc.vector.bn_stats(stats[:, j, :], x_in[:, j, :])
                    if j < TG - 1:
                        ins.then_inc(step, 1)
                        k_n[0] += 1
                link(ins)
                nc.vector.nop(nofuse=True)
                for j in range(TG):
                    ins = nc.vector.bn_aggr(mv[:, j, :], stats[:, j, :])
                ins.then_inc(var_ready, 1)

            def normalise(g):
                dve.wait_ge(std_ready, g + 1)
                link(nc.vector.reciprocal(rstd[:], std[:]))
                for j in range(TG):
                    n = g * TG + j
                    ge(dve, hi_done, n + 1 - TG)
                    ge(dve, xT_done, n + 1 - TG)
                    ge(dve, lo_done, n + 1 - TG)
                    ge(dve, xn_st[j], 16 * g)
                    nc.vector.tensor_scalar(xn[:, j, :], x_in[:, j, :], mv[:, j, 0:1], rstd[:, j:j + 1],
                                            ALU.subtract, ALU.mult).then_inc(xn_done, 1)

            def first(g, more=True):
                for s in range(TG + 1):
                    if s == 4 and more:
                        statistics(g + 1)
                    if s < TG:
                        n = g * TG + s
                        dve.wait_ge(hi_done, n + 1)
                        nc.vector.tensor_tensor(zs1[:, n, 1, :], xn[:, s, :], zs1[:, n, 0, :], ALU.subtract).then_inc(lo_done, 1)
                        if s == TG - 1 and more:
                            normalise(g + 1)
                        dve.wait_ge(sq_done, n + 1)
                        ge(dve, sd_done, g * TG + before(s, 2))
                        nc.vector.reduce_sum(ss[:, s % 2, :], sq[:, s % 2, :].rearrange("p (h e) -> p h e", e=HEAD),
                                             AX).then_inc(ss_done, 1)
                    if s >= 1:
                        j = s - 1
                        n = g * TG + j
                        dve.wait_ge(sd_done, n + 1)
                        link(nc.vector.reciprocal(rs, sd[:, j % 2, :]))
                        ge(dve, v_done, n)
                        link(nc.vector.tensor_tensor(rr, rs[:, 0:8], rs[:, 8:16], ALU.mult))
                        ge(dve, dots_done, g * TG + before(j, 2))
                        nc.vector.tensor_tensor(v_sb[:, j % 2, :].rearrange("p (h e) -> p h e", e=HEAD),
                                                ps_kv[j % 2][:, 512:1024].rearrange("p (h e) -> p h e", e=HEAD),
                                                rr.unsqueeze(2).to_broadcast([P, 8, HEAD]), ALU.mult).then_inc(v_done, 1)

            statistics(0)
            normalise(0)
            linked(first, last_apart=True)
            dve.wait_ge(dots_done, NT)
            dd = ps_dots.rearrange("p (c e) -> p c e", c=4)
            for h in range(2):
                q = slice(h * HEAD, (h + 1) * HEAD)
                nc.vector.tensor_scalar(dT[q, :, q], dd[q, :, q], 1.0 / N, None, ALU.mult).then_inc(dT_done, 1)

            def mix(g):
                for j in range(TG):
                    n = g * TG + j
                    dve.wait_ge(mix_done, n + 1)
                    ge(dve, xp_st[j], 16 * g)
                    link(nc.vector.tensor_tensor(xn[:, j, :], bank(j % 4)[:, 0:D], x_in[:, j, :], ALU.add))
                    nc.vector.tensor_tensor(xn[:, j, :], xn[:, j, :], bo_sb, ALU.add).then_inc(xp_ready, 1)

            dve.wait_ge(lo_done, NT)
            linked(mix)

            for l in range(2):
                def layer(g):
                    G = g + TG * l
                    dve.wait_ge(logit_done, G + 1)
                    nc.vector.tensor_tensor(lg[:], ps_lg, envb_sb[:, l, :].unsqueeze(1).to_broadcast([P, TG, EXPERTS]),
                                            ALU.add).then_inc(lg_read, 1)
                    dve.wait_ge(lg_read, G + 1)
                    link(nc.vector.reduce_max(red[:, 0, :], lg[:], AX))
                    nc.vector.tensor_tensor(lg[:], lg[:], red[:, 0, :].unsqueeze(2).to_broadcast([P, TG, EXPERTS]),
                                            ALU.subtract).then_inc(lg_sub, 1)
                    dve.wait_ge(lg_exp, G + 1)
                    link(nc.vector.reduce_sum(red[:, 1, :], lg[:], AX))
                    link(nc.vector.reciprocal(red[:, 2, :], red[:, 1, :]))
                    link(nc.vector.tensor_tensor(wts[:], lg[:], red[:, 2, :].unsqueeze(2).to_broadcast([P, TG, EXPERTS]),
                                                 ALU.mult))
                    nc.vector.reduce_sum(wsum[:], wts[:], AX).then_inc(wts_ready, 1)

                    def evacuate(b):
                        dve.wait_ge(a_used, TG * (2 * G + b + 1))
                        cols = slice(b * HR, (b + 1) * HR)
                        if l == 0:
                            if b == 0:
                                ge(dve, inv_st, 16 * g)
                            link(nc.vector.tensor_scalar(inv[:, cols], ps_cnt[b][:, 0:HR], 1.0, None, ALU.max))
                            link(nc.vector.reciprocal(inv[:, cols], inv[:, cols]))
                        else:
                            dve.wait_ge(inv_ld, 16 * (g + 1))
                        for half in range(2):
                            nc.vector.tensor_tensor(aggT[:, half, cols], ps_agg[b][half][:, 0:HR], inv[:, cols],
                                                    ALU.mult).then_inc(agg_evac, 1)

                    evacuate(0)
                    for s in range(TG + 1):
                        if s == 3:
                            evacuate(1)
                        if s < TG:
                            n = G * TG + s
                            dve.wait_ge(w_done, n + 1)
                            dve.wait_ge(acc_init, n + 1)
                            for e in range(EXPERTS):
                                ins = nc.vector.scalar_tensor_tensor(
                                    acc[:, s % 2, :], ps_out[s % 2][:, e * D:(e + 1) * D], wts[:, s, e:e + 1],
                                    acc[:, s % 2, :], ALU.mult, ALU.add)
                                if e < EXPERTS - 1:
                                    link(ins)
                            ins.then_inc(acc_done, 1)
                            if l == 1:
                                dve.wait_ge(acc_done, n + 1)
                                dve.wait_ge(xp_ld[s], 16 * (g + 1))
                                ge(dve, end_ready, g * TG - TG + s + 1)
                                nc.vector.scalar_tensor_tensor(x1[:, s, :], acc[:, s % 2, :], 0.0, xp_in[:, s, :],
                                                               ALU.max, ALU.add).then_inc(x1_done, 1)
                                dve.wait_ge(x1_done, g * TG + s + 1)
                                link(nc.vector.bn_stats(stats[:, s, :], x1[:, s, :]))
                        if s >= 1 and l == 0:
                            j = s - 1
                            n = G * TG + j
                            dve.wait_ge(hi2_done, n + 1)
                            nc.vector.tensor_tensor(zs2[:, n, 1, :], zn[:, j % 4, :], zs2[:, n, 0, :],
                                                    ALU.subtract).then_inc(lo2_done, 1)
                    if l == 1:
                        nc.vector.nop(nofuse=True)
                        for j in range(TG):
                            ins = nc.vector.bn_aggr(mv[:, j, :], stats[:, j, :])
                        ins.then_inc(var2_ready, 1)
                        dve.wait_ge(std2_ready, g + 1)
                        link(nc.vector.reciprocal(rstd[:], std[:]))
                        if isinstance(g, int) and g == 0:
                            dve.wait_ge(ffn_in, 48)
                        for j in range(TG):
                            ge(dve, end_st[j], 32 * g)
                            link(nc.vector.tensor_scalar(xn2[:, j, :], x1[:, j, :], mv[:, j, 0:1], rstd[:, j:j + 1],
                                                         ALU.subtract, ALU.mult))
                            nc.vector.tensor_tensor(base[:, j, :], x1[:, j, :], xn2[:, j, :], ALU.add).then_inc(end_ready, 1)
                            link(nc.vector.tensor_tensor_reduce(junk, xn2[:, j, :], wr_sb, 1.0, 0.0, ALU.mult, ALU.add,
                                                                red[:, 3, j:j + 1]))
                        link(nc.vector.tensor_scalar(wcol[:, bass.ds(g * TG, TG)], red[:, 3, :], br_sb, None, ALU.add))

                linked(layer)

            nc.vector.sem_inc(wcol_ready, 1)
            dve.wait_ge(wcol_cut, 4)
            for j in range(TG):
                dve.wait_ge(end_st[j], 32 * TG)
            link(nc.vector.memset(xn2[:, 0, :], 0.0))
            link(nc.vector.memset(u_t, 0))

            asked = [0]

            def as_float(u, target):
                link(nc.vector.tensor_scalar(t1, u, 31, 0x7FFFFFFF, ALU.arith_shift_right, ALU.bitwise_and))
                link(nc.vector.tensor_tensor(target, t1, u, ALU.bitwise_xor))
                link(nc.vector.tensor_scalar(target, target, -1, None, ALU.bitwise_xor))

            def count(target, op):
                link(nc.vector.tensor_scalar(hits, wcol[:], target.bitcast(f32), None, op, ALU.add, accum_out=part))
                nc.vector.sem_inc(cand_ready, 1)
                asked[0] += 1
                dve.wait_ge(counted, asked[0])

            for b in range(31, -1, -1):
                bit = (1 << b) if b < 31 else -(1 << 31)
                link(nc.vector.tensor_scalar(cand, u_t, bit, None, ALU.bitwise_or))
                as_float(cand, take)
                count(take, ALU.is_ge)
                link(nc.vector.tensor_scalar(t1, bank(5)[:, 0:1], TOPK - 0.5, float(bit), ALU.is_ge, ALU.mult))
                link(nc.vector.tensor_tensor(u_t, u_t, t1, ALU.bitwise_or))
            as_float(u_t, take)
            thr = take.bitcast(f32)
            count(take, ALU.is_gt)
            link(nc.vector.tensor_copy(ntot, bank(5)[:, 0:1]))
            link(nc.vector.tensor_scalar(ntot, ntot, -1.0, float(TOPK), ALU.mult, ALU.add))
            link(nc.vector.tensor_scalar(gt, wcol[:], thr, None, ALU.is_gt))
            link(nc.vector.tensor_scalar(eq, wcol[:], thr, None, ALU.is_equal))

            def ranks(flags, into):
                nc.vector.sem_inc(cand_ready, 1)
                asked[0] += 1
                dve.wait_ge(counted, asked[0])
                link(nc.vector.tensor_copy(tot, bank(6)[:, 64:64 + NT]))
                link(nc.vector.tensor_tensor_scan(scan, tot, tot, 0.0, ALU.add, ALU.bypass))
                link(nc.vector.tensor_tensor(scan, scan, tot, ALU.subtract))
                link(nc.vector.tensor_tensor(into, bank(6)[:, 0:NT], scan, ALU.add))

            ranks(eq, cum)
            link(nc.vector.tensor_scalar(cum, cum, ntot, None, ALU.is_le))
            link(nc.vector.tensor_tensor(eq, eq, cum, ALU.mult))
            link(nc.vector.tensor_tensor(sel, eq, gt, ALU.add))
            ranks(sel, cum)
            link(nc.vector.tensor_scalar(slot_i, cum, -1.0, None, ALU.add))
            link(nc.vector.tensor_scalar(hits, sel, -1.0, 1.0, ALU.mult, ALU.add))
            link(nc.vector.tensor_copy(I(tot), hits))
            link(nc.vector.copy_predicated(slot_i, I(tot), skip_i))
            nc.vector.sem_inc(slots_ready, 2)

            def ffn(g):
                ge(dve, yo_ready, CH * g)
                for j in range(CH):
                    dve.wait_ge(g_in[j], 32 * (g + 1))
                    link(nc.vector.tensor_tensor_reduce(fj, xg[:, j, :], wr_sb, 1.0, 0.0, ALU.mult, ALU.add, fw[:, j:j + 1]))
                link(nc.vector.tensor_scalar(fw, fw, br_sb, None, ALU.add))
                for j in range(CH):
                    dve.wait_ge(y_done, CH * g + j + 1)
                    ge(dve, y_st[j], 16 * g)
                    ge(dve, yo_ready, CH * g + (j - 1 if j >= 2 else 0))
                    nc.vector.tensor_tensor(yt[:, j % 2, :], bank(2 + j % 2)[:, 0:D], b2_sb, ALU.add).then_inc(y_read, 1)
                    dve.wait_ge(y_read, CH * g + j + 1)
                    nc.vector.scalar_tensor_tensor(yo[:, j, :], yt[:, j % 2, :], fw[:, j:j + 1], bg[:, j, :],
                                                   ALU.mult, ALU.add).then_inc(yo_ready, 1)

            dve.wait_ge(ffn_in, 96)
            start = base_n[0] + k_n[0]
            base_n[0], k_n[0] = start, 0
            ffn(0)
            per = k_n[0]
            with dve.Fori(1, CH) as g:
                base_n[0], k_n[0] = start + g * per, 0
                ffn(g)

        @block.tensor
        def _(pe):
            pe.wait_ge(consts, 1)
            a = sum(range(1, ROW_BITS + 1)) % 2
            c = 0

            def turn_over(K):
                pe.wait_ge(order_out, c)
                for m in range(F // P):
                    last = nc.tensor.transpose(ps_sort[:, m * P:(m + 1) * P], K[:, m * P:(m + 1) * P], ident[:])
                    if m % (F // P // 2) == F // P // 2 - 1:
                        last.then_inc(tposed, 1)

            for k in range(ROW_BITS + 1, BITS + 1):
                for stages in (k - ROW_BITS, ROW_BITS):
                    c += 1
                    turn_over(keys[a])
                    a = (a + 1 + stages) % 2
            c += 1
            turn_over(keys[0])
            c += 1
            turn_over(keys[1])

            pe.wait_ge(below_ready, 1)
            nc.tensor.matmul(bank(0)[:, 0:2 * TG], ones_f[0:EP, :], below[0:EP, :], start=True, stop=True).then_inc(below_summed, 1)

            pe.wait_ge(wkv_ready, 1)
            pe.wait_ge(bound_ready, 1)

            def first(g):
                for s in range(TG + 2):
                    if s < TG:
                        pe.wait_ge(xn_done, g * TG + s + 1)
                        ge(pe, xT_copied, g * TG + before(s, 2))
                        for kc in range(2):
                            last = nc.tensor.transpose(ps_T[:, s % 2, kc * P:(kc + 1) * P], xn[:, s, kc * P:(kc + 1) * P], ident[:])
                        last.then_inc(xT_done, 1)
                    if 1 <= s <= TG:
                        j = s - 1
                        pe.wait_ge(xT_copied, g * TG + j + 1)
                        ge(pe, v_done, g * TG + before(j, 2))
                        for b in range(2):
                            for kc in range(2):
                                last = nc.tensor.matmul(ps_kv[j % 2][:, b * 512:(b + 1) * 512], xnT[:, j, kc * P:(kc + 1) * P],
                                                        wkv_sb[:, kc, b * 512:(b + 1) * 512], start=(kc == 0), stop=(kc == 1))
                        last.then_inc(kv_done, 1)
                    if s >= 2:
                        j = s - 2
                        pe.wait_ge(v_done, g * TG + j + 1)
                        for c4 in range(4):
                            q = slice(c4 * P, (c4 + 1) * P)
                            last = nc.tensor.matmul(ps_dots[:, q], v_sb[:, j % 2, q], k_sb[:, j % 2, q],
                                                    start=(isinstance(g, int) and g == 0 and j == 0 and c4 == 0), stop=True,
                                                    skip_group_check=True)
                        last.then_inc(dots_done, 1)

            groups(pe, first)
            pe.wait_ge(dT_done, 2)
            for c4 in range(4):
                last = nc.tensor.matmul(ps_kv[0][:, c4 * D:(c4 + 1) * D], dT[:, c4, :], wo_sb[:, c4, :], start=True, stop=True)
            last.then_inc(gm_done, 1)
            pe.wait_ge(gm_copied, 1)
            for half in range(2):
                for c4 in range(4):
                    last = nc.tensor.matmul(ps_kv[1][:, half * D:(half + 1) * D], wq_sb[:, c4, half * P:(half + 1) * P],
                                            g_sb[:, c4, :], start=(c4 == 0), stop=(c4 == 3))
            last.then_inc(gm_done, 1)
            pe.wait_ge(gm_copied, 2)

            def mix(g):
                for j in range(TG):
                    pe.wait_ge(x_ld[j], 16 * TG + 32 * (g + 1))
                    ge(pe, xp_ready, g * TG + before(j, 4) if j >= 4 else (g * TG - TG + max(i for i in range(TG) if i % 4 == j % 4) + 1))
                    for kc in range(2):
                        last = nc.tensor.matmul(bank(j % 4)[:, 0:D], xnT[:, j, kc * P:(kc + 1) * P], m_sb[:, kc, :],
                                                start=(kc == 0), stop=(kc == 1))
                    last.then_inc(mix_done, 1)

            groups(pe, mix)
            pe.wait_ge(xp_ready, NT)
            pe.wait_ge(small_in, 32)

            for l in range(2):
                zs = zs1 if l == 0 else zs2
                pe.wait_ge(lo_done if l == 0 else lo2_done, NT)
                if l == 1:
                    pe.wait_ge(hi2_done, NT)

                def aggregate(g, b, between=None):
                    G = g + TG * l
                    ge(pe, agg_evac, 4 * G + 2 * b)
                    for u in range(TG):
                        if between is not None and u == 2:
                            between()
                        pe.wait_ge(a_in[u], 16 * (2 * G + b + 1))
                        for cc in range(TG):
                            ct = u * TG + cc
                            if l == 0:
                                nc.tensor.matmul(ps_cnt[b][:, 0:HR], ones16[:], a_ring[:, u, cc, :],
                                                 start=(ct == 0), stop=(ct == NT - 1))
                            for half in range(2):
                                for part_ in range(2):
                                    last = nc.tensor.matmul(
                                        ps_agg[b][half][:, 0:HR], zs[:, ct, part_, half * P:(half + 1) * P], a_ring[:, u, cc, :],
                                        start=(ct == 0 and part_ == 0), stop=(ct == NT - 1 and part_ == 1))
                        last.then_inc(a_used, 1)

                def layer(g):
                    G = g + TG * l
                    for js in T_ORDER:
                        ge(pe, acc_done, G * TG - (1 if js[0] >= 4 else 0))
                        for j in js:
                            pe.wait_ge(z_ld[j], 16 * (G + 1))
                            for kc in range(2):
                                last = nc.tensor.transpose(ps_zT[:, j * D + kc * P:j * D + (kc + 1) * P],
                                                           z_in[:, j, kc * P:(kc + 1) * P], ident[:])
                        last.then_inc(t_done, 1)

                    def logits():
                        pe.wait_ge(t_copied, (G + 1) * TB)
                        for j in range(TG):
                            for kc in range(2):
                                last = nc.tensor.matmul(ps_lg[:, j, :], zT[:, j, kc * P:(kc + 1) * P], envw_sb[:, l, kc, :],
                                                        start=(kc == 0), stop=(kc == 1))
                        last.then_inc(logit_done, 1)

                    def experts(j):
                        ge(pe, acc_done, G * TG + before(j, 2))
                        if j == 1:
                            pe.wait_ge(lg_read, G + 1)
                        for b in range(2):
                            q = slice(b * 512, (b + 1) * 512)
                            for i, kc in enumerate((2, 3, 0, 1)):
                                if b == 0 and i == 2:
                                    pe.wait_ge(agg_evac, 4 * G + (2 if j < 3 else 4))
                                w = zT[:, j, (kc - 2) * P:(kc - 1) * P] if kc >= 2 else aggT[:, kc, j * P:(j + 1) * P]
                                last = nc.tensor.matmul(ps_out[j % 2][:, q], w, gw_sb[:, kc, q], start=(i == 0), stop=(i == 3))
                        last.then_inc(w_done, 1)

                    aggregate(g, 0, logits)
                    if isinstance(g, int) and g == 0:
                        pe.wait_ge(gw_in, 16 * (l + 1))
                    for j in range(3):
                        experts(j)
                    aggregate(g, 1)
                    for j in range(3, TG):
                        experts(j)

                groups(pe, layer)

            def summed(n):
                pe.wait_ge(cand_ready, n)

            for n in range(33):
                summed(n + 1)
                nc.tensor.matmul(bank(5)[:, 0:1], ones_f[:], part, start=True, stop=True).then_inc(counted, 1)
            for n, flags in ((33, eq), (34, sel)):
                summed(n + 1)
                nc.tensor.matmul(bank(6)[:, 0:NT], tri[:], flags, start=True, stop=True)
                nc.tensor.matmul(bank(6)[:, 64:64 + NT], ones_f[:], flags, start=True, stop=True).then_inc(counted, 1)

            pe.wait_ge(ffn_in, 96)

            def ffn(g):
                for j in range(CH):
                    pe.wait_ge(g_in[j], 32 * (g + 1))
                    ge(pe, f_tc, CH * g + (j - 1 if j >= 2 else 0))
                    for kc in range(2):
                        last = nc.tensor.transpose(ps_T[:, j % 2, kc * P:(kc + 1) * P], xg[:, j, kc * P:(kc + 1) * P], ident[:])
                    last.then_inc(f_t, 1)
                pe.wait_ge(f_tc, CH * (g + 1))
                for half in range(2):
                    for m in range(8):
                        q = half * 8 + m
                        ge(pe, h_act, 16 * g + q - 1)
                        for kc in range(2):
                            last = nc.tensor.matmul(bank(q % 2)[:, 0:FH], w1_sb[:, kc, m * P:(m + 1) * P],
                                                    x2T[:, kc, half * FH:(half + 1) * FH], start=(kc == 0), stop=(kc == 1))
                        last.then_inc(h_done, 1)
                for j in range(CH):
                    pe.wait_ge(h_act, 16 * g + (8 if j < 2 else 16))
                    ge(pe, y_read, CH * g + (j - 1 if j >= 2 else 0))
                    for m in range(8):
                        last = nc.tensor.matmul(bank(2 + j % 2)[:, 0:D], hT[:, m, j * P:(j + 1) * P], w2_sb[:, m, :],
                                                start=(m == 0), stop=(m == 7))
                    last.then_inc(y_done, 1)

            ffn(0)
            with pe.Fori(1, CH) as g:
                ffn(g)


def kernel(**inputs):
    import numpy as np
    import concourse.bacc as bacc
    from concourse import mybir
    from concourse.bass_utils import run_bass_kernel_spmd

    def arr(name):
        return np.asarray(inputs[name])

    def pieces(w, n):
        return w.reshape(n, P, -1).transpose(1, 0, 2)

    x = np.zeros((NP, D), np.float32)
    x[:N] = arr("x")
    W = arr("L0_gnn_W")
    wqkv = arr("L0_mix_w_qkv")
    envw = arr("L0_gnn_envW")
    laid = {
        "x": x, "src": arr("src"), "dst": arr("dst"),
        "gw": np.stack([pieces(W[l].transpose(1, 0, 2).reshape(2 * D, EXPERTS * D), 4) for l in range(2)]),
        "envw": envw.reshape(2, 2, P, EXPERTS).transpose(2, 0, 1, 3),
        "envb": np.broadcast_to(arr("L0_gnn_envb")[None], (P, 2, EXPERTS)),
        "wkv": pieces(wqkv[512:].T, 2),
        "wq": pieces(wqkv[:512], 4),
        "wo": pieces(arr("L0_mix_w_out").T, 4),
        "bo": np.broadcast_to(arr("L0_mix_b_out")[None], (P, D)),
        "wr": np.broadcast_to(arr("L0_ffn_wr").reshape(1, D), (P, D)),
        "br": np.broadcast_to(arr("L0_ffn_br").reshape(1, 1), (P, 1)),
        "w1": pieces(arr("L0_ffn_w1"), 2),
        "b1": arr("L0_ffn_b1").reshape(8, P).T,
        "w2": pieces(arr("L0_ffn_w2"), 8),
        "b2": np.broadcast_to(arr("L0_ffn_b2")[None], (P, D)),
    }
    nc = bacc.Bacc("TRN2", target_bir_lowering=False, num_devices=1)
    arrays, args = {}, []
    for name, a in laid.items():
        a = np.ascontiguousarray(a)
        arrays[f"in_{name}"] = a
        args.append(nc.dram_tensor(f"in_{name}", a.shape, mybir.dt.from_np(a.dtype), kind="ExternalInput").ap())
    args.append(nc.dram_tensor("out_0", (NP + P, D), mybir.dt.float32, kind="ExternalOutput").ap())
    build(nc, *args)
    r = run_bass_kernel_spmd(nc, [arrays], core_ids=[0])
    return r.results[0]["out_0"][:N]
```

```python
import concourse.bass as bass
from concourse import mybir
from contextlib import ExitStack
import numpy as np

P = 128
N = 6250
D = 256
E = 206250
TG = 7
NT = TG * TG
NP = NT * P
GR = TG * P
HR = GR // 2
EXPERTS = 4
H = 1024
KV = 1024
HEAD = 64
EPS = 1e-5
F = 2048
BITS, ROW_BITS = 18, 11
EP = 125
EC = E // EP
CB = 13
NODE = (1 << CB) - 1
KEY_BASE = 0x40000000
KEY_PAD = 0x44000000
SPARE = 7168
A_ROWS = SPARE + (1 << (BITS - CB))
TURN = F // P
TURNS = E // F
LAST = -(-(E - TURNS * F) // P)
TOPK = N // 2 - 1
CH = 5
CHUNKS = CH * CH
SLOTS = CHUNKS * P
DIGIT = 4
FH = CH * P // 2


def before(j, ring):
    if j >= ring:
        return j - ring + 1
    return max(i for i in range(TG) if i % ring == j % ring) - TG + 1


def ge(eng, sem, value, nop=False):
    if not (isinstance(value, int) and value <= 0):
        eng.wait_ge(sem, value)
        if nop and not isinstance(value, int):
            eng.nop(nofuse=True)


def build(nc, x, src, dst, gw, envw, envb, wkv, wq, wo, bo, wr, br, w1, b1, w2, b2, out):
    f32, i32, f16 = mybir.dt.float32, mybir.dt.int32, mybir.dt.float16
    ALU = mybir.AluOpType
    ACT = mybir.ActivationFunctionType
    AX = mybir.AxisListType.X
    ctx = ExitStack()
    with ctx:
        def sb(name, shape, dt):
            return ctx.enter_context(nc.sbuf_tensor(name, shape, dt))

        def sem(name):
            return ctx.enter_context(nc.semaphore(name))

        def sems(name, n):
            return [sem(f"{name}{i}") for i in range(n)]

        def dram(name, shape, dt):
            return nc.dram_tensor(name, shape, dt).ap()

        class Carver:

            def __init__(self, base):
                self.base, self.at = base, 0

            def __call__(self, n, dt=f32):
                a = self.base[:, self.at:self.at + n]
                self.at += n
                assert self.at <= self.base.shape[1]
                return a if dt == f32 else a.bitcast(dt)

        ZW = NT * D
        zs1 = sb("zs1", [P, NT, 2, D], f16)
        arena = sb("arena", [P, ZW + TG * TG * HR // 2], f32)
        zs2 = arena[:, 0:ZW].bitcast(f16).rearrange("p (t s d) -> p t s d", t=NT, s=2)
        a_ring = arena[:, ZW:].bitcast(f16).rearrange("p (u c r) -> p u c r", u=TG, c=TG)
        addr = sb("addr", [P, F], i32)
        cnt16 = sb("cnt16", [P, F], f16)
        cur_addr = sb("cur_addr", [P, 2, TURN], i32)
        cur_cnt = sb("cur_cnt", [P, 2, TURN], f16)
        gw_sb = sb("gw_sb", [P, 4, EXPERTS * D], f32)
        aggT = sb("aggT", [P, 2, GR], f32)
        zT = sb("zT", [P, TG, D], f32)
        z_in = sb("z_in", [P, TG, D], f32)
        zn = sb("zn", [P, 4, D], f32)
        acc = sb("acc", [P, 2, D], f32)
        inv = sb("inv", [P, GR], f32)
        ident = sb("ident", [P, P], f32)
        ones_f = sb("ones_f", [P, P], f32)
        tri = sb("tri", [P, P], f32)
        ones16 = sb("ones16", [P, P], f16)
        eps = sb("eps", [P, 1], f32)
        envw_sb = sb("envw_sb", [P, 2, 2, EXPERTS], f32)
        envb_sb = sb("envb_sb", [P, 2, EXPERTS], f32)
        lg = sb("lg", [P, TG, EXPERTS], f32)
        wts = sb("wts", [P, TG, EXPERTS], f32)
        red = sb("red", [P, 4, TG], f32)
        wsum = sb("wsum", [P, TG], f32)
        mv = sb("mv", [P, TG, 2], f32)
        stats = sb("stats", [P, TG, 6], f32)
        std = sb("std", [P, TG], f32)
        rstd = sb("rstd", [P, TG], f32)
        wcol = sb("wcol", [P, NT], f32)
        bound = sb("bound", [P, 2 * TG], i32)
        ps = ctx.enter_context(nc.psum_tensor("ps", [P, 8, 512], f32))

        c = Carver(arena)
        keys = [c(F), c(F)]
        src_in, dst_in = c(EC, i32), c(EC, i32)
        pos, spare, same, run, tmp = c(F), c(F, i32), c(F, i32), c(F), c(F, i32)
        qid, qbit, qxor, sgn = c(1, i32), c(9, i32), c(8, i32), c(9)
        edge_next, edge_prev, carry, crow, cexcl = c(1), c(1), c(1), c(P), c(P + 1)
        below = c(2 * TG)
        assert c.at <= ZW + TG * TG * HR // 2
        c = Carver(arena)
        x_in = c(TG * D).rearrange("p (j d) -> p j d", j=TG)
        xn = c(TG * D).rearrange("p (j d) -> p j d", j=TG)
        xnT = c(TG * D).rearrange("p (j d) -> p j d", j=TG)
        sq = c(2 * KV).rearrange("p (s e) -> p s e", s=2)
        k_sb = c(KV).rearrange("p (s e) -> p s e", s=2)
        v_sb = c(KV).rearrange("p (s e) -> p s e", s=2)
        wkv_sb = c(2 * KV).rearrange("p (c e) -> p c e", c=2)
        wmean = c(32).rearrange("p (c h) -> p c h", c=2)
        ss = c(32).rearrange("p (s h) -> p s h", s=2)
        sd = c(32).rearrange("p (s h) -> p s h", s=2)
        rs = c(16)
        rr = c(8)
        wq_sb = c(4 * D).rearrange("p (c e) -> p c e", c=4)
        wo_sb = c(4 * D).rearrange("p (c e) -> p c e", c=4)
        dT = c(4 * P).rearrange("p (c e) -> p c e", c=4)
        g_sb = c(4 * D).rearrange("p (c e) -> p c e", c=4)
        m_sb = c(2 * D).rearrange("p (c e) -> p c e", c=2)
        bo_sb = c(D)
        z1_words = zs1[:].rearrange("p t s d -> p (t s d)").bitcast(f32)
        c = Carver(z1_words)
        xp_in = c(TG * D).rearrange("p (j d) -> p j d", j=TG)
        x1 = c(TG * D).rearrange("p (j d) -> p j d", j=TG)
        xn2 = c(TG * D).rearrange("p (j d) -> p j d", j=TG)
        base = c(TG * D).rearrange("p (j d) -> p j d", j=TG)
        wr_sb, junk = c(D), c(D)
        br_sb = c(1)
        w1_sb = c(2 * H).rearrange("p (c e) -> p c e", c=2)
        c = Carver(arena)
        w2_sb = c(8 * D).rearrange("p (c e) -> p c e", c=8)
        b1_sb, b2_sb = c(8), c(D)
        hT = c(8 * CH * P).rearrange("p (m r) -> p m r", m=8)
        x2T = c(2 * CH * P).rearrange("p (k r) -> p k r", k=2)
        xg = c(CH * D).rearrange("p (j d) -> p j d", j=CH)
        bg = c(CH * D).rearrange("p (j d) -> p j d", j=CH)
        yo = c(CH * D).rearrange("p (j d) -> p j d", j=CH)
        yt = c(2 * D).rearrange("p (j d) -> p j d", j=2)
        fj, fw = c(D), c(CH)
        CN = (1 << DIGIT) - 1
        u_t, digit, thr_i = c(1, i32), c(1, i32), c(1, i32)
        ladder, cand, t1 = c(CN, i32), c(CN, i32), c(CN, i32)
        hits, part, met = c(CN * NT), c(CN), c(CN)
        digit_f = c(1)
        gt, eq, cum, tot, scan, sel = c(NT), c(NT), c(NT), c(NT), c(NT), c(NT)
        ntot = c(1)
        slot_i, slot_p, slot_c = c(NT, i32), c(NT, i32), c(NT, i32)
        nid, at_p, at_c = c(NT), c(NT), c(NT)
        places, chunks = c(P), c(CHUNKS)
        pads = c(CHUNKS)
        is_p = c(TG * P).rearrange("p (t r) -> p t r", t=TG), c(TG * P).rearrange("p (t r) -> p t r", t=TG)
        is_c = c(NT * CHUNKS).rearrange("p (t r) -> p t r", t=NT)
        idx = c(CHUNKS, i32)
        cur_g, cur_s = c(CH, i32), c(CH, i32)

        A = dram("A", [A_ROWS << CB, 1], f16)
        A_tiles = A[0:NP << CB, :].rearrange("(ct p r) o -> p ct (r o)", p=P, r=NODE + 1)
        zero_rows = zs1[:].rearrange("p t s d -> p (t s d)")[:, 0:NP]
        zd = [dram("zd0", [NP, D], f32), dram("zd1", [NP, D], f32)]
        xTd = dram("xTd", [P, NT, D], f32)
        xpd = dram("xpd", [NP, D], f32)
        invd = dram("invd", [1, NP], f32)
        xn2d = dram("xn2d", [NP + P, D], f32)
        d_last, d_carry = dram("d_last", [P, 1], f32), dram("d_carry", [P, 1], f32)

        def rows(t):
            return t.rearrange("(n p) d -> p n d", p=P)

        consts = sem("consts")
        order_in = sem("order_in")
        edges_in, step = sem("edges_in"), sem("step")
        order_out, tposed, half_copied = sem("order_out"), sem("tposed"), sem("half_copied")
        sorted_s, carry_s, lists_ready = sem("sorted_s"), sem("carry_s"), sem("lists_ready")
        zero_made, a_zeroed = sem("zero_made"), sem("a_zeroed")
        scat, landed = sems("scat", 3), sem("landed")
        small_in, wmix_in, gw_in, ffn_in = sem("small_in"), sem("wmix_in"), sem("gw_in"), sem("ffn_in")
        below_ready, below_summed, bound_ready = sem("below_ready"), sem("below_summed"), sem("bound_ready")
        early_free = sem("early_free")
        x_ld, xn_st, xT_st = sems("x_ld", TG), sems("xn_st", TG), sems("xT_st", TG)
        var_ready, std_ready = sem("var_ready"), sem("std_ready")
        xn_done, hi_done, xT_done, xT_copied = sem("xn_done"), sem("hi_done"), sem("xT_done"), sem("xT_copied")
        wkv_ready, kv_done, sq_done, ss_done, sd_done = sem("wkv_ready"), sem("kv_done"), sem("sq_done"), sem("ss_done"), sem("sd_done")
        v_done, dots_done, dT_done, lo_done = sem("v_done"), sem("dots_done"), sem("dT_done"), sem("lo_done")
        gm_done, gm_copied = sem("gm_done"), sem("gm_copied")
        mix_done, xp_ready, xp_st = sem("mix_done"), sem("xp_ready"), sems("xp_st", TG)
        a_in, a_used, agg_evac = sems("a_in", TG), sem("a_used"), sem("agg_evac")
        z_ld, t_done, t_copied = sems("z_ld", TG), sem("t_done"), sem("t_copied")
        logit_done, lg_read, lg_sub, lg_exp, wts_ready = sem("logit_done"), sem("lg_read"), sem("lg_sub"), sem("lg_exp"), sem("wts_ready")
        w_done, acc_init, acc_done = sem("w_done"), sem("acc_init"), sem("acc_done")
        zn_ready, hi2_done, lo2_done, zn_st = sem("zn_ready"), sem("hi2_done"), sem("lo2_done"), sems("zn_st", 4)
        inv_st, inv_ld, xp_ld = sem("inv_st"), sem("inv_ld"), sems("xp_ld", TG)
        x1_done, var2_ready, std2_ready, end_ready = sem("x1_done"), sem("var2_ready"), sem("std2_ready"), sem("end_ready")
        end_st = sems("end_st", TG)
        list_consts, is_p_ready, is_p_used, idx_ready, fj_done = sem("list_consts"), sem("is_p_ready"), sem("is_p_used"), sem("idx_ready"), sem("fj_done")
        wcol_ready, wcol_cut, cand_ready, counted = sem("wcol_ready"), sem("wcol_cut"), sem("cand_ready"), sem("counted")
        idx_cp = sem("idx_cp")
        xg_in, bg_in, y_st = sems("xg_in", CH), sems("bg_in", CH), sems("y_st", CH)
        f_t, f_tc, h_done, h_act, y_done, y_read, yo_ready = (
            sem("f_t"), sem("f_tc"), sem("h_done"), sem("h_act"), sem("y_done"), sem("y_read"), sem("yo_ready"))

        NSTEP = [0]
        T_ORDER = [(4, 5), (6,), (0, 1), (2, 3)]
        TB = len(T_ORDER)

        def bank(b, n=1):
            return ps[:, b:b + n, :].rearrange("p b c -> p (b c)")

        ps_sort = bank(0, 4)
        ps_kv = [bank(0, 2), bank(2, 2)]
        ps_T = ps[:, 4:6, 0:D]
        ps_dots = bank(6)
        ps_agg = [[bank(0), bank(1)], [bank(2), bank(3)]]
        ps_out = [bank(4, 2), bank(6, 2)]
        ps_cnt = [bank(2), bank(0)]
        ps_zT = bank(4, 4)
        ps_lg = bank(7)[:, 256:256 + TG * EXPERTS].rearrange("p (j k) -> p j k", j=TG)

        block = ctx.enter_context(nc.Block())

        def groups(eng, body, last_apart=False):
            body(0)
            with eng.Fori(1, TG - 1 if last_apart else TG) as g:
                body(g)
            if last_apart:
                body(TG - 1)

        @block.sync
        def _(sp):
            sp.dma_start(src_in[0:EP, :], src.rearrange("(p t) -> p t", p=EP)).then_inc(edges_in, 16)
            sp.dma_start(dst_in[0:EP, :], dst.rearrange("(p t) -> p t", p=EP)).then_inc(edges_in, 16)
            sp.dma_start(envw_sb[:], envw).then_inc(small_in, 16)
            sp.dma_start(envb_sb[:], envb).then_inc(small_in, 16)
            sp.dma_start(gw_sb[:], gw[0]).then_inc(gw_in, 16)
            sp.wait_ge(sorted_s, 1)
            sp.dma_start(edge_next[0:P - 1, :], keys[0][1:P, 0:1]).then_inc(carry_s, 16)
            sp.dma_start(edge_prev[1:P, :], keys[0][0:P - 1, F - 1:F]).then_inc(carry_s, 16)
            sp.wait_ge(sorted_s, 2)
            sp.dma_start(d_last[:, :], keys[1][:, F - 1:F]).then_inc(carry_s, 16)
            sp.wait_ge(carry_s, 48)
            sp.dma_start(crow[0:1, 0:P], d_last.rearrange("p o -> o p")).then_inc(carry_s, 16)
            sp.wait_ge(sorted_s, 3)
            sp.dma_start(d_carry.rearrange("p o -> o p"), cexcl[0:1, 0:P]).then_inc(carry_s, 16)
            sp.wait_ge(carry_s, 80)
            sp.dma_start(carry[:, :], d_carry[:, :]).then_inc(carry_s, 16)

            sp.wait_ge(early_free, 1)
            sp.dma_start(wkv_sb, wkv).then_inc(wmix_in, 16)
            sp.dma_start(wq_sb, wq).then_inc(wmix_in, 16)
            sp.dma_start(wo_sb, wo).then_inc(wmix_in, 16)
            sp.dma_start(bo_sb, bo).then_inc(wmix_in, 16)

            def loads(g):
                for j in range(TG):
                    ge(sp, xn_done, g * TG - TG + j + 1, nop=True)
                    sp.dma_start(x_in[:, j, :], rows(x)[:, g * TG + j, :]).then_inc(x_ld[j], 16)

            def stores(g):
                for j in range(TG):
                    ge(sp, xn_done, g * TG + j + 1, nop=True)
                    sp.dma_start(rows(zd[0])[:, g * TG + j, :], xn[:, j, :]).then_inc(xn_st[j], 16)
                    ge(sp, xT_copied, g * TG + j + 1, nop=True)
                    sp.dma_start(xTd[:, g * TG + j, :], xnT[:, j, :]).then_inc(xT_st[j], 16)

            loads(0)
            loads(1)
            stores(0)
            with sp.Fori(1, TG - 1) as g:
                loads(g + 1)
                stores(g)
            stores(TG - 1)
            for j in range(TG):
                sp.wait_ge(xn_st[j], 16 * TG)
                sp.wait_ge(xT_st[j], 16 * TG)

            def mix_loads(g):
                for j in range(TG):
                    ge(sp, xp_ready, g * TG - TG + j + 1, nop=True)
                    if isinstance(g, int) and g == 0:
                        sp.wait_ge(kv_done, NT)
                    sp.dma_start(x_in[:, j, :], rows(x)[:, g * TG + j, :]).then_inc(x_ld[j], 16)
                    sp.dma_start(xnT[:, j, :], xTd[:, g * TG + j, :]).then_inc(x_ld[j], 16)

            def mix_stores(g):
                for j in range(TG):
                    ge(sp, xp_ready, g * TG + j + 1, nop=True)
                    sp.dma_start(rows(xpd)[:, g * TG + j, :], xn[:, j, :]).then_inc(xp_st[j], 16)

            mix_loads(0)
            mix_loads(1)
            mix_stores(0)
            with sp.Fori(1, TG - 1) as g:
                mix_loads(g + 1)
                mix_stores(g)
            mix_stores(TG - 1)
            for j in range(TG):
                sp.wait_ge(xp_st[j], 16 * TG)

            sp.wait_ge(bound_ready, 1)
            for l in range(2):
                def tiles_of_a(g, b, us=range(TG)):
                    if l == 0 and 0 in us:
                        sp.wait_ge(landed, sp.value_load(bound[0:1, bass.ds(2 * g + b, 1)], min_val=1, max_val=TURNS + 1))
                        sp.nop(nofuse=True)
                    for u in us:
                        ge(sp, a_used, TG * (2 * (TG * l + g) + b - 1) + u + 1, nop=True)
                        sp.dma_start(a_ring[:, u, :, :],
                                     A_tiles[:, u * TG:(u + 1) * TG, bass.ds(g * GR + b * HR, HR)]).then_inc(a_in[u], 16)

                def ends(g):
                    for j in range(TG):
                        ge(sp, end_ready, g * TG + j + 1, nop=True)
                        sp.dma_start(rows(xn2d[0:NP, :])[:, g * TG + j, :], xn2[:, j, :]).then_inc(end_st[j], 16)
                        sp.dma_start(rows(out[0:NP, :])[:, g * TG + j, :], base[:, j, :]).then_inc(end_st[j], 16)

                def z_loads(g, js):
                    for j in js:
                        ge(sp, acc_init, NT * l + g * TG - TG + j + 1, nop=True)
                        sp.dma_start(z_in[:, j, :], rows(zd[l])[:, g * TG + j, :]).then_inc(z_ld[j], 16)

                def layer(g):
                    first = isinstance(g, int) and g == 0
                    if l == 1 and first:
                        tiles_of_a(g, 0)
                        sp.wait_ge(w_done, NT)
                        sp.dma_start(gw_sb[:], gw[1]).then_inc(gw_in, 16)
                        for s in range(4):
                            sp.wait_ge(zn_st[s], 16 * TG * (2 if s < 3 else 1))
                        z_loads(g, range(TG))
                        sp.wait_ge(inv_st, 16 * TG)
                    else:
                        z_loads(g, range(0, 5))
                        tiles_of_a(g, 0, range(0, 4))
                        z_loads(g, range(5, TG))
                        tiles_of_a(g, 0, range(4, TG))
                    if l == 1:
                        ge(sp, agg_evac, 4 * (TG + g), nop=True)
                        sp.dma_start(inv[:], invd[0:1, bass.ds(g * GR, GR)].to_broadcast([P, GR])).then_inc(inv_ld, 16)
                        if first:
                            sp.wait_ge(a_used, 2 * TG * TG)
                            sp.dma_start(wr_sb, wr).then_inc(ffn_in, 16)
                            sp.dma_start(br_sb, br).then_inc(ffn_in, 16)
                            sp.dma_start(w1_sb, w1).then_inc(ffn_in, 16)
                        for j in range(TG):
                            ge(sp, x1_done, g * TG - TG + j + 1, nop=True)
                            sp.dma_start(xp_in[:, j, :], rows(xpd)[:, g * TG + j, :]).then_inc(xp_ld[j], 16)
                        if not first:
                            ends(g - 1)
                    tiles_of_a(g, 1)

                groups(sp, layer)
                if l == 1:
                    ends(TG - 1)
            sp.wait_ge(a_used, 4 * TG * TG)
            sp.wait_ge(w_done, 2 * NT)
            sp.dma_start(w2_sb, w2).then_inc(ffn_in, 16)
            sp.dma_start(b1_sb, b1).then_inc(ffn_in, 16)
            sp.dma_start(b2_sb, b2).then_inc(ffn_in, 16)

        @block.gpsimd
        def _(pool):
            nc.gpsimd.memset(ones_f[:], 1.0).then_inc(order_in, 1)
            pool.wait_ge(order_in, 1)
            nc.gpsimd.affine_select(out=ident[:], in_=ones_f[:], compare_op=ALU.is_equal, fill=0.0, base=0,
                                    pattern=[[-1, P]], channel_multiplier=1).then_inc(consts, 1)
            nc.gpsimd.iota(qid, pattern=[[0, 1]], base=0, channel_multiplier=1).then_inc(consts, 1)
            nc.gpsimd.iota(pos, pattern=[[1, F]], base=0, channel_multiplier=F,
                           allow_small_or_imprecise_dtypes=True).then_inc(consts, 1)
            nc.gpsimd.iota(same, pattern=[[1, F]], base=0, channel_multiplier=F).then_inc(consts, 1)
            nc.gpsimd.affine_select(out=tri[:], in_=ones_f[:], compare_op=ALU.is_ge, fill=0.0, base=0,
                                    pattern=[[1, P]], channel_multiplier=-1).then_inc(consts, 1)

            pool.wait_ge(a_zeroed, 16 * (NT + 2))
            pool.wait_ge(lists_ready, 2)
            by_turn = addr[:].rearrange("p (m q) -> p q m", q=P)
            by_turn_cnt = cnt16[:].rearrange("p (m q) -> p q m", q=P)
            cp = [0]

            def turn(i, s, n=TURN, sem_=None, q=None):
                q = 2 * i + s if q is None else q
                nc.gpsimd.tensor_copy(cur_addr[:, s, 0:n], by_turn[:, q, 0:n]).then_inc(idx_cp, 1)
                nc.gpsimd.tensor_copy(cur_cnt[:, s, 0:n], by_turn_cnt[:, q, 0:n]).then_inc(idx_cp, 1)
                ge(pool, idx_cp, 2 * q + 2, nop=True)
                for m in range(n):
                    nc.gpsimd.indirect_dma_start(A, bass.IndirectOffsetOnAxis(ap=cur_addr[:, s, m:m + 1], axis=0),
                                                 cur_cnt[:, s, m:m + 1], None).then_inc(scat[s] if sem_ is None else sem_, 16)

            def pair(i):
                for s in (0, 1):
                    if not (isinstance(i, int) and i == 0):
                        ge(pool, scat[s], 16 * TURN * i, nop=True)
                        pool.sem_inc(landed, 1)
                    turn(i, s)

            pair(0)
            with pool.Fori(1, TURNS // 2) as i:
                pair(i)
            pool.wait_ge(scat[0], 16 * TURN * (TURNS // 2))
            pool.sem_inc(landed, 1)
            turn(0, 0, LAST, scat[2], TURNS)
            pool.wait_ge(scat[1], 16 * TURN * (TURNS // 2))
            pool.sem_inc(landed, 1)
            pool.wait_ge(scat[2], 16 * LAST)
            pool.sem_inc(landed, 1)

            pool.wait_ge(w_done, 2 * NT)
            nc.gpsimd.iota(nid, pattern=[[P, NT]], base=0, channel_multiplier=1,
                           allow_small_or_imprecise_dtypes=True).then_inc(list_consts, 1)
            nc.gpsimd.iota(places, pattern=[[1, P]], base=0, channel_multiplier=0,
                           allow_small_or_imprecise_dtypes=True).then_inc(list_consts, 1)
            nc.gpsimd.iota(chunks, pattern=[[1, CHUNKS]], base=0, channel_multiplier=0,
                           allow_small_or_imprecise_dtypes=True).then_inc(list_consts, 1)
            nc.gpsimd.iota(ladder, pattern=[[1, CN]], base=1, channel_multiplier=0).then_inc(list_consts, 1)
            nc.gpsimd.iota(pads, pattern=[[P, CHUNKS]], base=NP - TOPK, channel_multiplier=1,
                           allow_small_or_imprecise_dtypes=True).then_inc(list_consts, 1)
            pool.wait_ge(list_consts, 5)
            nc.gpsimd.affine_select(out=pads, in_=pads, compare_op=ALU.is_ge, fill=0.0, base=-TOPK,
                                    pattern=[[P, CHUNKS]], channel_multiplier=1).then_inc(list_consts, 1)
            pool.wait_ge(wcol_ready, 1)
            nc.gpsimd.affine_select(out=wcol[:, NT - 1:NT], in_=wcol[:, NT - 1:NT], compare_op=ALU.is_ge,
                                    fill=-3.0e38, base=N - 1 - (NT - 1) * P, pattern=[[0, 1]],
                                    channel_multiplier=-1).then_inc(wcol_cut, 1)
            for j in range(TG):
                pool.wait_ge(end_st[j], 32 * TG)
            pool.wait_ge(idx_ready, 1)

            CP0 = 2 * TURNS + 2

            def gather(i, rows_, into, j, arrived):
                nc.gpsimd.indirect_dma_start(into[:, j, :], None, rows_,
                                             bass.IndirectOffsetOnAxis(ap=i[:, j:j + 1], axis=0)).then_inc(arrived[j], 16)

            def features(g):
                ge(pool, f_t, CH * g, nop=True)
                ge(pool, fj_done, g, nop=True)
                for j in range(CH):
                    ge(pool, xg_in[j], 16 * g, nop=True)
                    ge(pool, bg_in[j], 16 * g, nop=True)
                nc.gpsimd.tensor_copy(cur_g, idx[:, bass.ds(g * CH, CH)]).then_inc(idx_cp, 1)
                ge(pool, idx_cp, CP0 + (1 if isinstance(g, int) and g == 0 else 2 * g), nop=True)
                for j in range(CH):
                    gather(cur_g, xn2d, xg, j, xg_in)

            def results(g, more=True):
                if not (isinstance(g, int) and g == 0):
                    for j in range(CH):
                        ge(pool, y_st[j], 16 * g, nop=True)
                nc.gpsimd.tensor_copy(cur_s, idx[:, bass.ds(g * CH, CH)]).then_inc(idx_cp, 1)
                ge(pool, idx_cp, CP0 + 2 * g + (3 if more else 2), nop=True)
                for j in range(CH):
                    ge(pool, yo_ready, CH * g + j + 1, nop=True)
                    nc.gpsimd.indirect_dma_start(out, bass.IndirectOffsetOnAxis(ap=cur_s[:, j:j + 1], axis=0),
                                                 yo[:, j, :], None).then_inc(y_st[j], 16)
                    if more:
                        gather(cur_g, out, bg, j, bg_in)

            features(0)
            for j in range(CH):
                gather(cur_g, out, bg, j, bg_in)
            features(1)
            results(0)
            with pool.Fori(1, CH - 1) as g:
                features(g + 1)
                results(g)
            results(CH - 1, False)
            for j in range(CH):
                pool.wait_ge(y_st[j], 16 * CH)

        @block.scalar
        def _(act):
            act.wait_ge(zero_made, 1)
            with act.Fori(0, NT) as t:
                act.dma_start(A_tiles[:, t, 0:NP], zero_rows).then_inc(a_zeroed, 16)
            for rows_ in (xn2d, out):
                act.dma_start(rows_[NP:NP + P, :], zero_rows.bitcast(f32)[:, 0:D]).then_inc(a_zeroed, 16)
            a = sum(range(1, ROW_BITS + 1)) % 2
            c = 0
            for k in range(ROW_BITS + 1, BITS + 1):
                for stages in (k - ROW_BITS, ROW_BITS):
                    c += 1
                    act.wait_ge(tposed, 2 * c - 1)
                    nc.scalar.copy(keys[1 - a][:, 0:F // 2], ps_sort[:, 0:F // 2]).then_inc(half_copied, 1)
                    a = (a + 1 + stages) % 2
            act.wait_ge(a_zeroed, 16 * (NT + 2))

            def deviations(g):
                act.wait_ge(var_ready, g + 1)
                nc.scalar.activation(std[:], mv[:, :, 1], ACT.Sqrt, bias=eps[:]).then_inc(std_ready, 1)

            def first(g, more=True):
                for s in range(TG + 2):
                    if s == 5 and more:
                        deviations(g + 1)
                    if s < TG:
                        n = g * TG + s
                        act.wait_ge(xn_done, n + 1)
                        nc.scalar.copy(zs1[:, n, 0, :], xn[:, s, :]).then_inc(hi_done, 1)
                        act.wait_ge(xT_done, n + 1)
                        ge(act, kv_done, n + 1 - TG)
                        ge(act, xT_st[s], 16 * g)
                        nc.scalar.copy(xnT[:, s, :], ps_T[:, s % 2, :]).then_inc(xT_copied, 1)
                    if 1 <= s <= TG:
                        j = s - 1
                        n = g * TG + j
                        act.wait_ge(kv_done, n + 1)
                        ge(act, ss_done, g * TG + before(j, 2))
                        nc.scalar.activation(sq[:, j % 2, :], ps_kv[j % 2], ACT.Square).then_inc(sq_done, 1)
                        ge(act, dots_done, g * TG + before(j, 2))
                        nc.scalar.copy(k_sb[:, j % 2, :], ps_kv[j % 2][:, 0:512])
                    if s >= 2:
                        j = s - 2
                        n = g * TG + j
                        act.wait_ge(ss_done, n + 1)
                        ge(act, v_done, g * TG + before(j, 2))
                        nc.scalar.activation(sd[:, j % 2, :], ss[:, j % 2, :], ACT.Sqrt, bias=eps[:],
                                             scale=1.0 / HEAD).then_inc(sd_done, 1)

            deviations(0)
            first(0)
            with act.Fori(1, TG - 1) as g:
                first(g)
            first(TG - 1, False)
            act.wait_ge(gm_done, 1)
            nc.scalar.copy(g_sb.rearrange("p c e -> p (c e)"), ps_kv[0]).then_inc(gm_copied, 1)
            act.wait_ge(gm_done, 2)
            nc.scalar.copy(m_sb.rearrange("p c e -> p (c e)"), ps_kv[1][:, 0:512]).then_inc(gm_copied, 1)

            for l in range(2):
                def layer(g):
                    G = g + TG * l
                    for i, js in enumerate(T_ORDER):
                        act.wait_ge(t_done, G * TB + i + 1)
                        nc.scalar.copy(zT[:, js[0]:js[-1] + 1, :].rearrange("p j d -> p (j d)"),
                                       ps_zT[:, js[0] * D:(js[-1] + 1) * D]).then_inc(t_copied, 1)
                    act.wait_ge(lg_sub, G + 1)
                    nc.scalar.activation(lg[:], lg[:], ACT.Exp).then_inc(lg_exp, 1)
                    for s in range(TG + 1):
                        if l == 0 and s == 5:
                            act.wait_ge(agg_evac, 4 * G + 4)
                            act.dma_start(invd[0:1, bass.ds(g * GR, GR)], inv[0:1, :]).then_inc(inv_st, 16)
                        if s < TG:
                            n = G * TG + s
                            act.wait_ge(wts_ready, G + 1)
                            act.wait_ge(z_ld[s], 16 * (G + 1))
                            if l == 1:
                                ge(act, x1_done, g * TG + before(s, 2))
                            else:
                                ge(act, hi2_done, g * TG + before(s, 2))
                            nc.scalar.activation(acc[:, s % 2, :], z_in[:, s, :], ACT.Copy,
                                                 scale=wsum[:, s:s + 1]).then_inc(acc_init, 1)
                        if s >= 1 and l == 0:
                            j = s - 1
                            n = G * TG + j
                            act.wait_ge(acc_done, n + 1)
                            ge(act, zn_st[j % 4], 16 * ((2 if j % 4 < 3 else 1) * g + j // 4))
                            ge(act, lo2_done, g * TG + before(j, 4))
                            nc.scalar.activation(zn[:, j % 4, :], acc[:, j % 2, :], ACT.Relu).then_inc(zn_ready, 1)
                            nc.scalar.activation(zs2[:, n, 0, :], acc[:, j % 2, :], ACT.Relu).then_inc(hi2_done, 1)
                            act.wait_ge(zn_ready, n + 1)
                            act.dma_start(rows(zd[1])[:, n, :], zn[:, j % 4, :]).then_inc(zn_st[j % 4], 16)
                    if l == 1:
                        act.wait_ge(var2_ready, g + 1)
                        nc.scalar.activation(std[:], mv[:, :, 1], ACT.Sqrt, bias=eps[:]).then_inc(std2_ready, 1)

                groups(act, layer)

            def x2_copies(g):
                for j in range(CH):
                    act.wait_ge(f_t, CH * g + j + 1)
                    ge(act, h_done, 16 * g)
                    nc.scalar.copy(x2T[:, :, j * P:(j + 1) * P],
                                   ps_T[:, j % 2, :].rearrange("p (k r) -> p k r", k=2)).then_inc(f_tc, 1)

            def ffn(g, more=True):
                for half in range(2):
                    for m in range(8):
                        q = half * 8 + m
                        act.wait_ge(h_done, 16 * g + q + 1)
                        if q == 0:
                            ge(act, y_done, CH * g)
                        nc.scalar.activation(hT[:, m, half * FH:(half + 1) * FH], bank(q % 2)[:, 0:FH],
                                             ACT.Gelu_apprx_tanh, bias=b1_sb[:, m:m + 1]).then_inc(h_act, 1)
                if more:
                    x2_copies(g + 1)

            act.wait_ge(ffn_in, 96)
            x2_copies(0)
            ffn(0)
            with act.Fori(1, CH - 1) as g:
                ffn(g)
            ffn(CH - 1, False)

        @block.vector
        def _(dve):
            base_n, k_n = [0], [0]

            def link(ins):
                k_n[0] += 1
                ins.then_inc(step, 1)
                dve.wait_ge(step, base_n[0] + k_n[0])

            def linked(body, count=TG, last_apart=False):
                start = base_n[0] + k_n[0]
                base_n[0], k_n[0] = start, 0
                body(0)
                per = k_n[0]
                looped = count - 1 if last_apart else count
                with dve.Fori(1, looped) as g:
                    base_n[0], k_n[0] = start + g * per, 0
                    body(g)
                    assert k_n[0] == per
                base_n[0], k_n[0] = start + looped * per, 0
                if last_apart:
                    body(count - 1, False)

            I = lambda ap: ap.bitcast(i32)
            nc.vector.memset(zero_rows.bitcast(f32), 0.0).then_inc(zero_made, 1)
            link(nc.vector.memset(I(keys[0]), KEY_PAD))
            link(nc.vector.memset(ones16[:], 1.0))
            link(nc.vector.memset(eps[:], EPS))
            dve.wait_ge(edges_in, 32)
            link(nc.vector.tensor_scalar(src_in[0:EP, :], src_in[0:EP, :], CB, KEY_BASE, ALU.logical_shift_left, ALU.bitwise_or))
            link(nc.vector.tensor_tensor(I(keys[0][0:EP, 0:EC]), dst_in[0:EP, :], src_in[0:EP, :], ALU.bitwise_or))
            dve.wait_ge(consts, 5)
            link(nc.vector.memset(qbit, 0))
            for b in range(7):
                link(nc.vector.tensor_scalar(qbit[:, b + 1:b + 2], qid, b, 1, ALU.logical_shift_right, ALU.bitwise_and))
            link(nc.vector.tensor_tensor(qxor, qbit[:, 0:8], qbit[:, 1:9], ALU.bitwise_xor))
            link(nc.vector.tensor_scalar(sgn[:, 0:8], qxor, -2.0, 1.0, ALU.mult, ALU.add))
            link(nc.vector.tensor_scalar(sgn[:, 8:9], sgn[:, 0:1], -1.0, None, ALU.mult))
            link(nc.vector.tensor_scalar(tmp, same, NODE, CB, ALU.bitwise_and, ALU.logical_shift_left))
            link(nc.vector.tensor_scalar(spare, same, CB, KEY_BASE | SPARE, ALU.logical_shift_right, ALU.bitwise_or))
            link(nc.vector.tensor_tensor(spare, spare, tmp, ALU.bitwise_or))

            a = [0]

            def exchange(d):
                s = keys[a[0]].rearrange("p (n two d) -> p n two d", two=2, d=d)
                t = keys[1 - a[0]].rearrange("p (n two d) -> p n two d", two=2, d=d)
                nc.vector.tensor_tensor(t[:, :, 0, :], s[:, :, 0, :], s[:, :, 1, :], ALU.min).then_inc(step, 1)
                k_n[0] += 1
                link(nc.vector.tensor_tensor(t[:, :, 1, :], s[:, :, 0, :], s[:, :, 1, :], ALU.max))
                a[0] = 1 - a[0]

            v = keys[0].rearrange("p (n four) -> p n four", four=4)
            link(nc.vector.tensor_scalar(v[:, :, 2:4], v[:, :, 2:4], -1.0, None, ALU.mult))
            turned = 0
            for k in range(1, BITS + 1):
                if k > ROW_BITS:
                    for half in (0, 1):
                        turned += 1
                        nc.vector.sem_inc(order_out, 1)
                        dve.wait_ge(tposed, 2 * turned)
                        link(nc.vector.tensor_copy(keys[1 - a[0]][:, F // 2:F], ps_sort[:, F // 2:F]))
                        dve.wait_ge(half_copied, turned)
                        a[0] = 1 - a[0]
                        if half == 0:
                            for b in range(k - ROW_BITS - 1, -1, -1):
                                exchange(1 << b)
                for b in range(min(k, ROW_BITS) - 1, -1, -1):
                    exchange(1 << b)
                K = keys[a[0]]
                if k < ROW_BITS - 1:
                    v = K.rearrange("p (n q) -> p n q", q=1 << (k + 2))[:, :, (1 << k):(3 << k)]
                    link(nc.vector.tensor_scalar(v, v, -1.0, None, ALU.mult))
                elif k == ROW_BITS - 1:
                    h = F // 2
                    nc.vector.tensor_scalar(K[:, 0:h], K[:, 0:h], sgn[:, 0:1], None, ALU.mult).then_inc(step, 1)
                    k_n[0] += 1
                    link(nc.vector.tensor_scalar(K[:, h:F], K[:, h:F], sgn[:, 8:9], None, ALU.mult))
                elif k < BITS:
                    b = k - ROW_BITS + 1
                    link(nc.vector.tensor_scalar(K, K, sgn[:, b:b + 1], None, ALU.mult))
            if a[0] == 1:
                link(nc.vector.tensor_copy(keys[0], keys[1]))
            K = keys[0]

            link(nc.vector.memset(edge_next, 0.0))
            link(nc.vector.memset(edge_prev, 0.0))
            link(nc.vector.memset(cexcl, 0.0))
            nc.vector.sem_inc(sorted_s, 1)
            link(nc.vector.tensor_tensor(same[:, 0:F - 1], K[:, 0:F - 1], K[:, 1:F], ALU.is_equal))
            link(nc.vector.tensor_tensor(run[:, 1:F], K[:, 0:F - 1], K[:, 1:F], ALU.not_equal))
            dve.wait_ge(carry_s, 32)
            link(nc.vector.tensor_tensor(same[:, F - 1:F], K[:, F - 1:F], edge_next, ALU.is_equal))
            link(nc.vector.tensor_tensor(run[:, 0:1], K[:, 0:1], edge_prev, ALU.not_equal))
            link(nc.vector.tensor_tensor(run, run, pos, ALU.mult))
            link(nc.vector.tensor_tensor_scan(keys[1], run, run, 0.0, ALU.max, ALU.max))
            nc.vector.sem_inc(sorted_s, 1)
            link(nc.vector.copy_predicated(I(K), same, spare))
            dve.wait_ge(carry_s, 64)
            link(nc.vector.tensor_tensor_scan(cexcl[0:1, 1:P + 1], crow[0:1, 0:P], crow[0:1, 0:P], 0.0, ALU.max, ALU.max))
            nc.vector.sem_inc(sorted_s, 1)
            nc.vector.sem_inc(order_out, 1)
            dve.wait_ge(carry_s, 96)
            link(nc.vector.scalar_tensor_tensor(keys[1], keys[1], carry, pos, ALU.max, ALU.subtract))
            link(nc.vector.tensor_scalar(keys[1], keys[1], -1.0, 1.0, ALU.mult, ALU.add))
            dve.wait_ge(tposed, 2 * turned + 2)
            link(nc.vector.tensor_copy(run, ps_sort))
            nc.vector.sem_inc(order_out, 1)
            link(nc.vector.tensor_scalar(tmp, I(run), NODE, CB, ALU.bitwise_and, ALU.logical_shift_left))
            link(nc.vector.tensor_scalar(same, I(run), CB, NODE, ALU.logical_shift_right, ALU.bitwise_and))
            nc.vector.tensor_tensor(addr[:], tmp, same, ALU.bitwise_or).then_inc(lists_ready, 1)
            dve.wait_ge(tposed, 2 * turned + 4)
            nc.vector.tensor_copy(cnt16[:], ps_sort).then_inc(lists_ready, 1)
            dve.wait_ge(lists_ready, 2)
            for i in range(2 * TG):
                limit = float(np.array(KEY_BASE + ((i + 1) * HR << CB), np.int32).view(np.float32))
                link(nc.vector.tensor_scalar(run[0:EP, 0:EC], src_in[0:EP, :].bitcast(f32), limit, None, ALU.is_lt, ALU.add,
                                             accum_out=below[0:EP, i:i + 1]))
            nc.vector.sem_inc(below_ready, 1)
            dve.wait_ge(below_summed, 1)
            link(nc.vector.tensor_copy(bound[:], bank(0)[:, 0:2 * TG]))
            link(nc.vector.tensor_scalar(bound[:], bound[:], ROW_BITS, None, ALU.logical_shift_right))
            nc.vector.tensor_scalar(bound[:], bound[:], 1, None, ALU.add).then_inc(bound_ready, 1)
            nc.vector.sem_inc(early_free, 1)

            dve.wait_ge(wmix_in, 64)
            heads = wkv_sb.rearrange("p c (h e) -> p c h e", e=HEAD)
            link(nc.vector.reduce_sum(wmean, heads, AX))
            link(nc.vector.tensor_scalar(wmean, wmean, 1.0 / HEAD, None, ALU.mult))
            for kc in range(2):
                link(nc.vector.tensor_tensor(heads[:, kc], heads[:, kc],
                                             wmean[:, kc, :].unsqueeze(2).to_broadcast([P, 16, HEAD]), ALU.subtract))
            nc.vector.memset(dT, 0.0).then_inc(wkv_ready, 1)

            def statistics(g):
                for j in range(TG):
                    dve.wait_ge(x_ld[j], 16 * (g + 1))
                    ins = nc.vector.bn_stats(stats[:, j, :], x_in[:, j, :])
                    if j < TG - 1:
                        ins.then_inc(step, 1)
                        k_n[0] += 1
                link(ins)
                nc.vector.nop(nofuse=True)
                for j in range(TG):
                    ins = nc.vector.bn_aggr(mv[:, j, :], stats[:, j, :])
                ins.then_inc(var_ready, 1)

            def normalise(g):
                dve.wait_ge(std_ready, g + 1)
                link(nc.vector.reciprocal(rstd[:], std[:]))
                for j in range(TG):
                    n = g * TG + j
                    ge(dve, hi_done, n + 1 - TG)
                    ge(dve, xT_done, n + 1 - TG)
                    ge(dve, lo_done, n + 1 - TG)
                    ge(dve, xn_st[j], 16 * g)
                    nc.vector.tensor_scalar(xn[:, j, :], x_in[:, j, :], mv[:, j, 0:1], rstd[:, j:j + 1],
                                            ALU.subtract, ALU.mult).then_inc(xn_done, 1)

            def first(g, more=True):
                for s in range(TG + 1):
                    if s == 4 and more:
                        statistics(g + 1)
                    if s < TG:
                        n = g * TG + s
                        dve.wait_ge(hi_done, n + 1)
                        nc.vector.tensor_tensor(zs1[:, n, 1, :], xn[:, s, :], zs1[:, n, 0, :], ALU.subtract).then_inc(lo_done, 1)
                        if s == TG - 1 and more:
                            normalise(g + 1)
                        dve.wait_ge(sq_done, n + 1)
                        ge(dve, sd_done, g * TG + before(s, 2))
                        nc.vector.reduce_sum(ss[:, s % 2, :], sq[:, s % 2, :].rearrange("p (h e) -> p h e", e=HEAD),
                                             AX).then_inc(ss_done, 1)
                    if s >= 1:
                        j = s - 1
                        n = g * TG + j
                        dve.wait_ge(sd_done, n + 1)
                        link(nc.vector.reciprocal(rs, sd[:, j % 2, :]))
                        ge(dve, v_done, n)
                        link(nc.vector.tensor_tensor(rr, rs[:, 0:8], rs[:, 8:16], ALU.mult))
                        ge(dve, dots_done, g * TG + before(j, 2))
                        nc.vector.tensor_tensor(v_sb[:, j % 2, :].rearrange("p (h e) -> p h e", e=HEAD),
                                                ps_kv[j % 2][:, 512:1024].rearrange("p (h e) -> p h e", e=HEAD),
                                                rr.unsqueeze(2).to_broadcast([P, 8, HEAD]), ALU.mult).then_inc(v_done, 1)

            statistics(0)
            normalise(0)
            linked(first, last_apart=True)
            dve.wait_ge(dots_done, NT)
            dd = ps_dots.rearrange("p (c e) -> p c e", c=4)
            for h in range(2):
                q = slice(h * HEAD, (h + 1) * HEAD)
                nc.vector.tensor_scalar(dT[q, :, q], dd[q, :, q], 1.0 / N, None, ALU.mult).then_inc(dT_done, 1)

            def mix(g):
                for j in range(TG):
                    n = g * TG + j
                    dve.wait_ge(mix_done, n + 1)
                    ge(dve, xp_st[j], 16 * g)
                    link(nc.vector.tensor_tensor(xn[:, j, :], bank(j % 4)[:, 0:D], x_in[:, j, :], ALU.add))
                    nc.vector.tensor_tensor(xn[:, j, :], xn[:, j, :], bo_sb, ALU.add).then_inc(xp_ready, 1)

            dve.wait_ge(lo_done, NT)
            linked(mix)

            for l in range(2):
                def layer(g):
                    G = g + TG * l
                    dve.wait_ge(logit_done, G + 1)
                    nc.vector.tensor_tensor(lg[:], ps_lg, envb_sb[:, l, :].unsqueeze(1).to_broadcast([P, TG, EXPERTS]),
                                            ALU.add).then_inc(lg_read, 1)
                    dve.wait_ge(lg_read, G + 1)
                    link(nc.vector.reduce_max(red[:, 0, :], lg[:], AX))
                    nc.vector.tensor_tensor(lg[:], lg[:], red[:, 0, :].unsqueeze(2).to_broadcast([P, TG, EXPERTS]),
                                            ALU.subtract).then_inc(lg_sub, 1)
                    dve.wait_ge(lg_exp, G + 1)
                    link(nc.vector.reduce_sum(red[:, 1, :], lg[:], AX))
                    link(nc.vector.reciprocal(red[:, 2, :], red[:, 1, :]))
                    link(nc.vector.tensor_tensor(wts[:], lg[:], red[:, 2, :].unsqueeze(2).to_broadcast([P, TG, EXPERTS]),
                                                 ALU.mult))
                    nc.vector.reduce_sum(wsum[:], wts[:], AX).then_inc(wts_ready, 1)

                    def evacuate(b):
                        dve.wait_ge(a_used, TG * (2 * G + b + 1))
                        cols = slice(b * HR, (b + 1) * HR)
                        if l == 0:
                            if b == 0:
                                ge(dve, inv_st, 16 * g)
                            link(nc.vector.tensor_scalar(inv[:, cols], ps_cnt[b][:, 0:HR], 1.0, None, ALU.max))
                            link(nc.vector.reciprocal(inv[:, cols], inv[:, cols]))
                        else:
                            dve.wait_ge(inv_ld, 16 * (g + 1))
                        for half in range(2):
                            nc.vector.tensor_tensor(aggT[:, half, cols], ps_agg[b][half][:, 0:HR], inv[:, cols],
                                                    ALU.mult).then_inc(agg_evac, 1)

                    evacuate(0)
                    for s in range(TG + 1):
                        if s == 3:
                            evacuate(1)
                        if s < TG:
                            n = G * TG + s
                            dve.wait_ge(w_done, n + 1)
                            dve.wait_ge(acc_init, n + 1)
                            for e in range(EXPERTS):
                                ins = nc.vector.scalar_tensor_tensor(
                                    acc[:, s % 2, :], ps_out[s % 2][:, e * D:(e + 1) * D], wts[:, s, e:e + 1],
                                    acc[:, s % 2, :], ALU.mult, ALU.add)
                                if e < EXPERTS - 1:
                                    link(ins)
                            ins.then_inc(acc_done, 1)
                            if l == 1:
                                dve.wait_ge(acc_done, n + 1)
                                dve.wait_ge(xp_ld[s], 16 * (g + 1))
                                ge(dve, end_ready, g * TG - TG + s + 1)
                                nc.vector.scalar_tensor_tensor(x1[:, s, :], acc[:, s % 2, :], 0.0, xp_in[:, s, :],
                                                               ALU.max, ALU.add).then_inc(x1_done, 1)
                                dve.wait_ge(x1_done, g * TG + s + 1)
                                link(nc.vector.bn_stats(stats[:, s, :], x1[:, s, :]))
                        if s >= 1 and l == 0:
                            j = s - 1
                            n = G * TG + j
                            dve.wait_ge(hi2_done, n + 1)
                            nc.vector.tensor_tensor(zs2[:, n, 1, :], zn[:, j % 4, :], zs2[:, n, 0, :],
                                                    ALU.subtract).then_inc(lo2_done, 1)
                    if l == 1:
                        nc.vector.nop(nofuse=True)
                        for j in range(TG):
                            ins = nc.vector.bn_aggr(mv[:, j, :], stats[:, j, :])
                        ins.then_inc(var2_ready, 1)
                        dve.wait_ge(std2_ready, g + 1)
                        link(nc.vector.reciprocal(rstd[:], std[:]))
                        if isinstance(g, int) and g == 0:
                            dve.wait_ge(ffn_in, 48)
                        for j in range(TG):
                            ge(dve, end_st[j], 32 * g)
                            link(nc.vector.tensor_scalar(xn2[:, j, :], x1[:, j, :], mv[:, j, 0:1], rstd[:, j:j + 1],
                                                         ALU.subtract, ALU.mult))
                            nc.vector.tensor_tensor(base[:, j, :], x1[:, j, :], xn2[:, j, :], ALU.add).then_inc(end_ready, 1)
                            link(nc.vector.tensor_tensor_reduce(junk, xn2[:, j, :], wr_sb, 1.0, 0.0, ALU.mult, ALU.add,
                                                                red[:, 3, j:j + 1]))
                        link(nc.vector.tensor_scalar(wcol[:, bass.ds(g * TG, TG)], red[:, 3, :], br_sb, None, ALU.add))

                linked(layer)

            nc.vector.sem_inc(wcol_ready, 1)
            dve.wait_ge(wcol_cut, 1)
            dve.wait_ge(list_consts, 6)
            link(nc.vector.memset(u_t, 0))
            asked = [0]

            def as_float(u, n, target):
                link(nc.vector.tensor_scalar(t1[:, 0:n], u, 31, 0x7FFFFFFF, ALU.arith_shift_right, ALU.bitwise_and))
                link(nc.vector.tensor_tensor(target, t1[:, 0:n], u, ALU.bitwise_xor))
                link(nc.vector.tensor_scalar(target, target, -1, None, ALU.bitwise_xor))

            def summed():
                nc.vector.sem_inc(cand_ready, 1)
                asked[0] += 1
                dve.wait_ge(counted, asked[0])

            w3 = wcol[:].unsqueeze(1).to_broadcast([P, CN, NT])
            h3 = hits.rearrange("p (c t) -> p c t", c=CN)
            for b in range(32 - DIGIT, -1, -DIGIT):
                link(nc.vector.tensor_scalar(cand, ladder, b, None, ALU.logical_shift_left))
                link(nc.vector.tensor_tensor(cand, cand, u_t.to_broadcast([P, CN]), ALU.bitwise_or))
                as_float(cand, CN, cand)
                link(nc.vector.tensor_tensor(h3, w3, cand.bitcast(f32).unsqueeze(2).to_broadcast([P, CN, NT]), ALU.is_ge))
                link(nc.vector.reduce_sum(part, h3, AX))
                summed()
                link(nc.vector.tensor_scalar(met, bank(5)[:, 0:CN], TOPK - 0.5, None, ALU.is_ge, ALU.add, accum_out=digit_f))
                link(nc.vector.tensor_copy(digit, digit_f))
                link(nc.vector.tensor_scalar(digit, digit, b, None, ALU.logical_shift_left))
                link(nc.vector.tensor_tensor(u_t, u_t, digit, ALU.bitwise_or))
            as_float(u_t, 1, thr_i)
            thr = thr_i.bitcast(f32)
            link(nc.vector.tensor_scalar(gt, wcol[:], thr, None, ALU.is_gt, ALU.add, accum_out=part[:, 0:1]))
            link(nc.vector.tensor_scalar(eq, wcol[:], thr, None, ALU.is_equal))

            def offsets():
                link(nc.vector.tensor_copy(tot, bank(6)[:, 64:64 + NT]))
                link(nc.vector.tensor_tensor_scan(scan, tot, tot, 0.0, ALU.add, ALU.bypass))
                link(nc.vector.tensor_tensor(scan, scan, tot, ALU.subtract))

            summed()
            link(nc.vector.tensor_scalar(ntot, bank(5)[:, 0:1], -1.0, float(TOPK), ALU.mult, ALU.add))
            offsets()
            link(nc.vector.tensor_tensor(cum, bank(6)[:, 0:NT], scan, ALU.add))
            link(nc.vector.tensor_scalar(cum, cum, ntot, None, ALU.is_le))
            link(nc.vector.tensor_tensor(eq, eq, cum, ALU.mult))
            link(nc.vector.tensor_tensor(sel, eq, gt, ALU.add))
            summed()
            offsets()
            link(nc.vector.tensor_tensor(cum, bank(6)[:, 0:NT], scan, ALU.add))
            link(nc.vector.tensor_tensor(cum, cum, sel, ALU.mult))
            link(nc.vector.tensor_scalar(slot_i, cum, -1.0, None, ALU.add))
            link(nc.vector.tensor_scalar(slot_p, slot_i, P - 1, None, ALU.bitwise_and))
            link(nc.vector.tensor_scalar(slot_c, slot_i, 7, None, ALU.arith_shift_right))
            link(nc.vector.tensor_copy(at_p, slot_p))
            link(nc.vector.tensor_copy(at_c, slot_c))
            link(nc.vector.tensor_tensor(is_c, chunks.unsqueeze(1).to_broadcast([P, NT, CHUNKS]),
                                         at_c.unsqueeze(2).to_broadcast([P, NT, CHUNKS]), ALU.is_equal))
            link(nc.vector.tensor_tensor(is_c, is_c, nid.unsqueeze(2).to_broadcast([P, NT, CHUNKS]), ALU.mult))
            for i in range(TG):
                ge(dve, is_p_used, i - 1)
                nc.vector.tensor_tensor(is_p[i % 2], places.unsqueeze(1).to_broadcast([P, TG, P]),
                                        at_p[:, i * TG:(i + 1) * TG].unsqueeze(2).to_broadcast([P, TG, P]),
                                        ALU.is_equal).then_inc(is_p_ready, 1)
            dve.wait_ge(is_p_used, TG)
            nc.vector.tensor_tensor(idx, bank(7)[:, 0:CHUNKS], pads, ALU.add).then_inc(idx_ready, 1)

            def ffn(g):
                ge(dve, yo_ready, CH * g)
                for j in range(CH):
                    dve.wait_ge(xg_in[j], 16 * (g + 1))
                    link(nc.vector.tensor_tensor_reduce(fj, xg[:, j, :], wr_sb, 1.0, 0.0, ALU.mult, ALU.add, fw[:, j:j + 1]))
                nc.vector.tensor_scalar(fw, fw, br_sb, None, ALU.add).then_inc(fj_done, 1)
                dve.wait_ge(fj_done, g + 1)
                for j in range(CH):
                    dve.wait_ge(y_done, CH * g + j + 1)
                    dve.wait_ge(bg_in[j], 16 * (g + 1))
                    ge(dve, y_st[j], 16 * g)
                    ge(dve, yo_ready, CH * g + (j - 1 if j >= 2 else 0))
                    nc.vector.tensor_tensor(yt[:, j % 2, :], bank(2 + j % 2)[:, 0:D], b2_sb, ALU.add).then_inc(y_read, 1)
                    dve.wait_ge(y_read, CH * g + j + 1)
                    nc.vector.scalar_tensor_tensor(yo[:, j, :], yt[:, j % 2, :], fw[:, j:j + 1], bg[:, j, :],
                                                   ALU.mult, ALU.add).then_inc(yo_ready, 1)

            dve.wait_ge(ffn_in, 96)
            linked(ffn, CH)

        @block.tensor
        def _(pe):
            pe.wait_ge(consts, 1)
            a = sum(range(1, ROW_BITS + 1)) % 2
            c = 0

            def turn_over(K):
                pe.wait_ge(order_out, c)
                for m in range(F // P):
                    last = nc.tensor.transpose(ps_sort[:, m * P:(m + 1) * P], K[:, m * P:(m + 1) * P], ident[:])
                    if m % (F // P // 2) == F // P // 2 - 1:
                        last.then_inc(tposed, 1)

            for k in range(ROW_BITS + 1, BITS + 1):
                for stages in (k - ROW_BITS, ROW_BITS):
                    c += 1
                    turn_over(keys[a])
                    a = (a + 1 + stages) % 2
            c += 1
            turn_over(keys[0])
            c += 1
            turn_over(keys[1])

            pe.wait_ge(below_ready, 1)
            nc.tensor.matmul(bank(0)[:, 0:2 * TG], ones_f[0:EP, :], below[0:EP, :], start=True, stop=True).then_inc(below_summed, 1)

            pe.wait_ge(wkv_ready, 1)
            pe.wait_ge(bound_ready, 1)

            def first(g):
                for s in range(TG + 2):
                    if s < TG:
                        pe.wait_ge(xn_done, g * TG + s + 1)
                        ge(pe, xT_copied, g * TG + before(s, 2))
                        for kc in range(2):
                            last = nc.tensor.transpose(ps_T[:, s % 2, kc * P:(kc + 1) * P], xn[:, s, kc * P:(kc + 1) * P], ident[:])
                        last.then_inc(xT_done, 1)
                    if 1 <= s <= TG:
                        j = s - 1
                        pe.wait_ge(xT_copied, g * TG + j + 1)
                        ge(pe, v_done, g * TG + before(j, 2))
                        for b in range(2):
                            for kc in range(2):
                                last = nc.tensor.matmul(ps_kv[j % 2][:, b * 512:(b + 1) * 512], xnT[:, j, kc * P:(kc + 1) * P],
                                                        wkv_sb[:, kc, b * 512:(b + 1) * 512], start=(kc == 0), stop=(kc == 1))
                        last.then_inc(kv_done, 1)
                    if s >= 2:
                        j = s - 2
                        pe.wait_ge(v_done, g * TG + j + 1)
                        for c4 in range(4):
                            q = slice(c4 * P, (c4 + 1) * P)
                            last = nc.tensor.matmul(ps_dots[:, q], v_sb[:, j % 2, q], k_sb[:, j % 2, q],
                                                    start=(isinstance(g, int) and g == 0 and j == 0 and c4 == 0), stop=True,
                                                    skip_group_check=True)
                        last.then_inc(dots_done, 1)

            groups(pe, first)
            pe.wait_ge(dT_done, 2)
            for c4 in range(4):
                last = nc.tensor.matmul(ps_kv[0][:, c4 * D:(c4 + 1) * D], dT[:, c4, :], wo_sb[:, c4, :], start=True, stop=True)
            last.then_inc(gm_done, 1)
            pe.wait_ge(gm_copied, 1)
            for half in range(2):
                for c4 in range(4):
                    last = nc.tensor.matmul(ps_kv[1][:, half * D:(half + 1) * D], wq_sb[:, c4, half * P:(half + 1) * P],
                                            g_sb[:, c4, :], start=(c4 == 0), stop=(c4 == 3))
            last.then_inc(gm_done, 1)
            pe.wait_ge(gm_copied, 2)

            def mix(g):
                for j in range(TG):
                    pe.wait_ge(x_ld[j], 16 * TG + 32 * (g + 1))
                    ge(pe, xp_ready, g * TG + before(j, 4) if j >= 4 else (g * TG - TG + max(i for i in range(TG) if i % 4 == j % 4) + 1))
                    for kc in range(2):
                        last = nc.tensor.matmul(bank(j % 4)[:, 0:D], xnT[:, j, kc * P:(kc + 1) * P], m_sb[:, kc, :],
                                                start=(kc == 0), stop=(kc == 1))
                    last.then_inc(mix_done, 1)

            groups(pe, mix)
            pe.wait_ge(xp_ready, NT)
            pe.wait_ge(small_in, 32)

            for l in range(2):
                zs = zs1 if l == 0 else zs2
                pe.wait_ge(lo_done if l == 0 else lo2_done, NT)
                if l == 1:
                    pe.wait_ge(hi2_done, NT)

                def aggregate(g, b, between=None):
                    G = g + TG * l
                    ge(pe, agg_evac, 4 * G + 2 * b)
                    for u in range(TG):
                        if between is not None and u == 2:
                            between()
                        pe.wait_ge(a_in[u], 16 * (2 * G + b + 1))
                        for cc in range(TG):
                            ct = u * TG + cc
                            if l == 0:
                                nc.tensor.matmul(ps_cnt[b][:, 0:HR], ones16[:], a_ring[:, u, cc, :],
                                                 start=(ct == 0), stop=(ct == NT - 1))
                            for half in range(2):
                                for part_ in range(2):
                                    last = nc.tensor.matmul(
                                        ps_agg[b][half][:, 0:HR], zs[:, ct, part_, half * P:(half + 1) * P], a_ring[:, u, cc, :],
                                        start=(ct == 0 and part_ == 0), stop=(ct == NT - 1 and part_ == 1))
                        last.then_inc(a_used, 1)

                def layer(g):
                    G = g + TG * l
                    for js in T_ORDER:
                        ge(pe, acc_done, G * TG - (1 if js[0] >= 4 else 0))
                        for j in js:
                            pe.wait_ge(z_ld[j], 16 * (G + 1))
                            for kc in range(2):
                                last = nc.tensor.transpose(ps_zT[:, j * D + kc * P:j * D + (kc + 1) * P],
                                                           z_in[:, j, kc * P:(kc + 1) * P], ident[:])
                        last.then_inc(t_done, 1)

                    def logits():
                        pe.wait_ge(t_copied, (G + 1) * TB)
                        for j in range(TG):
                            for kc in range(2):
                                last = nc.tensor.matmul(ps_lg[:, j, :], zT[:, j, kc * P:(kc + 1) * P], envw_sb[:, l, kc, :],
                                                        start=(kc == 0), stop=(kc == 1))
                        last.then_inc(logit_done, 1)

                    def experts(j):
                        ge(pe, acc_done, G * TG + before(j, 2))
                        if j == 1:
                            pe.wait_ge(lg_read, G + 1)
                        for b in range(2):
                            q = slice(b * 512, (b + 1) * 512)
                            for i, kc in enumerate((2, 3, 0, 1)):
                                if b == 0 and i == 2:
                                    pe.wait_ge(agg_evac, 4 * G + (2 if j < 3 else 4))
                                w = zT[:, j, (kc - 2) * P:(kc - 1) * P] if kc >= 2 else aggT[:, kc, j * P:(j + 1) * P]
                                last = nc.tensor.matmul(ps_out[j % 2][:, q], w, gw_sb[:, kc, q], start=(i == 0), stop=(i == 3))
                        last.then_inc(w_done, 1)

                    aggregate(g, 0, logits)
                    if isinstance(g, int) and g == 0:
                        pe.wait_ge(gw_in, 16 * (l + 1))
                    for j in range(3):
                        experts(j)
                    aggregate(g, 1)
                    for j in range(3, TG):
                        experts(j)

                groups(pe, layer)

            rounds = 32 // DIGIT
            for n in range(rounds):
                pe.wait_ge(cand_ready, n + 1)
                nc.tensor.matmul(bank(5)[:, 0:CN], ones_f[:], part, start=True, stop=True).then_inc(counted, 1)
            pe.wait_ge(cand_ready, rounds + 1)
            nc.tensor.matmul(bank(5)[:, 0:1], ones_f[:], part[:, 0:1], start=True, stop=True)
            nc.tensor.matmul(bank(6)[:, 0:NT], tri[:], eq, start=True, stop=True)
            nc.tensor.matmul(bank(6)[:, 64:64 + NT], ones_f[:], eq, start=True, stop=True).then_inc(counted, 1)
            pe.wait_ge(cand_ready, rounds + 2)
            nc.tensor.matmul(bank(6)[:, 0:NT], tri[:], sel, start=True, stop=True)
            nc.tensor.matmul(bank(6)[:, 64:64 + NT], ones_f[:], sel, start=True, stop=True).then_inc(counted, 1)
            for i in range(TG):
                pe.wait_ge(is_p_ready, i + 1)
                for t in range(TG):
                    last = nc.tensor.matmul(bank(7)[:, 0:CHUNKS], is_p[i % 2][:, t, :], is_c[:, i * TG + t, :],
                                            start=(i == 0 and t == 0), stop=(i == TG - 1 and t == TG - 1))
                last.then_inc(is_p_used, 1)

            pe.wait_ge(ffn_in, 96)

            def x2_transposes(g):
                for j in range(CH):
                    pe.wait_ge(xg_in[j], 16 * (g + 1))
                    ge(pe, f_tc, CH * g + (j - 1 if j >= 2 else 0))
                    for kc in range(2):
                        last = nc.tensor.transpose(ps_T[:, j % 2, kc * P:(kc + 1) * P], xg[:, j, kc * P:(kc + 1) * P], ident[:])
                    last.then_inc(f_t, 1)

            def ffn(g, more=True):
                pe.wait_ge(f_tc, CH * (g + 1))
                for half in range(2):
                    for m in range(8):
                        q = half * 8 + m
                        ge(pe, h_act, 16 * g + q - 1)
                        for kc in range(2):
                            last = nc.tensor.matmul(bank(q % 2)[:, 0:FH], w1_sb[:, kc, m * P:(m + 1) * P],
                                                    x2T[:, kc, half * FH:(half + 1) * FH], start=(kc == 0), stop=(kc == 1))
                        last.then_inc(h_done, 1)
                if more:
                    x2_transposes(g + 1)
                for j in range(CH):
                    pe.wait_ge(h_act, 16 * g + (8 if j < 2 else 16))
                    ge(pe, y_read, CH * g + (j - 1 if j >= 2 else 0))
                    for m in range(8):
                        last = nc.tensor.matmul(bank(2 + j % 2)[:, 0:D], hT[:, m, j * P:(j + 1) * P], w2_sb[:, m, :],
                                                start=(m == 0), stop=(m == 7))
                    last.then_inc(y_done, 1)

            x2_transposes(0)
            ffn(0)
            with pe.Fori(1, CH - 1) as g:
                ffn(g)
            ffn(CH - 1, False)


def kernel(**inputs):
    import numpy as np
    import concourse.bacc as bacc
    from concourse import mybir
    from concourse.bass_utils import run_bass_kernel_spmd

    def arr(name):
        return np.asarray(inputs[name])

    def pieces(w, n):
        return w.reshape(n, P, -1).transpose(1, 0, 2)

    x = np.zeros((NP, D), np.float32)
    x[:N] = arr("x")
    W = arr("L0_gnn_W")
    wqkv = arr("L0_mix_w_qkv")
    envw = arr("L0_gnn_envW")
    laid = {
        "x": x, "src": arr("src"), "dst": arr("dst"),
        "gw": np.stack([pieces(W[l].transpose(1, 0, 2).reshape(2 * D, EXPERTS * D), 4) for l in range(2)]),
        "envw": envw.reshape(2, 2, P, EXPERTS).transpose(2, 0, 1, 3),
        "envb": np.broadcast_to(arr("L0_gnn_envb")[None], (P, 2, EXPERTS)),
        "wkv": pieces(wqkv[512:].T, 2),
        "wq": pieces(wqkv[:512], 4),
        "wo": pieces(arr("L0_mix_w_out").T, 4),
        "bo": np.broadcast_to(arr("L0_mix_b_out")[None], (P, D)),
        "wr": np.broadcast_to(arr("L0_ffn_wr").reshape(1, D), (P, D)),
        "br": np.broadcast_to(arr("L0_ffn_br").reshape(1, 1), (P, 1)),
        "w1": pieces(arr("L0_ffn_w1"), 2),
        "b1": arr("L0_ffn_b1").reshape(8, P).T,
        "w2": pieces(arr("L0_ffn_w2"), 8),
        "b2": np.broadcast_to(arr("L0_ffn_b2")[None], (P, D)),
    }
    nc = bacc.Bacc("TRN2", target_bir_lowering=False, num_devices=1)
    arrays, args = {}, []
    for name, a in laid.items():
        a = np.ascontiguousarray(a)
        arrays[f"in_{name}"] = a
        args.append(nc.dram_tensor(f"in_{name}", a.shape, mybir.dt.from_np(a.dtype), kind="ExternalInput").ap())
    args.append(nc.dram_tensor("out_0", (NP + P, D), mybir.dt.float32, kind="ExternalOutput").ap())
    build(nc, *args)
    r = run_bass_kernel_spmd(nc, [arrays], core_ids=[0])
    return r.results[0]["out_0"][:N]
```

```python
import concourse.bass as bass
from concourse import mybir
from contextlib import ExitStack
import numpy as np

P = 128
N = 6250
D = 256
E = 206250
TG = 7
NT = TG * TG
NP = NT * P
GR = TG * P
HR = GR // 2
EXPERTS = 4
H = 1024
KV = 1024
HEAD = 64
EPS = 1e-5
F = 2048
F_ACT = 3 * F // 4
BITS, ROW_BITS = 18, 11
EP = 125
EC = E // EP
CB = 13
NODE = (1 << CB) - 1
KEY_BASE = 0x40000000
KEY_PAD = 0x44000000
EW_BITS = 7
EW = -(-EC // (1 << EW_BITS)) << EW_BITS
SPARE = 7168
A_ROWS = SPARE + (1 << (BITS - CB))
TURN = F // P
TURNS = E // F
LAST = -(-(E - TURNS * F) // P)
EARLY = [(3, 0), (3, 1), (4, 0), (4, 1), (5, 0), (5, 1), (6, 0)]
HALVES = [2] * (TG - 1) + [1]


def known(s, b):
    return sum(EARLY[s]) if b < HALVES[s] else 0


def early_before(at):
    return sum(n for place, n in zip(EARLY, HALVES) if place < at)


ALIKE = [[(0, 1), (1, 3), (3, 4), (4, 5), (5, 6), (6, 7)], [(0, 1), (1, 3), (3, 5), (5, 6), (6, 7)]]
PIECES = [(0, 4), (4, TG)]
TOPK = N // 2 - 1
CH = 5
CHUNKS = CH * CH
WS = 256.0
DIGIT = 4
FH = CH * P // 2


def before(j, ring):
    if j >= ring:
        return j - ring + 1
    return max(i for i in range(TG) if i % ring == j % ring) - TG + 1


def passes():
    order = []
    for g in range(TG):
        for b in range(2):
            order.append((0, g, b, range(TG)))
            if (g, b) in EARLY:
                s = EARLY.index((g, b))
                order += [(2, s, h, range(known(s, h))) for h in range(HALVES[s])]
    order += [(1, g, b, range(known(g, b), TG)) for g in range(TG) for b in range(2)]
    table, n, last, loads, counted = {}, 0, [0] * TG, [0] * TG, [0] * TG
    for l, g, b, us in order:
        table[l, g, b] = (us, n, list(last), list(loads), list(counted))
        for u in us:
            if l == 0:
                counted[u] = TG * (2 * g + b) + u + 1
            n += 1
            last[u] = n
            loads[u] += 1
    return table, n


PASSES, A_CHUNKS = passes()


def along(values, g, lo):
    if isinstance(g, int):
        return values(g)
    return g * (values(lo + 1) - values(lo)) + (values(lo) - lo * (values(lo + 1) - values(lo)))


def ge(eng, sem, value, nop=False):
    if not (isinstance(value, int) and value <= 0):
        eng.wait_ge(sem, value)
        if nop and not isinstance(value, int):
            eng.nop(nofuse=True)


def build(nc, x, src, dst, gw, envw, envb, wkv, wq, wo, bo, wr, br, w1, b1, w2, b2, out):
    f32, i32, f16 = mybir.dt.float32, mybir.dt.int32, mybir.dt.float16
    ALU = mybir.AluOpType
    ACT = mybir.ActivationFunctionType
    AX = mybir.AxisListType.X
    ctx = ExitStack()
    with ctx:
        def sb(name, shape, dt):
            return ctx.enter_context(nc.sbuf_tensor(name, shape, dt))

        def sem(name):
            return ctx.enter_context(nc.semaphore(name))

        def sems(name, n):
            return [sem(f"{name}{i}") for i in range(n)]

        def dram(name, shape, dt):
            return nc.dram_tensor(name, shape, dt).ap()

        class Carver:

            def __init__(self, base):
                self.base, self.at = base, 0

            def __call__(self, n, dt=f32):
                a = self.base[:, self.at:self.at + n]
                self.at += n
                assert self.at <= self.base.shape[1]
                return a if dt == f32 else a.bitcast(dt)

        ZW = NT * D
        zs1 = sb("zs1", [P, NT, 2, D], f16)
        arena = sb("arena", [P, ZW + TG * TG * HR // 2], f32)
        zs2 = arena[:, 0:ZW].bitcast(f16).rearrange("p (t s d) -> p t s d", t=NT, s=2)
        a_ring = arena[:, ZW:].bitcast(f16).rearrange("p (u c r) -> p u c r", u=TG, c=TG)
        addr = sb("addr", [P, F], i32)
        cnt16 = sb("cnt16", [P, F], f16)
        cur_addr = sb("cur_addr", [P, 2, TURN], i32)
        cur_cnt = sb("cur_cnt", [P, 2, TURN], f16)
        gws = sb("gws", [P, 2, 4, EXPERTS * D], f16)
        envs = sb("envs", [P, 2, 2, 2, EXPERTS], f16)
        mean = sb("mean", [P, 2, HR], f32)
        aggT = sb("aggT", [P, 2, 2, GR], f16)
        zT = sb("zT", [P, TG, 2, 2, P], f16)
        z_in = sb("z_in", [P, TG, D], f32)
        zn = sb("zn", [P, 4, D], f32)
        acc = sb("acc", [P, 2, D], f32)
        inv = sb("inv", [P, GR], f32)
        ident = sb("ident", [P, P], f32)
        ones_f = sb("ones_f", [P, P], f32)
        tri = sb("tri", [P, P], f32)
        ident16 = sb("ident16", [P, P], f16)
        eps = sb("eps", [P, 1], f32)
        envw_sb = sb("envw_sb", [P, 2, 2, EXPERTS], f32)
        envb_sb = sb("envb_sb", [P, 2, EXPERTS], f32)
        lg = sb("lg", [P, TG, EXPERTS], f32)
        wts = sb("wts", [P, TG, EXPERTS], f32)
        red = sb("red", [P, 4, TG], f32)
        wsum = sb("wsum", [P, TG], f32)
        mv = sb("mv", [P, TG, 2], f32)
        stats = sb("stats", [P, TG, 6], f32)
        std = sb("std", [P, TG], f32)
        rstd = sb("rstd", [P, TG], f32)
        wcol = sb("wcol", [P, NT], f32)
        bound = sb("bound", [P, 2 * TG], i32)
        ps = ctx.enter_context(nc.psum_tensor("ps", [P, 8, 512], f32))

        c = Carver(arena)
        keys = [c(F), c(F)]
        src_in, dst_in = c(EC, i32), c(EC, i32)
        pos, spare, same, run, tmp = c(F), c(F, i32), c(F, i32), c(F), c(F, i32)
        qid, qbit, qxor, sgn = c(1, i32), c(9, i32), c(8, i32), c(9)
        edge_next, edge_prev, carry, cexcl = c(1), c(1), c(1), c(P + 1)
        below, zeros_row = c(2 * TG), c(P)
        assert c.at <= ZW + TG * TG * HR // 2
        c = Carver(arena)
        x_in = c(TG * D).rearrange("p (j d) -> p j d", j=TG)
        xn = c(TG * D).rearrange("p (j d) -> p j d", j=TG)
        xnT = c(TG * D).rearrange("p (j d) -> p j d", j=TG)
        sq = c(2 * KV).rearrange("p (s e) -> p s e", s=2)
        k_sb = c(KV).rearrange("p (s e) -> p s e", s=2)
        v_sb = c(KV).rearrange("p (s e) -> p s e", s=2)
        wkv_sb = c(2 * KV).rearrange("p (c e) -> p c e", c=2)
        wmean = c(32).rearrange("p (c h) -> p c h", c=2)
        ss = c(32).rearrange("p (s h) -> p s h", s=2)
        sd = c(32).rearrange("p (s h) -> p s h", s=2)
        rs = c(16)
        rr = c(8)
        wq_sb = c(4 * D).rearrange("p (c e) -> p c e", c=4)
        wo_sb = c(4 * D).rearrange("p (c e) -> p c e", c=4)
        dT = c(4 * P).rearrange("p (c e) -> p c e", c=4)
        g_sb = c(4 * D).rearrange("p (c e) -> p c e", c=4)
        m_sb = c(2 * D).rearrange("p (c e) -> p c e", c=2)
        bo_sb = c(D)
        gw_raw = [c(4 * EXPERTS * D)]
        z1_words = zs1[:].rearrange("p t s d -> p (t s d)").bitcast(f32)
        c = Carver(z1_words)
        xp_in = c(TG * D).rearrange("p (j d) -> p j d", j=TG)
        x1 = c(TG * D).rearrange("p (j d) -> p j d", j=TG)
        gw_raw.append(z1_words[:, c.at:c.at + 4 * EXPERTS * D])
        xn2 = c(TG * D).rearrange("p (j d) -> p j d", j=TG)
        base = c(TG * D).rearrange("p (j d) -> p j d", j=TG)
        wr_sb, junk = c(D), c(D)
        br_sb = c(1)
        early_in = c(4 * HR).rearrange("p (b h r) -> p b h r", b=2, h=2)
        w1_raw = c(2 * H)
        c = Carver(arena)
        w2_raw = c(8 * D)
        w1s = c(2 * H, f16).rearrange("p (s c e) -> p s c e", s=2, c=2)
        w2s = c(8 * D, f16).rearrange("p (s c e) -> p s c e", s=2, c=8)
        b1_sb, b2_sb = c(8), c(D)
        h_sb = c(2 * FH).rearrange("p (u r) -> p u r", u=2)
        hT = c(8 * CH * P, f16).rearrange("p (s m r) -> p s m r", s=2, m=8)
        x2T = c(2 * CH * P, f16).rearrange("p (s k r) -> p s k r", s=2, k=2)
        xg = c(CH * D).rearrange("p (j d) -> p j d", j=CH)
        bg = c(CH * D).rearrange("p (j d) -> p j d", j=CH)
        yo = c(CH * D).rearrange("p (j d) -> p j d", j=CH)
        yt = c(2 * D).rearrange("p (j d) -> p j d", j=2)
        fj, fw = c(D), c(CH)
        CN = (1 << DIGIT) - 1
        u_t, digit, thr_i = c(1, i32), c(1, i32), c(1, i32)
        ladder, cand, t1 = c(CN, i32), c(CN, i32), c(CN, i32)
        hits, part, met = c(CN * NT), c(CN), c(CN)
        digit_f = c(1)
        gt, eq, cum, tot, scan, sel = c(NT), c(NT), c(NT), c(NT), c(NT), c(NT)
        ntot = c(1)
        slot_i, slot_p, slot_c = c(NT, i32), c(NT, i32), c(NT, i32)
        nid, at_p, at_c = c(NT), c(NT), c(NT)
        places, chunks = c(P), c(CHUNKS)
        pads = c(CHUNKS)
        is_p = c(TG * P).rearrange("p (t r) -> p t r", t=TG), c(TG * P).rearrange("p (t r) -> p t r", t=TG)
        is_c = c(NT * CHUNKS).rearrange("p (t r) -> p t r", t=NT)
        idx = c(CHUNKS, i32)
        cur_g, cur_s = c(CH, i32), c(CH, i32)

        A = dram("A", [A_ROWS << CB, 1], f16)
        A_tiles = A[0:NP << CB, :].rearrange("(ct p r) o -> p ct (r o)", p=P, r=NODE + 1)
        zero_rows = zs1[:].rearrange("p t s d -> p (t s d)")[:, 0:NP]
        zd = [dram("zd0", [NP, D], f32), dram("zd1", [NP, D], f32)]
        xTd = dram("xTd", [P, NT, D], f32)
        xpd = dram("xpd", [NP, D], f32)
        earlyd = dram("earlyd", [2 * len(EARLY) * P, 2, HR], f32)
        invd = dram("invd", [1, NP], f32)
        xn2d = dram("xn2d", [NP + P, D], f32)

        def rows(t):
            return t.rearrange("(n p) d -> p n d", p=P)

        consts = sem("consts")
        order_in = sem("order_in")
        edges_in, step = sem("edges_in"), sem("step")
        order_out, tposed, act_copied = sem("order_out"), sem("tposed"), sem("act_copied")
        sorted_s, carry_s, carried, lists_ready = sem("sorted_s"), sem("carry_s"), sem("carried"), sem("lists_ready")
        zero_made, a_zeroed = sem("zero_made"), sem("a_zeroed")
        scat, landed = sems("scat", 3), sem("landed")
        small_in, wmix_in, gw_in, ffn_in = sem("small_in"), sem("wmix_in"), sem("gw_in"), sem("ffn_in")
        env_split, gw_hi, gw_lo = sem("env_split"), sem("gw_hi"), sem("gw_lo")
        w_scaled, w_hi, w_lo = sem("w_scaled"), sem("w_hi"), sem("w_lo")
        below_ready, below_summed, bound_ready = sem("below_ready"), sem("below_summed"), sem("bound_ready")
        early_free = sem("early_free")
        x_ld, n_st = sems("x_ld", TG), sems("n_st", TG)
        var_ready, std_ready = sem("var_ready"), sem("std_ready")
        xn_done, hi_done, xT_done, xT_copied = sem("xn_done"), sem("hi_done"), sem("xT_done"), sem("xT_copied")
        wkv_ready, kv_done, sq_done, ss_done, sd_done = sem("wkv_ready"), sem("kv_done"), sem("sq_done"), sem("ss_done"), sem("sd_done")
        v_done, dots_done, dT_done, lo_done = sem("v_done"), sem("dots_done"), sem("dT_done"), sem("lo_done")
        gm_done, gm_copied = sem("gm_done"), sem("gm_copied")
        mix_done, xp_ready, xp_st = sem("mix_done"), sem("xp_ready"), sems("xp_st", 2)
        a_in, a_used, agg_evac = sems("a_in", TG), sem("a_used"), sem("agg_evac")
        agg_hi, agg_lo = sem("agg_hi"), sem("agg_lo")
        a_counted, cnt_ready, cnt_done = sem("a_counted"), sem("cnt_ready"), sem("cnt_done")
        z_ld = x_ld
        Z0 = [16 * TG * (3 if j < len(PIECES) else 1) for j in range(TG)]
        early_evac, early_st, early_ld = sem("early_evac"), sems("early_st", 2), sems("early_ld", 2)
        t_done, t_copied = sem("t_done"), sem("t_copied")
        logit_done, lg_read, lg_sub, lg_exp, wts_ready = sem("logit_done"), sem("lg_read"), sem("lg_sub"), sem("lg_exp"), sem("wts_ready")
        w_done, acc_init, acc_done = sem("w_done"), sem("acc_init"), sem("acc_done")
        zn_ready, hi2_done, lo2_done, zn_st = sem("zn_ready"), sem("hi2_done"), sem("lo2_done"), sems("zn_st", 4)
        inv_st, inv_ld, xp_ld = sem("inv_st"), sem("inv_ld"), sems("xp_ld", TG)
        x1_done, end_ready = sem("x1_done"), sem("end_ready")
        end_st = sems("end_st", TG)
        list_consts, is_p_ready, is_p_used, idx_ready, fj_done = sem("list_consts"), sem("is_p_ready"), sem("is_p_used"), sem("idx_ready"), sem("fj_done")
        wcol_ready, wcol_cut, cand_ready, counted = sem("wcol_ready"), sem("wcol_cut"), sem("cand_ready"), sem("counted")
        idx_cp = sem("idx_cp")
        x2_lo, h_lo = sem("x2_lo"), sem("h_lo")
        xg_in, bg_in, y_st = sems("xg_in", CH), sems("bg_in", CH), sems("y_st", CH)
        f_t, f_tc, h_done, h_act, y_done, y_read, yo_ready = (
            sem("f_t"), sem("f_tc"), sem("h_done"), sem("h_act"), sem("y_done"), sem("y_read"), sem("yo_ready"))

        T_ORDER = [(4, 5), (6,), (0, 1), (2, 3)]
        TB = len(T_ORDER)

        def bank(b, n=1):
            return ps[:, b:b + n, :].rearrange("p b c -> p (b c)")

        ps_sort, ps_carry = bank(0, 4), bank(4)
        ps_kv = [bank(0, 2), bank(2, 2)]
        ps_T = ps[:, 4:6, 0:D]
        ps_x2 = ps_T
        ps_dots = bank(6)
        ps_agg = [[bank(0), bank(1)], [bank(2), bank(3)]]
        ps_out = [bank(4, 2), bank(6, 2)]
        ps_cnt = [bank(2), bank(0)]
        ps_zT = bank(4, 4).bitcast(f16).rearrange("p (j s k r) -> p j s k r", j=2 * 4, s=2, k=2)
        ps_lg = bank(7)[:, 256:256 + TG * EXPERTS].rearrange("p (j k) -> p j k", j=TG)

        ffn_weights = ((w1s, w1_raw), (w2s, w2_raw))

        def flat(t):
            return t.rearrange("p c e -> p (c e)")

        PRODUCTS = ((0, 0), (0, 1), (1, 0))

        block = ctx.enter_context(nc.Block())

        def groups(eng, body, last_apart=False):
            body(0)
            with eng.Fori(1, TG - 1 if last_apart else TG) as g:
                body(g)
            if last_apart:
                body(TG - 1)

        def alike(eng, l, body):
            for lo, hi in ALIKE[l]:
                if hi == lo + 1:
                    body(lo, lo)
                else:
                    with eng.Fori(lo, hi) as g:
                        body(g, lo)

        @block.sync
        def _(sp):
            sp.dma_start(src_in[0:EP, :], src.rearrange("(p t) -> p t", p=EP)).then_inc(edges_in, 16)
            sp.dma_start(dst_in[0:EP, :], dst.rearrange("(p t) -> p t", p=EP)).then_inc(edges_in, 16)
            sp.dma_start(envw_sb[:], envw).then_inc(small_in, 16)
            sp.dma_start(envb_sb[:], envb).then_inc(small_in, 16)
            sp.wait_ge(sorted_s, 1)
            sp.dma_start(edge_next[0:P - 1, :], keys[0][1:P, 0:1]).then_inc(carry_s, 16)
            sp.dma_start(edge_prev[1:P, :], keys[0][0:P - 1, F - 1:F]).then_inc(carry_s, 16)

            sp.wait_ge(early_free, 1)
            sp.dma_start(wkv_sb, wkv).then_inc(wmix_in, 16)
            sp.dma_start(wq_sb, wq).then_inc(wmix_in, 16)
            sp.dma_start(wo_sb, wo).then_inc(wmix_in, 16)
            sp.dma_start(bo_sb, bo).then_inc(wmix_in, 16)
            sp.dma_start(gw_raw[0], gw[0]).then_inc(gw_in, 16)

            def loads(g):
                for j in range(TG):
                    ge(sp, xn_done, g * TG - TG + j + 1, nop=True)
                    sp.dma_start(x_in[:, j, :], rows(x)[:, g * TG + j, :]).then_inc(x_ld[j], 16)

            def stores(g):
                for j in range(TG):
                    ge(sp, xn_done, g * TG + j + 1, nop=True)
                    sp.dma_start(rows(zd[0])[:, g * TG + j, :], xn[:, j, :]).then_inc(n_st[j], 16)
                    ge(sp, xT_copied, g * TG + j + 1, nop=True)
                    sp.dma_start(xTd[:, g * TG + j, :], xnT[:, j, :]).then_inc(n_st[j], 16)

            loads(0)
            loads(1)
            stores(0)
            with sp.Fori(1, TG - 1) as g:
                loads(g + 1)
                stores(g)
            stores(TG - 1)
            for j in range(TG):
                sp.wait_ge(n_st[j], 32 * TG)

            def mix_load(g, i):
                lo, hi = PIECES[i]
                ge(sp, xp_ready, g * TG - TG + hi, nop=True)
                sp.dma_start(x_in[:, lo:hi, :], rows(x)[:, bass.ds(g * TG + lo, hi - lo), :]).then_inc(x_ld[i], 16)
                sp.dma_start(xnT[:, lo:hi, :], xTd[:, bass.ds(g * TG + lo, hi - lo), :]).then_inc(x_ld[i], 16)

            def mix_store(g, i):
                lo, hi = PIECES[i]
                ge(sp, xp_ready, g * TG + hi, nop=True)
                sp.dma_start(rows(xpd)[:, bass.ds(g * TG + lo, hi - lo), :], xn[:, lo:hi, :]).then_inc(xp_st[i], 16)

            def mixing(g):
                for i in range(2):
                    mix_load(g + 1, i)
                    mix_store(g, i)

            sp.wait_ge(kv_done, NT)
            mix_load(0, 0)
            mix_load(0, 1)
            mixing(0)
            with sp.Fori(1, TG - 1) as g:
                mixing(g)
            for i in range(2):
                mix_store(TG - 1, i)
            for i in range(2):
                sp.wait_ge(xp_st[i], 16 * TG)
            sp.wait_ge(gw_lo, 4)

            sp.wait_ge(bound_ready, 1)
            for l in range(2):
                def tiles_of_a(g, lo, b, us=None, kind=l):
                    if kind == 0 and (us is None or 0 in us):
                        sp.wait_ge(landed, sp.value_load(bound[0:1, bass.ds(2 * g + b, 1)], min_val=1, max_val=TURNS + 1))
                        sp.nop(nofuse=True)
                    for u in PASSES[kind, lo, b][0] if us is None else us:
                        ge(sp, a_used, along(lambda g_: PASSES[kind, g_, b][2][u], g, lo), nop=True)
                        ge(sp, a_counted, along(lambda g_: PASSES[kind, g_, b][4][u], g, lo), nop=True)
                        sp.dma_start(a_ring[:, u, :, :],
                                     A_tiles[:, u * TG:(u + 1) * TG, bass.ds(g * GR + b * HR, HR)]).then_inc(a_in[u], 16)

                def early_tiles(lo, b):
                    if l == 0 and (lo, b) in EARLY:
                        row_group = EARLY.index((lo, b))
                        for half in range(HALVES[row_group]):
                            tiles_of_a(row_group, row_group, half, kind=2)

                def ends(g):
                    for j in range(TG):
                        ge(sp, end_ready, g * TG + j + 1, nop=True)
                        sp.dma_start(rows(xn2d[0:NP, :])[:, g * TG + j, :], xn2[:, j, :]).then_inc(end_st[j], 16)
                        sp.dma_start(rows(out[0:NP, :])[:, g * TG + j, :], base[:, j, :]).then_inc(end_st[j], 16)

                def z_loads(g, js):
                    for j in js:
                        ge(sp, acc_init, NT * l + g * TG - TG + j + 1, nop=True)
                        sp.dma_start(z_in[:, j, :], rows(zd[l])[:, g * TG + j, :]).then_inc(z_ld[j], 16)

                def layer(g, lo):
                    first = lo == 0
                    if l == 1 and first:
                        tiles_of_a(g, lo, 0)
                        sp.wait_ge(a_used, PASSES[1, 0, 0][1])
                        sp.dma_start(gw_raw[1], gw[1]).then_inc(gw_in, 16)
                        for s in range(4):
                            sp.wait_ge(zn_st[s], 16 * TG * (2 if s < 3 else 1))
                        z_loads(g, range(TG))
                        sp.wait_ge(inv_st, 16 * TG)
                        for half in range(2):
                            sp.wait_ge(early_st[half], 16 * sum(HALVES))
                    elif l == 1:
                        tiles_of_a(g, lo, 0)
                        z_loads(g, range(TG))
                    else:
                        z_loads(g, range(0, 5))
                        tiles_of_a(g, lo, 0, range(0, 4))
                        z_loads(g, range(5, TG))
                        tiles_of_a(g, lo, 0, range(4, TG))
                    early_tiles(lo, 0)
                    if l == 1:
                        ge(sp, agg_evac, 4 * (TG + g), nop=True)
                        sp.dma_start(inv[:], invd[0:1, bass.ds(g * GR, GR)].to_broadcast([P, GR])).then_inc(inv_ld, 16)
                        for b in range(2):
                            if known(lo, b):
                                ge(sp, agg_evac, 4 * (TG + g) + 2 * b - 2, nop=True)
                                sp.dma_start(early_in[:, b], earlyd[bass.ds((2 * g + b) * P, P)]).then_inc(early_ld[b], 16)
                        if first:
                            sp.wait_ge(gw_lo, 8)
                            sp.dma_start(wr_sb, wr).then_inc(ffn_in, 16)
                            sp.dma_start(br_sb, br).then_inc(ffn_in, 16)
                            sp.dma_start(w1_raw, w1).then_inc(ffn_in, 16)
                        for j in range(TG):
                            ge(sp, x1_done, g * TG - TG + j + 1, nop=True)
                            sp.dma_start(xp_in[:, j, :], rows(xpd)[:, g * TG + j, :]).then_inc(xp_ld[j], 16)
                        if not first:
                            ends(g - 1)
                    tiles_of_a(g, lo, 1)
                    early_tiles(lo, 1)

                alike(sp, l, layer)
                if l == 1:
                    ends(TG - 1)
            sp.wait_ge(a_used, A_CHUNKS)
            sp.wait_ge(w_done, 2 * NT)
            sp.dma_start(w2_raw, w2).then_inc(ffn_in, 16)
            sp.dma_start(b1_sb, b1).then_inc(ffn_in, 16)
            sp.dma_start(b2_sb, b2).then_inc(ffn_in, 16)

        @block.gpsimd
        def _(pool):
            nc.gpsimd.memset(ones_f[:], 1.0).then_inc(order_in, 1)
            pool.wait_ge(order_in, 1)
            nc.gpsimd.affine_select(out=ident[:], in_=ones_f[:], compare_op=ALU.is_equal, fill=0.0, base=0,
                                    pattern=[[-1, P]], channel_multiplier=1).then_inc(consts, 1)
            nc.gpsimd.iota(qid, pattern=[[0, 1]], base=0, channel_multiplier=1).then_inc(consts, 1)
            nc.gpsimd.iota(pos, pattern=[[1, F]], base=0, channel_multiplier=F,
                           allow_small_or_imprecise_dtypes=True).then_inc(consts, 1)
            nc.gpsimd.iota(same, pattern=[[1, F]], base=0, channel_multiplier=F).then_inc(consts, 1)
            nc.gpsimd.affine_select(out=tri[:], in_=ones_f[:], compare_op=ALU.is_ge, fill=0.0, base=0,
                                    pattern=[[1, P]], channel_multiplier=-1).then_inc(consts, 1)

            pool.wait_ge(a_zeroed, 16 * (NT + 2))
            pool.wait_ge(lists_ready, 2)
            by_turn = addr[:].rearrange("p (m q) -> p q m", q=P)
            by_turn_cnt = cnt16[:].rearrange("p (m q) -> p q m", q=P)

            def turn(i, s, n=TURN, sem_=None, q=None):
                q = 2 * i + s if q is None else q
                nc.gpsimd.tensor_copy(cur_addr[:, s, 0:n], by_turn[:, q, 0:n]).then_inc(idx_cp, 1)
                nc.gpsimd.tensor_copy(cur_cnt[:, s, 0:n], by_turn_cnt[:, q, 0:n]).then_inc(idx_cp, 1)
                ge(pool, idx_cp, 2 * q + 2, nop=True)
                for m in range(n):
                    nc.gpsimd.indirect_dma_start(A, bass.IndirectOffsetOnAxis(ap=cur_addr[:, s, m:m + 1], axis=0),
                                                 cur_cnt[:, s, m:m + 1], None).then_inc(scat[s] if sem_ is None else sem_, 16)

            def pair(i):
                for s in (0, 1):
                    if not (isinstance(i, int) and i == 0):
                        ge(pool, scat[s], 16 * TURN * i, nop=True)
                        pool.sem_inc(landed, 1)
                    turn(i, s)

            pair(0)
            with pool.Fori(1, TURNS // 2) as i:
                pair(i)
            pool.wait_ge(scat[0], 16 * TURN * (TURNS // 2))
            pool.sem_inc(landed, 1)
            turn(0, 0, LAST, scat[2], TURNS)
            pool.wait_ge(scat[1], 16 * TURN * (TURNS // 2))
            pool.sem_inc(landed, 1)
            pool.wait_ge(scat[2], 16 * LAST)
            pool.sem_inc(landed, 1)

            pool.wait_ge(w_done, 2 * NT)
            nc.gpsimd.iota(nid, pattern=[[P, NT]], base=0, channel_multiplier=1,
                           allow_small_or_imprecise_dtypes=True).then_inc(list_consts, 1)
            nc.gpsimd.iota(places, pattern=[[1, P]], base=0, channel_multiplier=0,
                           allow_small_or_imprecise_dtypes=True).then_inc(list_consts, 1)
            nc.gpsimd.iota(chunks, pattern=[[1, CHUNKS]], base=0, channel_multiplier=0,
                           allow_small_or_imprecise_dtypes=True).then_inc(list_consts, 1)
            nc.gpsimd.iota(ladder, pattern=[[1, CN]], base=1, channel_multiplier=0).then_inc(list_consts, 1)
            nc.gpsimd.iota(pads, pattern=[[P, CHUNKS]], base=NP - TOPK, channel_multiplier=1,
                           allow_small_or_imprecise_dtypes=True).then_inc(list_consts, 1)
            pool.wait_ge(list_consts, 5)
            nc.gpsimd.affine_select(out=pads, in_=pads, compare_op=ALU.is_ge, fill=0.0, base=-TOPK,
                                    pattern=[[P, CHUNKS]], channel_multiplier=1).then_inc(list_consts, 1)
            pool.wait_ge(wcol_ready, 1)
            nc.gpsimd.affine_select(out=wcol[:, NT - 1:NT], in_=wcol[:, NT - 1:NT], compare_op=ALU.is_ge,
                                    fill=-3.0e38, base=N - 1 - (NT - 1) * P, pattern=[[0, 1]],
                                    channel_multiplier=-1).then_inc(wcol_cut, 1)
            for j in range(TG):
                pool.wait_ge(end_st[j], 32 * TG)
            pool.wait_ge(ffn_in, 96)
            for w, raw in ffn_weights:
                nc.gpsimd.tensor_scalar(raw, raw, WS, None, ALU.mult).then_inc(w_scaled, 1)
            for i, (w, raw) in enumerate(ffn_weights):
                pool.wait_ge(w_hi, i + 1)
                nc.gpsimd.tensor_tensor(flat(w[:, 1]), raw, flat(w[:, 0]), ALU.subtract).then_inc(w_lo, 1)
            pool.wait_ge(idx_ready, 1)

            CP0 = 2 * TURNS + 2

            def gather(i, rows_, into, j, arrived):
                nc.gpsimd.indirect_dma_start(into[:, j, :], None, rows_,
                                             bass.IndirectOffsetOnAxis(ap=i[:, j:j + 1], axis=0)).then_inc(arrived[j], 16)

            def features(g):
                ge(pool, f_t, CH * g, nop=True)
                ge(pool, fj_done, g, nop=True)
                for j in range(CH):
                    ge(pool, xg_in[j], 16 * g, nop=True)
                    ge(pool, bg_in[j], 16 * g, nop=True)
                nc.gpsimd.tensor_copy(cur_g, idx[:, bass.ds(g * CH, CH)]).then_inc(idx_cp, 1)
                ge(pool, idx_cp, CP0 + (1 if isinstance(g, int) and g == 0 else 2 * g), nop=True)
                for j in range(CH):
                    gather(cur_g, xn2d, xg, j, xg_in)

            def results(g, more=True):
                if not (isinstance(g, int) and g == 0):
                    for j in range(CH):
                        ge(pool, y_st[j], 16 * g, nop=True)
                nc.gpsimd.tensor_copy(cur_s, idx[:, bass.ds(g * CH, CH)]).then_inc(idx_cp, 1)
                ge(pool, idx_cp, CP0 + 2 * g + (3 if more else 2), nop=True)
                for j in range(CH):
                    ge(pool, yo_ready, CH * g + j + 1, nop=True)
                    nc.gpsimd.indirect_dma_start(out, bass.IndirectOffsetOnAxis(ap=cur_s[:, j:j + 1], axis=0),
                                                 yo[:, j, :], None).then_inc(y_st[j], 16)
                    if more:
                        gather(cur_g, out, bg, j, bg_in)

            features(0)
            for j in range(CH):
                gather(cur_g, out, bg, j, bg_in)
            features(1)
            results(0)
            with pool.Fori(1, CH - 1) as g:
                features(g + 1)
                results(g)
            results(CH - 1, False)
            for j in range(CH):
                pool.wait_ge(y_st[j], 16 * CH)

        @block.scalar
        def _(act):
            act.wait_ge(zero_made, 1)
            with act.Fori(0, NT) as t:
                act.dma_start(A_tiles[:, t, 0:NP], zero_rows).then_inc(a_zeroed, 16)
            for rows_ in (xn2d, out):
                act.dma_start(rows_[NP:NP + P, :], zero_rows.bitcast(f32)[:, 0:D]).then_inc(a_zeroed, 16)
            a = sum(range(1, ROW_BITS + 1)) % 2
            c = 0
            for k in range(ROW_BITS + 1, BITS + 1):
                for stages in (k - ROW_BITS, ROW_BITS):
                    c += 1
                    act.wait_ge(tposed, 2 * c - 1)
                    nc.scalar.copy(keys[1 - a][:, 0:F_ACT], ps_sort[:, 0:F_ACT]).then_inc(act_copied, 1)
                    a = (a + 1 + stages) % 2
            for turned_over in (run, cnt16[:]):
                c += 1
                act.wait_ge(tposed, 2 * c - 1)
                nc.scalar.copy(turned_over[:, 0:F_ACT], ps_sort[:, 0:F_ACT]).then_inc(act_copied, 1)
            act.wait_ge(a_zeroed, 16 * (NT + 2))

            def deviations(g):
                act.wait_ge(var_ready, g + 1)
                nc.scalar.activation(std[:], mv[:, :, 1], ACT.Sqrt, bias=eps[:]).then_inc(std_ready, 1)

            def first(g, more=True):
                for s in range(TG + 2):
                    if s == 5 and more:
                        deviations(g + 1)
                    if s < TG:
                        n = g * TG + s
                        act.wait_ge(xn_done, n + 1)
                        nc.scalar.copy(zs1[:, n, 0, :], xn[:, s, :]).then_inc(hi_done, 1)
                        act.wait_ge(xT_done, n + 1)
                        ge(act, kv_done, n + 1 - TG)
                        ge(act, n_st[s], 32 * g)
                        nc.scalar.copy(xnT[:, s, :], ps_T[:, s % 2, :]).then_inc(xT_copied, 1)
                    if s >= 2:
                        j = s - 2
                        n = g * TG + j
                        act.wait_ge(ss_done, n + 1)
                        ge(act, v_done, g * TG + before(j, 2))
                        nc.scalar.activation(sd[:, j % 2, :], ss[:, j % 2, :], ACT.Sqrt, bias=eps[:],
                                             scale=1.0 / HEAD).then_inc(sd_done, 1)
                    if 1 <= s <= TG:
                        j = s - 1
                        n = g * TG + j
                        act.wait_ge(kv_done, n + 1)
                        ge(act, ss_done, g * TG + before(j, 2))
                        nc.scalar.activation(sq[:, j % 2, :], ps_kv[j % 2], ACT.Square).then_inc(sq_done, 1)
                        ge(act, dots_done, g * TG + before(j, 2))
                        nc.scalar.copy(k_sb[:, j % 2, :], ps_kv[j % 2][:, 0:512])

            deviations(0)
            first(0)
            with act.Fori(1, TG - 1) as g:
                first(g)
            first(TG - 1, False)
            act.wait_ge(gm_done, 1)
            nc.scalar.copy(g_sb.rearrange("p c e -> p (c e)"), ps_kv[0]).then_inc(gm_copied, 1)
            act.wait_ge(gm_done, 2)
            nc.scalar.copy(m_sb.rearrange("p c e -> p (c e)"), ps_kv[1][:, 0:512]).then_inc(gm_copied, 1)

            def split_gw(l):
                act.wait_ge(gw_in, 16 * (l + 1))
                for kc in range(4):
                    nc.scalar.activation(gws[:, 0, kc, :], gw_raw[l][:, kc * EXPERTS * D:(kc + 1) * EXPERTS * D], ACT.Copy,
                                         scale=WS).then_inc(gw_hi, 1)

            split_gw(0)
            for l in range(2):
                def early_sums(lo, b):
                    if l == 0 and (lo, b) in EARLY:
                        row_group = EARLY.index((lo, b))
                        act.wait_ge(agg_lo, 4 * lo + 2 * b + 2)
                        for h in range(HALVES[row_group]):
                            n = 2 * row_group + h
                            act.wait_ge(a_used, PASSES[2, row_group, h][1] + known(row_group, h))
                            for half in range(2):
                                ge(act, early_st[half], 16 * n)
                                nc.scalar.copy(mean[:, half, :], ps_agg[h][half][:, 0:HR]).then_inc(early_evac, 1)
                            for half in range(2):
                                act.wait_ge(early_evac, 2 * n + half + 1)
                                act.dma_start(earlyd[n * P:(n + 1) * P, half, :], mean[:, half, :]).then_inc(early_st[half], 16)

                def layer(g, lo):
                    G = g + TG * l
                    for i, js in enumerate(T_ORDER):
                        act.wait_ge(t_done, G * TB + i + 1)
                        nc.scalar.copy(zT[:, js[0]:js[-1] + 1], ps_zT[:, js[0]:js[-1] + 1]).then_inc(t_copied, 1)
                    if l == 1 and lo == 0:
                        act.wait_ge(w_done, NT)
                        split_gw(1)
                    act.wait_ge(lg_sub, G + 1)
                    nc.scalar.activation(lg[:], lg[:], ACT.Exp).then_inc(lg_exp, 1)

                    def mean_hi(b):
                        for half in range(2):
                            act.wait_ge(agg_evac, 4 * G + 2 * b + half + 1)
                            nc.scalar.copy(aggT[:, 0, half, b * HR:(b + 1) * HR], mean[:, half, :]).then_inc(agg_hi, 1)

                    mean_hi(0)
                    for s in range(TG + 1):
                        if l == 0 and s == 5:
                            act.wait_ge(agg_evac, 4 * G + 4)
                            act.dma_start(invd[0:1, bass.ds(g * GR, GR)], inv[0:1, :]).then_inc(inv_st, 16)
                        if s < TG:
                            n = G * TG + s
                            act.wait_ge(wts_ready, G + 1)
                            act.wait_ge(z_ld[s], Z0[s] + 16 * (G + 1))
                            if l == 1:
                                ge(act, x1_done, g * TG + before(s, 2))
                            else:
                                ge(act, hi2_done, g * TG + before(s, 2))
                            nc.scalar.activation(acc[:, s % 2, :], z_in[:, s, :], ACT.Copy,
                                                 scale=wsum[:, s:s + 1]).then_inc(acc_init, 1)
                        if s >= 1 and l == 0:
                            j = s - 1
                            n = G * TG + j
                            act.wait_ge(acc_done, n + 1)
                            ge(act, zn_st[j % 4], 16 * ((2 if j % 4 < 3 else 1) * g + j // 4))
                            ge(act, lo2_done, g * TG + before(j, 4))
                            nc.scalar.activation(zn[:, j % 4, :], acc[:, j % 2, :], ACT.Relu).then_inc(zn_ready, 1)
                            nc.scalar.activation(zs2[:, n, 0, :], acc[:, j % 2, :], ACT.Relu).then_inc(hi2_done, 1)
                            act.wait_ge(zn_ready, n + 1)
                            act.dma_start(rows(zd[1])[:, n, :], zn[:, j % 4, :]).then_inc(zn_st[j % 4], 16)
                        if s == 3:
                            early_sums(lo, 0)
                            mean_hi(1)
                    early_sums(lo, 1)
                    if l == 1:
                        act.wait_ge(var_ready, TG + g + 1)
                        nc.scalar.activation(std[:], mv[:, :, 1], ACT.Sqrt, bias=eps[:]).then_inc(std_ready, 1)

                alike(act, l, layer)

            def x2_copies(g):
                for j in range(CH):
                    act.wait_ge(f_t, CH * g + j + 1)
                    ge(act, h_done, 16 * g)
                    nc.scalar.copy(x2T[:, 0, :, j * P:(j + 1) * P],
                                   ps_x2[:, j % 2, :].rearrange("p (k r) -> p k r", k=2)).then_inc(f_tc, 1)

            def ffn(g, more=True):
                for half in range(2):
                    for m in range(8):
                        q = half * 8 + m
                        act.wait_ge(h_done, 16 * g + q + 1)
                        ge(act, h_lo, 16 * g + q - 1)
                        nc.scalar.activation(h_sb[:, q % 2, :], bank(q % 2)[:, 0:FH], ACT.Gelu_apprx_tanh,
                                             bias=b1_sb[:, m:m + 1], scale=1.0 / WS).then_inc(h_act, 1)
                if more:
                    x2_copies(g + 1)

            for i, (w, raw) in enumerate(ffn_weights):
                act.wait_ge(w_scaled, i + 1)
                nc.scalar.copy(flat(w[:, 0]), raw).then_inc(w_hi, 1)
            x2_copies(0)
            ffn(0)
            with act.Fori(1, CH - 1) as g:
                ffn(g)
            ffn(CH - 1, False)

        @block.vector
        def _(dve):
            base_n, k_n = [0], [0]

            def link(ins):
                k_n[0] += 1
                ins.then_inc(step, 1)
                dve.wait_ge(step, base_n[0] + k_n[0])

            def linked(body, count=TG, last_apart=False):
                start = base_n[0] + k_n[0]
                base_n[0], k_n[0] = start, 0
                body(0)
                per = k_n[0]
                looped = count - 1 if last_apart else count
                with dve.Fori(1, looped) as g:
                    base_n[0], k_n[0] = start + g * per, 0
                    body(g)
                    assert k_n[0] == per
                base_n[0], k_n[0] = start + looped * per, 0
                if last_apart:
                    body(count - 1, False)

            def linked_alike(l, body):
                for lo, hi in ALIKE[l]:
                    if hi == lo + 1:
                        before_it = k_n[0]
                        body(lo, lo)
                        per = k_n[0] - before_it
                    else:
                        start = base_n[0] + k_n[0]
                        with dve.Fori(lo, hi) as g:
                            base_n[0], k_n[0] = g * per + (start - lo * per), 0
                            body(g, lo)
                            assert k_n[0] == per
                        base_n[0], k_n[0] = start + (hi - lo) * per, 0

            I = lambda ap: ap.bitcast(i32)
            nc.vector.memset(zero_rows.bitcast(f32), 0.0).then_inc(zero_made, 1)
            link(nc.vector.memset(I(keys[0]), KEY_PAD))
            link(nc.vector.memset(keys[1][:, EW:F], 0.0))
            link(nc.vector.memset(eps[:], EPS))
            link(nc.vector.memset(edge_next, 0.0))
            link(nc.vector.memset(edge_prev, 0.0))
            link(nc.vector.memset(cexcl, 0.0))
            link(nc.vector.memset(zeros_row, 0.0))
            dve.wait_ge(edges_in, 32)
            link(nc.vector.tensor_scalar(src_in[0:EP, :], src_in[0:EP, :], CB, KEY_BASE, ALU.logical_shift_left, ALU.bitwise_or))
            link(nc.vector.tensor_tensor(I(keys[0][0:EP, 0:EC]), dst_in[0:EP, :], src_in[0:EP, :], ALU.bitwise_or))
            dve.wait_ge(consts, 5)
            link(nc.vector.memset(qbit, 0))
            for b in range(7):
                link(nc.vector.tensor_scalar(qbit[:, b + 1:b + 2], qid, b, 1, ALU.logical_shift_right, ALU.bitwise_and))
            link(nc.vector.tensor_tensor(qxor, qbit[:, 0:8], qbit[:, 1:9], ALU.bitwise_xor))
            link(nc.vector.tensor_scalar(sgn[:, 0:8], qxor, -2.0, 1.0, ALU.mult, ALU.add))
            link(nc.vector.tensor_scalar(sgn[:, 8:9], sgn[:, 0:1], -1.0, None, ALU.mult))
            link(nc.vector.tensor_scalar(tmp, same, NODE, CB, ALU.bitwise_and, ALU.logical_shift_left))
            link(nc.vector.tensor_scalar(spare, same, CB, KEY_BASE | SPARE, ALU.logical_shift_right, ALU.bitwise_or))
            link(nc.vector.tensor_tensor(spare, spare, tmp, ALU.bitwise_or))

            a = [0]

            def exchange(d, handed_over=False, width=F):
                halves = (slice(0, F // 2), slice(F // 2, F)) if handed_over else (slice(0, width),)
                for q in halves:
                    s = keys[a[0]][:, q].rearrange("p (n two d) -> p n two d", two=2, d=d)
                    t = keys[1 - a[0]][:, q].rearrange("p (n two d) -> p n two d", two=2, d=d)
                    nc.vector.tensor_tensor(t[:, :, 0, :], s[:, :, 0, :], s[:, :, 1, :], ALU.min).then_inc(step, 1)
                    k_n[0] += 1
                    link(nc.vector.tensor_tensor(t[:, :, 1, :], s[:, :, 0, :], s[:, :, 1, :], ALU.max))
                    if handed_over:
                        nc.vector.sem_inc(order_out, 1)
                a[0] = 1 - a[0]

            v = keys[0].rearrange("p (n four) -> p n four", four=4)
            link(nc.vector.tensor_scalar(v[:, :, 2:4], v[:, :, 2:4], -1.0, None, ALU.mult))
            turned = 0
            for k in range(1, BITS + 1):
                if k > ROW_BITS:
                    for half in (0, 1):
                        turned += 1
                        dve.wait_ge(tposed, 2 * turned)
                        link(nc.vector.tensor_copy(keys[1 - a[0]][:, F_ACT:F], ps_sort[:, F_ACT:F]))
                        dve.wait_ge(act_copied, turned)
                        a[0] = 1 - a[0]
                        if half == 0:
                            for b in range(k - ROW_BITS - 1, -1, -1):
                                exchange(1 << b, handed_over=(b == 0))
                for b in range(min(k, ROW_BITS) - 1, -1, -1):
                    exchange(1 << b, width=EW if k <= EW_BITS else F)
                K = keys[a[0]]
                if k < ROW_BITS - 1:
                    v = K.rearrange("p (n q) -> p n q", q=1 << (k + 2))[:, :, (1 << k):(3 << k)]
                    link(nc.vector.tensor_scalar(v, v, -1.0, None, ALU.mult))
                    if k == EW_BITS:
                        size = 2 << k
                        for n in range(EW // size, F // size):
                            link(nc.vector.memset(I(K[:, max(EW, n * size):(n + 1) * size]), KEY_PAD - (n % 2 << 31)))
                elif k == ROW_BITS - 1:
                    h = F // 2
                    nc.vector.tensor_scalar(K[:, 0:h], K[:, 0:h], sgn[:, 0:1], None, ALU.mult).then_inc(step, 1)
                    k_n[0] += 1
                    link(nc.vector.tensor_scalar(K[:, h:F], K[:, h:F], sgn[:, 8:9], None, ALU.mult))
                elif k < BITS:
                    b = k - ROW_BITS + 1
                    for q in (slice(0, F // 2), slice(F // 2, F)):
                        link(nc.vector.tensor_scalar(K[:, q], K[:, q], sgn[:, b:b + 1], None, ALU.mult))
                        nc.vector.sem_inc(order_out, 1)
            if a[0] == 1:
                link(nc.vector.tensor_copy(keys[0], keys[1]))
            K = keys[0]

            nc.vector.sem_inc(sorted_s, 1)
            link(nc.vector.tensor_tensor(same[:, 0:F - 1], K[:, 0:F - 1], K[:, 1:F], ALU.is_equal))
            link(nc.vector.tensor_tensor(run[:, 1:F], K[:, 0:F - 1], K[:, 1:F], ALU.not_equal))
            dve.wait_ge(carry_s, 32)
            link(nc.vector.tensor_tensor(same[:, F - 1:F], K[:, F - 1:F], edge_next, ALU.is_equal))
            link(nc.vector.tensor_tensor(run[:, 0:1], K[:, 0:1], edge_prev, ALU.not_equal))
            link(nc.vector.tensor_tensor(run, run, pos, ALU.mult))
            link(nc.vector.tensor_tensor_scan(keys[1], run, run, 0.0, ALU.max, ALU.max))
            nc.vector.sem_inc(sorted_s, 1)
            link(nc.vector.copy_predicated(I(K), same, spare))
            nc.vector.sem_inc(order_out, 2)
            dve.wait_ge(carried, 1)
            link(nc.vector.tensor_tensor_scan(cexcl[0:1, 1:P + 1], ps_carry[0:1, 0:P], zeros_row[0:1, :], 0.0, ALU.max, ALU.max))
            nc.vector.sem_inc(sorted_s, 1)
            dve.wait_ge(tposed, 2 * turned + 2)
            link(nc.vector.tensor_copy(run[:, F_ACT:F], ps_sort[:, F_ACT:F]))
            dve.wait_ge(act_copied, turned + 1)
            link(nc.vector.tensor_scalar(tmp, I(run), NODE, CB, ALU.bitwise_and, ALU.logical_shift_left))
            link(nc.vector.tensor_scalar(same, I(run), CB, NODE, ALU.logical_shift_right, ALU.bitwise_and))
            nc.vector.tensor_tensor(addr[:], tmp, same, ALU.bitwise_or).then_inc(lists_ready, 1)
            dve.wait_ge(carried, 2)
            link(nc.vector.tensor_copy(carry, ps_carry[:, P:P + 1]))
            link(nc.vector.scalar_tensor_tensor(keys[1], keys[1], carry, pos, ALU.max, ALU.subtract))
            for q in (slice(0, F // 2), slice(F // 2, F)):
                link(nc.vector.tensor_scalar(keys[1][:, q], keys[1][:, q], -1.0, 1.0, ALU.mult, ALU.add))
                nc.vector.sem_inc(order_out, 1)
            dve.wait_ge(tposed, 2 * turned + 4)
            dve.wait_ge(act_copied, turned + 2)
            nc.vector.tensor_copy(cnt16[:, F_ACT:F], ps_sort[:, F_ACT:F]).then_inc(lists_ready, 1)
            dve.wait_ge(lists_ready, 2)
            for i in range(2 * TG):
                limit = float(np.array(KEY_BASE + ((i + 1) * HR << CB), np.int32).view(np.float32))
                link(nc.vector.tensor_scalar(run[0:EP, 0:EC], src_in[0:EP, :].bitcast(f32), limit, None, ALU.is_lt, ALU.add,
                                             accum_out=below[0:EP, i:i + 1]))
            nc.vector.sem_inc(below_ready, 1)
            dve.wait_ge(below_summed, 1)
            link(nc.vector.tensor_copy(bound[:], bank(0)[:, 0:2 * TG]))
            link(nc.vector.tensor_scalar(bound[:], bound[:], ROW_BITS, None, ALU.logical_shift_right))
            nc.vector.tensor_scalar(bound[:], bound[:], 1, None, ALU.add).then_inc(bound_ready, 1)
            nc.vector.sem_inc(early_free, 1)

            dve.wait_ge(wmix_in, 64)
            heads = wkv_sb.rearrange("p c (h e) -> p c h e", e=HEAD)
            link(nc.vector.reduce_sum(wmean, heads, AX))
            link(nc.vector.tensor_scalar(wmean, wmean, 1.0 / HEAD, None, ALU.mult))
            for kc in range(2):
                link(nc.vector.tensor_tensor(heads[:, kc], heads[:, kc],
                                             wmean[:, kc, :].unsqueeze(2).to_broadcast([P, 16, HEAD]), ALU.subtract))
            nc.vector.memset(dT, 0.0).then_inc(wkv_ready, 1)
            link(nc.vector.tensor_copy(ident16[:], ident[:]))
            dve.wait_ge(small_in, 32)
            link(nc.vector.tensor_scalar(envs[:, 0], envw_sb[:], WS, None, ALU.mult))
            nc.vector.scalar_tensor_tensor(envs[:, 1], envw_sb[:], WS, envs[:, 0], ALU.mult, ALU.subtract).then_inc(env_split, 1)

            def statistics(g):
                for j in range(TG):
                    dve.wait_ge(x_ld[j], 16 * (g + 1))
                    ins = nc.vector.bn_stats(stats[:, j, :], x_in[:, j, :])
                    if j < TG - 1:
                        ins.then_inc(step, 1)
                        k_n[0] += 1
                link(ins)
                nc.vector.nop(nofuse=True)
                for j in range(TG):
                    ins = nc.vector.bn_aggr(mv[:, j, :], stats[:, j, :])
                ins.then_inc(var_ready, 1)

            def normalise(g):
                dve.wait_ge(std_ready, g + 1)
                link(nc.vector.reciprocal(rstd[:], std[:]))
                for j in range(TG):
                    n = g * TG + j
                    ge(dve, hi_done, n + 1 - TG)
                    ge(dve, xT_done, n + 1 - TG)
                    ge(dve, lo_done, n + 1 - TG)
                    ge(dve, n_st[j], 32 * g)
                    nc.vector.tensor_scalar(xn[:, j, :], x_in[:, j, :], mv[:, j, 0:1], rstd[:, j:j + 1],
                                            ALU.subtract, ALU.mult).then_inc(xn_done, 1)

            def first(g, more=True):
                for s in range(TG + 1):
                    if s == 4 and more:
                        statistics(g + 1)
                    if s < TG:
                        n = g * TG + s
                        dve.wait_ge(hi_done, n + 1)
                        nc.vector.tensor_tensor(zs1[:, n, 1, :], xn[:, s, :], zs1[:, n, 0, :], ALU.subtract).then_inc(lo_done, 1)
                    if s >= 1:
                        j = s - 1
                        n = g * TG + j
                        dve.wait_ge(sd_done, n + 1)
                        link(nc.vector.reciprocal(rs, sd[:, j % 2, :]))
                        ge(dve, v_done, n)
                        link(nc.vector.tensor_tensor(rr, rs[:, 0:8], rs[:, 8:16], ALU.mult))
                        ge(dve, dots_done, g * TG + before(j, 2))
                        nc.vector.tensor_tensor(v_sb[:, j % 2, :].rearrange("p (h e) -> p h e", e=HEAD),
                                                ps_kv[j % 2][:, 512:1024].rearrange("p (h e) -> p h e", e=HEAD),
                                                rr.unsqueeze(2).to_broadcast([P, 8, HEAD]), ALU.mult).then_inc(v_done, 1)
                    if s < TG:
                        n = g * TG + s
                        if s == TG - 1 and more:
                            normalise(g + 1)
                        dve.wait_ge(sq_done, n + 1)
                        ge(dve, sd_done, g * TG + before(s, 2))
                        nc.vector.reduce_sum(ss[:, s % 2, :], sq[:, s % 2, :].rearrange("p (h e) -> p h e", e=HEAD),
                                             AX).then_inc(ss_done, 1)

            statistics(0)
            normalise(0)
            linked(first, last_apart=True)
            dve.wait_ge(dots_done, NT)
            dd = ps_dots.rearrange("p (c e) -> p c e", c=4)
            for h in range(2):
                q = slice(h * HEAD, (h + 1) * HEAD)
                nc.vector.tensor_scalar(dT[q, :, q], dd[q, :, q], 1.0 / N, None, ALU.mult).then_inc(dT_done, 1)

            def mix(g):
                for j in range(TG):
                    n = g * TG + j
                    dve.wait_ge(mix_done, n + 1)
                    ge(dve, xp_st[j >= PIECES[1][0]], 16 * g)
                    link(nc.vector.tensor_tensor(xn[:, j, :], bank(j % 4)[:, 0:D], x_in[:, j, :], ALU.add))
                    nc.vector.tensor_tensor(xn[:, j, :], xn[:, j, :], bo_sb, ALU.add).then_inc(xp_ready, 1)

            dve.wait_ge(lo_done, NT)
            linked(mix)

            def split_gw(l):
                for kc in range(4):
                    dve.wait_ge(gw_hi, 4 * l + kc + 1)
                    nc.vector.scalar_tensor_tensor(gws[:, 1, kc, :], gw_raw[l][:, kc * EXPERTS * D:(kc + 1) * EXPERTS * D], WS,
                                                   gws[:, 0, kc, :], ALU.mult, ALU.subtract).then_inc(gw_lo, 1)

            split_gw(0)
            for l in range(2):
                def layer(g, lo):
                    G = g + TG * l
                    if l == 1 and lo == 0:
                        split_gw(1)
                    dve.wait_ge(logit_done, G + 1)
                    nc.vector.scalar_tensor_tensor(lg[:], ps_lg, 1.0 / WS,
                                                   envb_sb[:, l, :].unsqueeze(1).to_broadcast([P, TG, EXPERTS]),
                                                   ALU.mult, ALU.add).then_inc(lg_read, 1)
                    dve.wait_ge(lg_read, G + 1)
                    link(nc.vector.reduce_max(red[:, 0, :], lg[:], AX))
                    nc.vector.tensor_tensor(lg[:], lg[:], red[:, 0, :].unsqueeze(2).to_broadcast([P, TG, EXPERTS]),
                                            ALU.subtract).then_inc(lg_sub, 1)
                    dve.wait_ge(lg_exp, G + 1)
                    link(nc.vector.reduce_sum(red[:, 1, :], lg[:], AX))
                    link(nc.vector.reciprocal(red[:, 2, :], red[:, 1, :]))
                    link(nc.vector.tensor_tensor(wts[:], lg[:], red[:, 2, :].unsqueeze(2).to_broadcast([P, TG, EXPERTS]),
                                                 ALU.mult))
                    link(nc.vector.reduce_sum(wsum[:], wts[:], AX))
                    nc.vector.tensor_scalar(wts[:], wts[:], 1.0 / WS, None, ALU.mult).then_inc(wts_ready, 1)

                    def count(b):
                        cols = slice(b * HR, (b + 1) * HR)
                        for half in range(2):
                            ge(dve, early_st[half], 16 * early_before((lo, b)))
                        ge(dve, agg_lo, 4 * G + 2 * b)
                        if b == 0:
                            ge(dve, inv_st, 16 * g)
                        for u in range(TG):
                            dve.wait_ge(a_in[u], along(lambda g_: 16 * PASSES[l, g_, b][3][u] + 16, g, lo))
                            of_u = inv[:, cols] if u == 0 else mean[:, u % 2, :]
                            nc.vector.reduce_sum(of_u, a_ring[:, u, :, :].rearrange("p c r -> p r c"), AX).then_inc(a_counted, 1)
                            dve.wait_ge(a_counted, TG * (2 * g + b) + u + 1)
                            if u > 0:
                                add = nc.vector.tensor_tensor(inv[:, cols], inv[:, cols], of_u, ALU.add)
                                if u < TG - 1:
                                    link(add)
                        add.then_inc(cnt_ready, 1)

                    def evacuate(b):
                        if l == 0:
                            count(b)
                        dve.wait_ge(a_used, along(lambda g_: PASSES[l, g_, b][1] + len(PASSES[l, g_, b][0]), g, lo))
                        cols = slice(b * HR, (b + 1) * HR)
                        if l == 0:
                            dve.wait_ge(cnt_done, 2 * g + b + 1)
                            link(nc.vector.tensor_scalar(inv[:, cols], ps_cnt[b][:, 0:HR], 1.0, None, ALU.max))
                            link(nc.vector.reciprocal(inv[:, cols], inv[:, cols]))
                        else:
                            dve.wait_ge(inv_ld, 16 * (g + 1))
                        ge(dve, agg_lo, 4 * G + 2 * b)
                        if l == 1:
                            for half in range(2):
                                ge(dve, early_st[half], 16 * sum(HALVES))
                        early_part = l == 1 and known(lo, b) > 0
                        if early_part:
                            dve.wait_ge(early_ld[b], 16 * (g + 1))
                            for half in range(2):
                                link(nc.vector.tensor_tensor(mean[:, half, :], ps_agg[b][half][:, 0:HR], early_in[:, b, half, :],
                                                             ALU.add))
                        for half in range(2):
                            sums = mean[:, half, :] if early_part else ps_agg[b][half][:, 0:HR]
                            nc.vector.tensor_tensor(mean[:, half, :], sums, inv[:, cols], ALU.mult).then_inc(agg_evac, 1)
                        for half in range(2):
                            dve.wait_ge(agg_hi, 4 * G + 2 * b + half + 1)
                            nc.vector.tensor_tensor(aggT[:, 1, half, cols], mean[:, half, :], aggT[:, 0, half, cols],
                                                    ALU.subtract).then_inc(agg_lo, 1)

                    evacuate(0)
                    for s in range(TG + 1):
                        if s == 3:
                            evacuate(1)
                        if s < TG:
                            n = G * TG + s
                            dve.wait_ge(w_done, n + 1)
                            dve.wait_ge(acc_init, n + 1)
                            if s == 0:
                                dve.wait_ge(wts_ready, G + 1)
                            for e in range(EXPERTS):
                                ins = nc.vector.scalar_tensor_tensor(
                                    acc[:, s % 2, :], ps_out[s % 2][:, e * D:(e + 1) * D], wts[:, s, e:e + 1],
                                    acc[:, s % 2, :], ALU.mult, ALU.add)
                                if e < EXPERTS - 1:
                                    link(ins)
                            ins.then_inc(acc_done, 1)
                            if l == 1:
                                dve.wait_ge(acc_done, n + 1)
                                dve.wait_ge(xp_ld[s], 16 * (g + 1))
                                ge(dve, end_ready, g * TG - TG + s + 1)
                                nc.vector.scalar_tensor_tensor(x1[:, s, :], acc[:, s % 2, :], 0.0, xp_in[:, s, :],
                                                               ALU.max, ALU.add).then_inc(x1_done, 1)
                                dve.wait_ge(x1_done, g * TG + s + 1)
                                link(nc.vector.bn_stats(stats[:, s, :], x1[:, s, :]))
                        if s >= 1 and l == 0:
                            j = s - 1
                            n = G * TG + j
                            dve.wait_ge(hi2_done, n + 1)
                            nc.vector.tensor_tensor(zs2[:, n, 1, :], zn[:, j % 4, :], zs2[:, n, 0, :],
                                                    ALU.subtract).then_inc(lo2_done, 1)
                    if l == 1:
                        nc.vector.nop(nofuse=True)
                        for j in range(TG):
                            ins = nc.vector.bn_aggr(mv[:, j, :], stats[:, j, :])
                        ins.then_inc(var_ready, 1)
                        dve.wait_ge(std_ready, TG + g + 1)
                        link(nc.vector.reciprocal(rstd[:], std[:]))
                        if lo == 0:
                            dve.wait_ge(ffn_in, 48)
                        for j in range(TG):
                            ge(dve, end_st[j], 32 * g)
                            link(nc.vector.tensor_scalar(xn2[:, j, :], x1[:, j, :], mv[:, j, 0:1], rstd[:, j:j + 1],
                                                         ALU.subtract, ALU.mult))
                            nc.vector.tensor_tensor(base[:, j, :], x1[:, j, :], xn2[:, j, :], ALU.add).then_inc(end_ready, 1)
                            link(nc.vector.tensor_tensor_reduce(junk, xn2[:, j, :], wr_sb, 1.0, 0.0, ALU.mult, ALU.add,
                                                                red[:, 3, j:j + 1]))
                        link(nc.vector.tensor_scalar(wcol[:, bass.ds(g * TG, TG)], red[:, 3, :], br_sb, None, ALU.add))

                linked_alike(l, layer)

            nc.vector.sem_inc(wcol_ready, 1)
            dve.wait_ge(wcol_cut, 1)
            dve.wait_ge(list_consts, 6)
            link(nc.vector.memset(u_t, 0))
            asked = [0]

            def as_float(u, n, target):
                link(nc.vector.tensor_scalar(t1[:, 0:n], u, 31, 0x7FFFFFFF, ALU.arith_shift_right, ALU.bitwise_and))
                link(nc.vector.tensor_tensor(target, t1[:, 0:n], u, ALU.bitwise_xor))
                link(nc.vector.tensor_scalar(target, target, -1, None, ALU.bitwise_xor))

            def summed():
                nc.vector.sem_inc(cand_ready, 1)
                asked[0] += 1
                dve.wait_ge(counted, asked[0])

            w3 = wcol[:].unsqueeze(1).to_broadcast([P, CN, NT])
            h3 = hits.rearrange("p (c t) -> p c t", c=CN)
            for b in range(32 - DIGIT, -1, -DIGIT):
                link(nc.vector.tensor_scalar(cand, ladder, b, None, ALU.logical_shift_left))
                link(nc.vector.tensor_tensor(cand, cand, u_t.to_broadcast([P, CN]), ALU.bitwise_or))
                as_float(cand, CN, cand)
                link(nc.vector.tensor_tensor(h3, w3, cand.bitcast(f32).unsqueeze(2).to_broadcast([P, CN, NT]), ALU.is_ge))
                link(nc.vector.reduce_sum(part, h3, AX))
                summed()
                link(nc.vector.tensor_scalar(met, bank(5)[:, 0:CN], TOPK - 0.5, None, ALU.is_ge, ALU.add, accum_out=digit_f))
                link(nc.vector.tensor_copy(digit, digit_f))
                link(nc.vector.tensor_scalar(digit, digit, b, None, ALU.logical_shift_left))
                link(nc.vector.tensor_tensor(u_t, u_t, digit, ALU.bitwise_or))
            as_float(u_t, 1, thr_i)
            thr = thr_i.bitcast(f32)
            link(nc.vector.tensor_scalar(gt, wcol[:], thr, None, ALU.is_gt, ALU.add, accum_out=part[:, 0:1]))
            link(nc.vector.tensor_scalar(eq, wcol[:], thr, None, ALU.is_equal))

            def offsets():
                link(nc.vector.tensor_copy(tot, bank(6)[:, 64:64 + NT]))
                link(nc.vector.tensor_tensor_scan(scan, tot, tot, 0.0, ALU.add, ALU.bypass))
                link(nc.vector.tensor_tensor(scan, scan, tot, ALU.subtract))

            summed()
            link(nc.vector.tensor_scalar(ntot, bank(5)[:, 0:1], -1.0, float(TOPK), ALU.mult, ALU.add))
            offsets()
            link(nc.vector.tensor_tensor(cum, bank(6)[:, 0:NT], scan, ALU.add))
            link(nc.vector.tensor_scalar(cum, cum, ntot, None, ALU.is_le))
            link(nc.vector.tensor_tensor(eq, eq, cum, ALU.mult))
            link(nc.vector.tensor_tensor(sel, eq, gt, ALU.add))
            summed()
            offsets()
            link(nc.vector.tensor_tensor(cum, bank(6)[:, 0:NT], scan, ALU.add))
            link(nc.vector.tensor_tensor(cum, cum, sel, ALU.mult))
            link(nc.vector.tensor_scalar(slot_i, cum, -1.0, None, ALU.add))
            link(nc.vector.tensor_scalar(slot_p, slot_i, P - 1, None, ALU.bitwise_and))
            link(nc.vector.tensor_scalar(slot_c, slot_i, 7, None, ALU.arith_shift_right))
            link(nc.vector.tensor_copy(at_p, slot_p))
            link(nc.vector.tensor_copy(at_c, slot_c))
            link(nc.vector.tensor_tensor(is_c, chunks.unsqueeze(1).to_broadcast([P, NT, CHUNKS]),
                                         at_c.unsqueeze(2).to_broadcast([P, NT, CHUNKS]), ALU.is_equal))
            link(nc.vector.tensor_tensor(is_c, is_c, nid.unsqueeze(2).to_broadcast([P, NT, CHUNKS]), ALU.mult))
            for i in range(TG):
                ge(dve, is_p_used, i - 1)
                nc.vector.tensor_tensor(is_p[i % 2], places.unsqueeze(1).to_broadcast([P, TG, P]),
                                        at_p[:, i * TG:(i + 1) * TG].unsqueeze(2).to_broadcast([P, TG, P]),
                                        ALU.is_equal).then_inc(is_p_ready, 1)
            dve.wait_ge(is_p_used, TG)
            nc.vector.tensor_tensor(idx, bank(7)[:, 0:CHUNKS], pads, ALU.add).then_inc(idx_ready, 1)

            def split_x2(g, j):
                dve.wait_ge(f_tc, CH * g + j + 1)
                nc.vector.tensor_tensor(x2T[:, 1, :, j * P:(j + 1) * P], ps_x2[:, j % 2, :].rearrange("p (k r) -> p k r", k=2),
                                        x2T[:, 0, :, j * P:(j + 1) * P], ALU.subtract).then_inc(x2_lo, 1)

            def ffn(g, more=True):
                ge(dve, yo_ready, CH * g)
                for j in range(CH):
                    dve.wait_ge(xg_in[j], 16 * (g + 1))
                    link(nc.vector.tensor_tensor_reduce(fj, xg[:, j, :], wr_sb, 1.0, 0.0, ALU.mult, ALU.add, fw[:, j:j + 1]))
                nc.vector.tensor_scalar(fw, fw, br_sb, None, ALU.add).then_inc(fj_done, 1)
                ge(dve, y_done, CH * g)
                for half in range(2):
                    for m in range(8):
                        q = half * 8 + m
                        dve.wait_ge(h_act, 16 * g + q + 1)
                        cols = slice(half * FH, (half + 1) * FH)
                        link(nc.vector.tensor_copy(hT[:, 0, m, cols], h_sb[:, q % 2, :]))
                        nc.vector.tensor_tensor(hT[:, 1, m, cols], h_sb[:, q % 2, :], hT[:, 0, m, cols],
                                                ALU.subtract).then_inc(h_lo, 1)
                dve.wait_ge(fj_done, g + 1)
                for j in range(CH):
                    if more:
                        split_x2(g + 1, j)
                    dve.wait_ge(y_done, CH * g + j + 1)
                    dve.wait_ge(bg_in[j], 16 * (g + 1))
                    ge(dve, y_st[j], 16 * g)
                    ge(dve, yo_ready, CH * g + (j - 1 if j >= 2 else 0))
                    nc.vector.scalar_tensor_tensor(yt[:, j % 2, :], bank(2 + j % 2)[:, 0:D], 1.0 / WS, b2_sb,
                                                   ALU.mult, ALU.add).then_inc(y_read, 1)
                    dve.wait_ge(y_read, CH * g + j + 1)
                    nc.vector.scalar_tensor_tensor(yo[:, j, :], yt[:, j % 2, :], fw[:, j:j + 1], bg[:, j, :],
                                                   ALU.mult, ALU.add).then_inc(yo_ready, 1)

            dve.wait_ge(ffn_in, 96)
            for j in range(CH):
                split_x2(0, j)
            linked(ffn, CH, last_apart=True)

        @block.tensor
        def _(pe):
            pe.wait_ge(consts, 1)
            a = sum(range(1, ROW_BITS + 1)) % 2
            c = 0

            def turn_over(K):
                for m in range(F // P):
                    if m * P % (F // 2) == 0:
                        pe.wait_ge(order_out, 2 * c - (m == 0))
                    last = nc.tensor.transpose(ps_sort[:, m * P:(m + 1) * P], K[:, m * P:(m + 1) * P], ident[:])
                    if (m + 1) * P in (F_ACT, F):
                        last.then_inc(tposed, 1)

            for k in range(ROW_BITS + 1, BITS + 1):
                for stages in (k - ROW_BITS, ROW_BITS):
                    c += 1
                    turn_over(keys[a])
                    a = (a + 1 + stages) % 2
            pe.wait_ge(sorted_s, 2)
            nc.tensor.transpose(ps_carry[0:1, 0:P], keys[1][:, F - 1:F], ident[:]).then_inc(carried, 1)
            c += 1
            turn_over(keys[0])
            pe.wait_ge(sorted_s, 3)
            nc.tensor.matmul(ps_carry[:, P:P + 1], cexcl[0:1, 0:P], ones_f[0:1, 0:1], start=True, stop=True).then_inc(carried, 1)
            c += 1
            pe.wait_ge(act_copied, c - 1)
            turn_over(keys[1])

            pe.wait_ge(below_ready, 1)
            nc.tensor.matmul(bank(0)[:, 0:2 * TG], ones_f[0:EP, :], below[0:EP, :], start=True, stop=True).then_inc(below_summed, 1)

            pe.wait_ge(wkv_ready, 1)
            pe.wait_ge(bound_ready, 1)

            def first(g):
                for s in range(TG + 3):
                    if s < TG:
                        pe.wait_ge(xn_done, g * TG + s + 1)
                        ge(pe, xT_copied, g * TG + before(s, 2))
                        for kc in range(2):
                            last = nc.tensor.transpose(ps_T[:, s % 2, kc * P:(kc + 1) * P], xn[:, s, kc * P:(kc + 1) * P], ident[:])
                        last.then_inc(xT_done, 1)
                    if 1 <= s <= TG:
                        j = s - 1
                        pe.wait_ge(xT_copied, g * TG + j + 1)
                        ge(pe, v_done, g * TG + before(j, 2))
                        for b in range(2):
                            for kc in range(2):
                                last = nc.tensor.matmul(ps_kv[j % 2][:, b * 512:(b + 1) * 512], xnT[:, j, kc * P:(kc + 1) * P],
                                                        wkv_sb[:, kc, b * 512:(b + 1) * 512], start=(kc == 0), stop=(kc == 1))
                        last.then_inc(kv_done, 1)
                    if s >= 3:
                        j = s - 3
                        pe.wait_ge(v_done, g * TG + j + 1)
                        for c4 in range(4):
                            q = slice(c4 * P, (c4 + 1) * P)
                            last = nc.tensor.matmul(ps_dots[:, q], v_sb[:, j % 2, q], k_sb[:, j % 2, q],
                                                    start=(isinstance(g, int) and g == 0 and j == 0 and c4 == 0), stop=True,
                                                    skip_group_check=True)
                        last.then_inc(dots_done, 1)

            groups(pe, first)
            pe.wait_ge(dT_done, 2)
            for c4 in range(4):
                last = nc.tensor.matmul(ps_kv[0][:, c4 * D:(c4 + 1) * D], dT[:, c4, :], wo_sb[:, c4, :], start=True, stop=True)
            last.then_inc(gm_done, 1)
            pe.wait_ge(gm_copied, 1)
            for half in range(2):
                for c4 in range(4):
                    last = nc.tensor.matmul(ps_kv[1][:, half * D:(half + 1) * D], wq_sb[:, c4, half * P:(half + 1) * P],
                                            g_sb[:, c4, :], start=(c4 == 0), stop=(c4 == 3))
            last.then_inc(gm_done, 1)
            pe.wait_ge(gm_copied, 2)

            def mix(g):
                for j in range(TG):
                    pe.wait_ge(x_ld[j >= PIECES[1][0]], 16 * TG + 32 * (g + 1))
                    ge(pe, xp_ready, g * TG + before(j, 4))
                    for kc in range(2):
                        last = nc.tensor.matmul(bank(j % 4)[:, 0:D], xnT[:, j, kc * P:(kc + 1) * P], m_sb[:, kc, :],
                                                start=(kc == 0), stop=(kc == 1))
                    last.then_inc(mix_done, 1)

            groups(pe, mix)
            pe.wait_ge(xp_ready, NT)
            pe.wait_ge(env_split, 1)

            for l in range(2):
                zs = zs1 if l == 0 else zs2
                pe.wait_ge(lo_done if l == 0 else lo2_done, NT)
                if l == 1:
                    pe.wait_ge(hi2_done, NT)

                def aggregate(g, lo, b, between=None):
                    G = g + TG * l
                    ge(pe, agg_evac, 4 * G + 2 * b)
                    ge(pe, early_evac, 2 * (early_before((lo, b)) if l == 0 else sum(HALVES)))
                    us = PASSES[l, lo, b][0]
                    for u in us:
                        if between is not None and u == min(us[0] + 2, TG - 1):
                            between()
                        pe.wait_ge(a_in[u], along(lambda g_: 16 * PASSES[l, g_, b][3][u] + 16, g, lo))
                        for cc in range(TG):
                            ct = u * TG + cc
                            for half in range(2):
                                for part_ in range(2):
                                    last = nc.tensor.matmul(
                                        ps_agg[b][half][:, 0:HR], zs[:, ct, part_, half * P:(half + 1) * P], a_ring[:, u, cc, :],
                                        start=(ct == us[0] * TG and part_ == 0), stop=(ct == NT - 1 and part_ == 1))
                        last.then_inc(a_used, 1)
                    if l == 0:
                        pe.wait_ge(cnt_ready, 2 * g + b + 1)
                        nc.tensor.matmul(ps_cnt[b][:, 0:HR], ones_f[:], inv[:, b * HR:(b + 1) * HR],
                                         start=True, stop=True).then_inc(cnt_done, 1)

                def early_sums(lo, b):
                    if l == 0 and (lo, b) in EARLY:
                        row_group = EARLY.index((lo, b))
                        for h in range(HALVES[row_group]):
                            us, _, _, loads, _ = PASSES[2, row_group, h]
                            pe.wait_ge(agg_evac, 4 * lo + 2 * b + 2)
                            ge(pe, early_evac, 4 * row_group - 2 + 2 * h)
                            for u in us:
                                pe.wait_ge(lo2_done, TG * (u + 1))
                                pe.wait_ge(a_in[u], 16 * loads[u] + 16)
                                for cc in range(TG):
                                    for half in range(2):
                                        for part_ in range(2):
                                            last = nc.tensor.matmul(
                                                ps_agg[h][half][:, 0:HR], zs2[:, u * TG + cc, part_, half * P:(half + 1) * P],
                                                a_ring[:, u, cc, :], start=(u == 0 and cc == 0 and part_ == 0),
                                                stop=(u == us[-1] and cc == TG - 1 and part_ == 1))
                                last.then_inc(a_used, 1)

                def layer(g, lo):
                    G = g + TG * l
                    for js in T_ORDER:
                        ge(pe, acc_done, G * TG - (1 if js[0] >= 4 else 0))
                        for j in js:
                            for part_ in range(2):
                                for kc in range(2):
                                    last = nc.tensor.transpose(ps_zT[:, j, part_, kc, :],
                                                               zs[:, g * TG + j, part_, kc * P:(kc + 1) * P], ident16[:])
                        last.then_inc(t_done, 1)

                    def logits():
                        pe.wait_ge(t_copied, (G + 1) * TB)
                        for j in range(TG):
                            for kc in range(2):
                                for a_, w_ in PRODUCTS:
                                    last = nc.tensor.matmul(ps_lg[:, j, :], zT[:, j, a_, kc, :], envs[:, w_, l, kc, :],
                                                            start=(kc == 0 and a_ + w_ == 0), stop=(kc == 1 and a_ == 1))
                        last.then_inc(logit_done, 1)

                    def of_features(j):
                        ge(pe, acc_done, G * TG + before(j, 2))
                        if j == 1:
                            pe.wait_ge(lg_read, G + 1)
                        products(j, [zT[:, j, :, kc, :] for kc in range(2)], 2, True)

                    def of_means(j):
                        pe.wait_ge(agg_lo, 4 * G + (2 if j < 3 else 4))
                        products(j, [aggT[:, :, kc, j * P:(j + 1) * P] for kc in range(2)], 0, False).then_inc(w_done, 1)

                    def products(j, ws, first_row, opens):
                        for kc, w in enumerate(ws):
                            for a_ in range(2):
                                for b in range(2):
                                    q = slice(b * 512, (b + 1) * 512)
                                    for w_ in range(2 - a_):
                                        last = nc.tensor.matmul(ps_out[j % 2][:, q], w[:, a_, :], gws[:, w_, first_row + kc, q],
                                                                start=(opens and kc == 0 and a_ + w_ == 0),
                                                                stop=(not opens and kc == 1 and a_ == 1))
                        return last

                    def experts(js):
                        for j in js[:2]:
                            of_features(j)
                        for j in js:
                            if j not in js[:2]:
                                of_features(j)
                            of_means(j)

                    aggregate(g, lo, 0, logits)
                    if lo == 0:
                        pe.wait_ge(gw_lo, 4 * (l + 1))
                    experts(range(3))
                    early_sums(lo, 0)
                    aggregate(g, lo, 1)
                    experts(range(3, TG))
                    early_sums(lo, 1)

                alike(pe, l, layer)

            rounds = 32 // DIGIT
            for n in range(rounds):
                pe.wait_ge(cand_ready, n + 1)
                nc.tensor.matmul(bank(5)[:, 0:CN], ones_f[:], part, start=True, stop=True).then_inc(counted, 1)
            pe.wait_ge(cand_ready, rounds + 1)
            nc.tensor.matmul(bank(5)[:, 0:1], ones_f[:], part[:, 0:1], start=True, stop=True)
            nc.tensor.matmul(bank(6)[:, 0:NT], tri[:], eq, start=True, stop=True)
            nc.tensor.matmul(bank(6)[:, 64:64 + NT], ones_f[:], eq, start=True, stop=True).then_inc(counted, 1)
            pe.wait_ge(cand_ready, rounds + 2)
            nc.tensor.matmul(bank(6)[:, 0:NT], tri[:], sel, start=True, stop=True)
            nc.tensor.matmul(bank(6)[:, 64:64 + NT], ones_f[:], sel, start=True, stop=True).then_inc(counted, 1)
            for i in range(TG):
                pe.wait_ge(is_p_ready, i + 1)
                for t in range(TG):
                    last = nc.tensor.matmul(bank(7)[:, 0:CHUNKS], is_p[i % 2][:, t, :], is_c[:, i * TG + t, :],
                                            start=(i == 0 and t == 0), stop=(i == TG - 1 and t == TG - 1))
                last.then_inc(is_p_used, 1)

            pe.wait_ge(w_lo, 2)

            def x2_transposes(g, j):
                pe.wait_ge(xg_in[j], 16 * (g + 1))
                ge(pe, x2_lo, CH * g + (j - 1 if j >= 2 else 0))
                for kc in range(2):
                    last = nc.tensor.transpose(ps_x2[:, j % 2, kc * P:(kc + 1) * P], xg[:, j, kc * P:(kc + 1) * P], ident[:])
                last.then_inc(f_t, 1)

            def ffn(g, more=True):
                pe.wait_ge(x2_lo, CH * (g + 1))
                for half in range(2):
                    for m in range(8):
                        q = half * 8 + m
                        ge(pe, h_act, 16 * g + q - 1)
                        for kc in range(2):
                            for w_, a_ in PRODUCTS:
                                last = nc.tensor.matmul(bank(q % 2)[:, 0:FH], w1s[:, w_, kc, m * P:(m + 1) * P],
                                                        x2T[:, a_, kc, half * FH:(half + 1) * FH],
                                                        start=(kc == 0 and a_ + w_ == 0), stop=(kc == 1 and w_ == 1))
                        last.then_inc(h_done, 1)
                for j in range(CH):
                    if more:
                        x2_transposes(g + 1, j)
                    pe.wait_ge(h_lo, 16 * g + (8 if j < 2 else 16))
                    ge(pe, y_read, CH * g + (j - 1 if j >= 2 else 0))
                    for m in range(8):
                        for a_, w_ in PRODUCTS:
                            last = nc.tensor.matmul(bank(2 + j % 2)[:, 0:D], hT[:, a_, m, j * P:(j + 1) * P], w2s[:, w_, m, :],
                                                    start=(m == 0 and a_ + w_ == 0), stop=(m == 7 and a_ == 1))
                    last.then_inc(y_done, 1)

            for j in range(CH):
                x2_transposes(0, j)
            ffn(0)
            with pe.Fori(1, CH - 1) as g:
                ffn(g)
            ffn(CH - 1, False)


def kernel(**inputs):
    import numpy as np
    import concourse.bacc as bacc
    from concourse import mybir
    from concourse.bass_utils import run_bass_kernel_spmd

    def arr(name):
        return np.asarray(inputs[name])

    def pieces(w, n):
        return w.reshape(n, P, -1).transpose(1, 0, 2)

    x = np.zeros((NP, D), np.float32)
    x[:N] = arr("x")
    W = arr("L0_gnn_W")
    wqkv = arr("L0_mix_w_qkv")
    envw = arr("L0_gnn_envW")
    laid = {
        "x": x, "src": arr("src"), "dst": arr("dst"),
        "gw": np.stack([pieces(W[l].transpose(1, 0, 2).reshape(2 * D, EXPERTS * D), 4).reshape(P, -1) for l in range(2)]),
        "envw": envw.reshape(2, 2, P, EXPERTS).transpose(2, 0, 1, 3),
        "envb": np.broadcast_to(arr("L0_gnn_envb")[None], (P, 2, EXPERTS)),
        "wkv": pieces(wqkv[512:].T, 2),
        "wq": pieces(wqkv[:512], 4),
        "wo": pieces(arr("L0_mix_w_out").T, 4),
        "bo": np.broadcast_to(arr("L0_mix_b_out")[None], (P, D)),
        "wr": np.broadcast_to(arr("L0_ffn_wr").reshape(1, D), (P, D)),
        "br": np.broadcast_to(arr("L0_ffn_br").reshape(1, 1), (P, 1)),
        "w1": pieces(arr("L0_ffn_w1"), 2).reshape(P, -1),
        "b1": arr("L0_ffn_b1").reshape(8, P).T,
        "w2": pieces(arr("L0_ffn_w2"), 8).reshape(P, -1),
        "b2": np.broadcast_to(arr("L0_ffn_b2")[None], (P, D)),
    }
    nc = bacc.Bacc("TRN2", target_bir_lowering=False, num_devices=1)
    arrays, args = {}, []
    for name, a in laid.items():
        a = np.ascontiguousarray(a)
        arrays[f"in_{name}"] = a
        args.append(nc.dram_tensor(f"in_{name}", a.shape, mybir.dt.from_np(a.dtype), kind="ExternalInput").ap())
    args.append(nc.dram_tensor("out_0", (NP + P, D), mybir.dt.float32, kind="ExternalOutput").ap())
    build(nc, *args)
    r = run_bass_kernel_spmd(nc, [arrays], core_ids=[0])
    return r.results[0]["out_0"][:N]
```
